# Optimizing a Trainium2 kernel written in Bass

```python
import numpy as np
import jax
import jax.numpy as jnp

def _softmax(x, axis=-1):
    return jax.nn.softmax(x, axis=axis)

def _gelu(x):
    return jax.nn.gelu(x, approximate=True)

def _silu(x):
    return jax.nn.silu(x)

def _sigmoid(x):
    return jax.nn.sigmoid(x)

def _layernorm(x, axis=-1, eps=1e-05):
    m = jnp.mean(x, axis=axis, keepdims=True)
    v = jnp.var(x, axis=axis, keepdims=True)
    return (x - m) / jnp.sqrt(v + eps)

def _scatter_add(tgt, idx, src, axis=0):
    return tgt.at[idx].add(src)

def _segment_sum(src, seg, n):
    return jax.ops.segment_sum(src, seg, n)
kernel_name = 'mk_conv_seq_d4_conv_nchw256_r4_3c2510'

def setup_inputs(seed: int=0):
    np.random.seed(seed)
    _w = jnp.asarray

    def _rec_inputs():
        import jax
        import jax.numpy as jnp
        _gk = jax.random.key(seed)
        x = 7.22e-05 + 1 * jax.random.normal(jax.random.fold_in(_gk, 1), (32, 64, 32, 32), jnp.float32)
        return x
    x = _rec_inputs()

    def _L0_conv_setup():
        import jax, jax.numpy as jnp
        import numpy as np
        IN_DIM = 64
        CONV_DIM = 16
        key = jax.random.key(seed)
        ks = jax.random.split(key, 7)
        B, C, H, W = (32, IN_DIM, 32, 32)
        scale_q = 1.0 / np.sqrt(C)
        x = jax.random.normal(ks[0], (B, C, H, W), dtype=jnp.float32)
        wq = jax.random.normal(ks[1], (CONV_DIM, C), dtype=jnp.float32) * scale_q
        bq = jnp.zeros((CONV_DIM,), dtype=jnp.float32)
        wk = jax.random.normal(ks[2], (CONV_DIM, C), dtype=jnp.float32) * scale_q
        bk = jnp.zeros((CONV_DIM,), dtype=jnp.float32)
        wv = jax.random.normal(ks[3], (C, C), dtype=jnp.float32) * scale_q
        bv = jnp.zeros((C,), dtype=jnp.float32)
        gamma = jnp.full((1,), 0.5, dtype=jnp.float32)
        return {'x': x, 'wq': wq, 'bq': bq, 'wk': wk, 'bk': bk, 'wv': wv, 'bv': bv, 'gamma': gamma}
    _L0_conv_all = _L0_conv_setup()
    _L0_conv_in = {k: v for k, v in _L0_conv_all.items() if k in ('wq', 'bq', 'wk', 'bk', 'wv', 'bv', 'gamma')}
    del _L0_conv_all

    def _L1_conv_setup():
        import jax, jax.numpy as jnp
        import numpy as np
        BN_EPS = 1e-05
        REG = jnp.array([[-1, -1, -1, 0, 0, 0, 1, 1, 1], [-1, 0, 1, -1, 0, 1, -1, 0, 1]], dtype=jnp.float32)

        def conv3x3(x, w, b):
            y = jax.lax.conv_general_dilated(x, w, window_strides=(1, 1), padding=((1, 1), (1, 1)), dimension_numbers=('NCHW', 'OIHW', 'NCHW'))
            return y + b[None, :, None, None]

        def deform_conv3x3(x, dy, dx, w):
            N, C, H, W = x.shape
            K = 9
            ky = jnp.repeat(jnp.arange(3), 3)
            kx = jnp.tile(jnp.arange(3), 3)
            py = dy + (jnp.arange(H) - 1)[None, None, :, None] + ky[None, :, None, None].astype(x.dtype)
            px = dx + (jnp.arange(W) - 1)[None, None, None, :] + kx[None, :, None, None].astype(x.dtype)
            y0 = jnp.floor(py)
            x0 = jnp.floor(px)
            wy = py - y0
            wx = px - x0
            y0i = y0.astype(jnp.int32)
            x0i = x0.astype(jnp.int32)
            nidx = jnp.arange(N)[:, None, None, None]

            def gather(yi, xi):
                valid = ((yi >= 0) & (yi < H) & (xi >= 0) & (xi < W)).astype(x.dtype)
                v = x[nidx, :, jnp.clip(yi, 0, H - 1), jnp.clip(xi, 0, W - 1)]
                return v * valid[..., None]
            sampled = gather(y0i, x0i) * ((1 - wy) * (1 - wx))[..., None] + gather(y0i, x0i + 1) * ((1 - wy) * wx)[..., None] + gather(y0i + 1, x0i) * (wy * (1 - wx))[..., None] + gather(y0i + 1, x0i + 1) * (wy * wx)[..., None]
            O = w.shape[0]
            return jnp.einsum('nkhwc,ock->nohw', sampled, w.reshape(O, C, K))
        key = jax.random.key(seed)
        ks = jax.random.split(key, 12)
        N, C, H, W = (2, 64, 24, 24)
        O = 64
        sc = 1.0 / np.sqrt(C * 9)
        return {'x': jax.random.normal(ks[0], (N, C, H, W), jnp.float32), 'mask_attention': jax.random.normal(ks[1], (N, C, H, W), jnp.float32), 'w_tm': jax.random.normal(ks[2], (4, C, 3, 3), jnp.float32) * sc, 'b_tm': jax.random.normal(ks[3], (4,), jnp.float32) * 0.01, 'w_tr': jax.random.normal(ks[4], (2, C, 3, 3), jnp.float32) * sc, 'b_tr': jax.random.normal(ks[5], (2,), jnp.float32) * 0.01, 'w_deform': jax.random.normal(ks[6], (O, C, 3, 3), jnp.float32) * sc, 'bn_gamma': jnp.ones((O,), jnp.float32), 'bn_beta': jnp.zeros((O,), jnp.float32), 'bn_mean': jax.random.normal(ks[7], (O,), jnp.float32) * 0.01, 'bn_var': jax.random.uniform(ks[8], (O,), jnp.float32, 0.5, 1.5)}
    _L1_conv_all = _L1_conv_setup()
    _L1_conv_in = {k: v for k, v in _L1_conv_all.items() if k in ('mask_attention', 'w_tm', 'b_tm', 'w_tr', 'b_tr', 'w_deform', 'bn_gamma', 'bn_beta', 'bn_mean', 'bn_var')}
    del _L1_conv_all

    def _L2_conv_setup():
        import jax, jax.numpy as jnp
        import numpy as np
        NUM_HEADS = 4
        NUM_GROUPS = 8
        EPS = 1e-05
        key = jax.random.key(seed)
        ks = jax.random.split(key, 4)
        B, C, H, W = (4, 64, 16, 16)
        x = jax.random.normal(ks[0], (B, C, H, W), dtype=jnp.float32)
        gn_w = jnp.ones((C,), dtype=jnp.float32)
        gn_b = jnp.zeros((C,), dtype=jnp.float32)
        w_qkv = jax.random.normal(ks[1], (3 * C, C), dtype=jnp.float32) * (1.0 / np.sqrt(C))
        b_qkv = jnp.zeros((3 * C,), dtype=jnp.float32)
        w_proj = jax.random.normal(ks[2], (C, C), dtype=jnp.float32) * (1.0 / np.sqrt(C))
        b_proj = jnp.zeros((C,), dtype=jnp.float32)
        return {'x': x, 'gn_w': gn_w, 'gn_b': gn_b, 'w_qkv': w_qkv, 'b_qkv': b_qkv, 'w_proj': w_proj, 'b_proj': b_proj}
    _L2_conv_all = _L2_conv_setup()
    _L2_conv_in = {k: v for k, v in _L2_conv_all.items() if k in ('gn_w', 'gn_b', 'w_qkv', 'b_qkv', 'w_proj', 'b_proj')}
    del _L2_conv_all

    def _L3_conv_setup():
        import jax, jax.numpy as jnp
        import numpy as np
        T = 5
        EPS = 1e-05
        NC = 16

        def _iternorm(X):
            B, C, H, W = X.shape
            g = C // NC
            x = jnp.transpose(X, (1, 0, 2, 3)).reshape(g, NC, -1)
            m = x.shape[-1]
            mean = x.mean(-1, keepdims=True)
            xc = x - mean
            I = jnp.eye(NC, dtype=X.dtype)
            Sigma = EPS * I + jnp.einsum('gdm,gem->gde', xc, xc) / m
            rTr = 1.0 / jnp.trace(Sigma, axis1=1, axis2=2)[:, None, None]
            Sn = Sigma * rTr
            P = jnp.broadcast_to(I, (g, NC, NC))
            for _ in range(T):
                P3 = jnp.matmul(jnp.matmul(P, P), P)
                P = 1.5 * P - 0.5 * jnp.matmul(P3, Sn)
            wm = P * jnp.sqrt(rTr)
            xn = jnp.matmul(wm, xc)
            Xn = jnp.transpose(xn.reshape(C, B, H, W), (1, 0, 2, 3))
            return Xn
        key = jax.random.key(seed)
        X = jax.random.normal(key, (32, 64, 32, 32), dtype=jnp.float32)
        weight = jnp.ones((1, 64, 1, 1), dtype=jnp.float32)
        bias = jnp.zeros((1, 64, 1, 1), dtype=jnp.float32)
        return {'X': X, 'weight': weight, 'bias': bias}
    _L3_conv_all = _L3_conv_setup()
    _L3_conv_in = {k: v for k, v in _L3_conv_all.items() if k in ('weight', 'bias')}
    del _L3_conv_all
    return {'x': x, 'L0_conv_wq': _L0_conv_in['wq'], 'L0_conv_bq': _L0_conv_in['bq'], 'L0_conv_wk': _L0_conv_in['wk'], 'L0_conv_bk': _L0_conv_in['bk'], 'L0_conv_wv': _L0_conv_in['wv'], 'L0_conv_bv': _L0_conv_in['bv'], 'L0_conv_gamma': _L0_conv_in['gamma'], 'L1_conv_mask_attention': _L1_conv_in['mask_attention'], 'L1_conv_w_tm': _L1_conv_in['w_tm'], 'L1_conv_b_tm': _L1_conv_in['b_tm'], 'L1_conv_w_tr': _L1_conv_in['w_tr'], 'L1_conv_b_tr': _L1_conv_in['b_tr'], 'L1_conv_w_deform': _L1_conv_in['w_deform'], 'L1_conv_bn_gamma': _L1_conv_in['bn_gamma'], 'L1_conv_bn_beta': _L1_conv_in['bn_beta'], 'L1_conv_bn_mean': _L1_conv_in['bn_mean'], 'L1_conv_bn_var': _L1_conv_in['bn_var'], 'L2_conv_gn_w': _L2_conv_in['gn_w'], 'L2_conv_gn_b': _L2_conv_in['gn_b'], 'L2_conv_w_qkv': _L2_conv_in['w_qkv'], 'L2_conv_b_qkv': _L2_conv_in['b_qkv'], 'L2_conv_w_proj': _L2_conv_in['w_proj'], 'L2_conv_b_proj': _L2_conv_in['b_proj'], 'L3_conv_weight': _L3_conv_in['weight'], 'L3_conv_bias': _L3_conv_in['bias']}

def reference(x, L0_conv_wq, L0_conv_bq, L0_conv_wk, L0_conv_bk, L0_conv_wv, L0_conv_bv, L0_conv_gamma, L1_conv_mask_attention, L1_conv_w_tm, L1_conv_b_tm, L1_conv_w_tr, L1_conv_b_tr, L1_conv_w_deform, L1_conv_bn_gamma, L1_conv_bn_beta, L1_conv_bn_mean, L1_conv_bn_var, L2_conv_gn_w, L2_conv_gn_b, L2_conv_w_qkv, L2_conv_b_qkv, L2_conv_w_proj, L2_conv_b_proj, L3_conv_weight, L3_conv_bias):
    import jax
    import jax.numpy as jnp

    def _L0_conv_ref(x, wq, bq, wk, bk, wv, bv, gamma):
        import jax, jax.numpy as jnp
        import numpy as np
        IN_DIM = 64
        CONV_DIM = 16
        B, C, H, W = x.shape
        N = H * W
        xf = x.reshape(B, C, N)
        q = jnp.einsum('oc,bcn->bon', wq, xf) + bq[None, :, None]
        k = jnp.einsum('oc,bcn->bon', wk, xf) + bk[None, :, None]
        v = jnp.einsum('oc,bcn->bon', wv, xf) + bv[None, :, None]
        attn = jnp.einsum('bci,bcj->bij', q, k)
        attn = jax.nn.softmax(attn, axis=1)
        out = jnp.einsum('bci,bij->bcj', v, attn)
        out = out.reshape(B, C, H, W)
        return x + gamma[0] * out

    def _L1_conv_ref(x, mask_attention, w_tm, b_tm, w_tr, b_tr, w_deform, bn_gamma, bn_beta, bn_mean, bn_var):
        import jax, jax.numpy as jnp
        import numpy as np
        BN_EPS = 1e-05
        REG = jnp.array([[-1, -1, -1, 0, 0, 0, 1, 1, 1], [-1, 0, 1, -1, 0, 1, -1, 0, 1]], dtype=jnp.float32)

        def conv3x3(x, w, b):
            y = jax.lax.conv_general_dilated(x, w, window_strides=(1, 1), padding=((1, 1), (1, 1)), dimension_numbers=('NCHW', 'OIHW', 'NCHW'))
            return y + b[None, :, None, None]

        def deform_conv3x3(x, dy, dx, w):
            N, C, H, W = x.shape
            K = 9
            ky = jnp.repeat(jnp.arange(3), 3)
            kx = jnp.tile(jnp.arange(3), 3)
            py = dy + (jnp.arange(H) - 1)[None, None, :, None] + ky[None, :, None, None].astype(x.dtype)
            px = dx + (jnp.arange(W) - 1)[None, None, None, :] + kx[None, :, None, None].astype(x.dtype)
            y0 = jnp.floor(py)
            x0 = jnp.floor(px)
            wy = py - y0
            wx = px - x0
            y0i = y0.astype(jnp.int32)
            x0i = x0.astype(jnp.int32)
            nidx = jnp.arange(N)[:, None, None, None]

            def gather(yi, xi):
                valid = ((yi >= 0) & (yi < H) & (xi >= 0) & (xi < W)).astype(x.dtype)
                v = x[nidx, :, jnp.clip(yi, 0, H - 1), jnp.clip(xi, 0, W - 1)]
                return v * valid[..., None]
            sampled = gather(y0i, x0i) * ((1 - wy) * (1 - wx))[..., None] + gather(y0i, x0i + 1) * ((1 - wy) * wx)[..., None] + gather(y0i + 1, x0i) * (wy * (1 - wx))[..., None] + gather(y0i + 1, x0i + 1) * (wy * wx)[..., None]
            O = w.shape[0]
            return jnp.einsum('nkhwc,ock->nohw', sampled, w.reshape(O, C, K))
        N, C, H, W = x.shape
        tm = conv3x3(x, w_tm, b_tm)
        T = tm.transpose(0, 2, 3, 1).reshape(N, H, W, 2, 2)
        off = jnp.einsum('nhwij,jk->nhwik', T, REG) - REG
        tr = conv3x3(x, w_tr, b_tr)
        off = off + tr.transpose(0, 2, 3, 1)[..., None]
        dy = off[..., 0, :].transpose(0, 3, 1, 2)
        dx = off[..., 1, :].transpose(0, 3, 1, 2)
        out = deform_conv3x3(x, dy, dx, w_deform)
        inv = jax.lax.rsqrt(bn_var + BN_EPS)
        out = (out - bn_mean[None, :, None, None]) * (inv * bn_gamma)[None, :, None, None] + bn_beta[None, :, None, None]
        return jax.nn.relu(out + x)

    def _L2_conv_ref(x, gn_w, gn_b, w_qkv, b_qkv, w_proj, b_proj):
        import jax, jax.numpy as jnp
        import numpy as np
        NUM_HEADS = 4
        NUM_GROUPS = 8
        EPS = 1e-05
        B, C, H, W = x.shape
        N = H * W
        nh = NUM_HEADS
        dh = C // nh
        xg = x.reshape(B, NUM_GROUPS, C // NUM_GROUPS, N)
        mu = jnp.mean(xg, axis=(2, 3), keepdims=True)
        var = jnp.var(xg, axis=(2, 3), keepdims=True)
        h = ((xg - mu) * jax.lax.rsqrt(var + EPS)).reshape(B, C, N)
        h = h * gn_w[None, :, None] + gn_b[None, :, None]
        qkv = jnp.einsum('oc,bcn->bon', w_qkv, h) + b_qkv[None, :, None]
        q, k, v = jnp.split(qkv, 3, axis=1)
        q = q.reshape(B, nh, dh, N)
        k = k.reshape(B, nh, dh, N)
        v = v.reshape(B, nh, dh, N)
        scores = jnp.einsum('bhdi,bhdj->bhij', q, k) / jnp.sqrt(jnp.array(dh, dtype=x.dtype))
        attn = jax.nn.softmax(scores, axis=-1)
        out = jnp.einsum('bhij,bhdj->bhdi', attn, v).reshape(B, C, N)
        out = jnp.einsum('oc,bcn->bon', w_proj, out) + b_proj[None, :, None]
        return x + out.reshape(B, C, H, W)

    def _L3_conv_ref(X, weight, bias):
        import jax, jax.numpy as jnp
        import numpy as np
        T = 5
        EPS = 1e-05
        NC = 16

        def _iternorm(X):
            B, C, H, W = X.shape
            g = C // NC
            x = jnp.transpose(X, (1, 0, 2, 3)).reshape(g, NC, -1)
            m = x.shape[-1]
            mean = x.mean(-1, keepdims=True)
            xc = x - mean
            I = jnp.eye(NC, dtype=X.dtype)
            Sigma = EPS * I + jnp.einsum('gdm,gem->gde', xc, xc) / m
            rTr = 1.0 / jnp.trace(Sigma, axis1=1, axis2=2)[:, None, None]
            Sn = Sigma * rTr
            P = jnp.broadcast_to(I, (g, NC, NC))
            for _ in range(T):
                P3 = jnp.matmul(jnp.matmul(P, P), P)
                P = 1.5 * P - 0.5 * jnp.matmul(P3, Sn)
            wm = P * jnp.sqrt(rTr)
            xn = jnp.matmul(wm, xc)
            Xn = jnp.transpose(xn.reshape(C, B, H, W), (1, 0, 2, 3))
            return Xn
        Xn = _iternorm(X)
        return Xn * weight + bias

    def _gn(v, G=32, eps=1e-05):
        B_, C_, H_, W_ = v.shape
        g = v.reshape(B_, G, C_ // G, H_, W_)
        m = jnp.mean(g, axis=(2, 3, 4), keepdims=True)
        s = jnp.var(g, axis=(2, 3, 4), keepdims=True)
        return ((g - m) / jnp.sqrt(s + eps)).reshape(v.shape)

    def _ln_c(v, eps=1e-06):
        m = jnp.mean(v, axis=1, keepdims=True)
        s = jnp.var(v, axis=1, keepdims=True)
        return (v - m) / jnp.sqrt(s + eps)

    def _ln_t(v, eps=1e-05):
        m = jnp.mean(v, axis=-1, keepdims=True)
        s = jnp.var(v, axis=-1, keepdims=True)
        return (v - m) / jnp.sqrt(s + eps)

    def _to_tokens(v):
        B_, C_, H_, W_ = v.shape
        return v.reshape(B_, C_, H_ * W_).transpose(0, 2, 1)

    def _from_tokens(t, like):
        B_, C_, H_, W_ = like.shape
        return t.transpose(0, 2, 1).reshape(B_, C_, H_, W_)
    x = _L0_conv_ref(x, L0_conv_wq, L0_conv_bq, L0_conv_wk, L0_conv_bk, L0_conv_wv, L0_conv_bv, L0_conv_gamma)
    x = _L1_conv_ref(x, L1_conv_mask_attention, L1_conv_w_tm, L1_conv_b_tm, L1_conv_w_tr, L1_conv_b_tr, L1_conv_w_deform, L1_conv_bn_gamma, L1_conv_bn_beta, L1_conv_bn_mean, L1_conv_bn_var)
    x = _L2_conv_ref(x, L2_conv_gn_w, L2_conv_gn_b, L2_conv_w_qkv, L2_conv_b_qkv, L2_conv_w_proj, L2_conv_b_proj)
    x = _L3_conv_ref(x, L3_conv_weight, L3_conv_bias)
    return x

_drawn_inputs = setup_inputs


def setup_inputs(seed=0):
    import zlib

    import numpy as np

    out = dict(_drawn_inputs(seed))
    spreads = {'L0_conv_bq': (0.0, 0.8),
     'L0_conv_bk': (0.0, 0.1),
     'L0_conv_bv': (0.0, 0.1),
     'L1_conv_bn_gamma': (1.0, 0.2),
     'L1_conv_bn_beta': (0.0, 0.1),
     'L2_conv_gn_w': (1.0, 0.2),
     'L2_conv_gn_b': (0.0, 0.625),
     'L2_conv_b_qkv': (0.0, 0.8),
     'L2_conv_b_proj': (0.0, 0.8),
     'L3_conv_weight': (1.0, 0.2),
     'L3_conv_bias': (0.0, 0.1)}
    factors = {'L1_conv_b_tr': 8.0, 'L1_conv_bn_mean': 8.0}
    for name, (base, spread) in spreads.items():
        noise = np.random.default_rng([zlib.crc32(name.encode()), seed]).standard_normal(out[name].shape)
        drawn = base * np.exp(spread * noise) if base else spread * noise
        out[name] = jnp.asarray(drawn.astype(out[name].dtype))
    for name, factor in factors.items():
        out[name] = (out[name] * factor).astype(out[name].dtype)
    return out
```

```python
from contextlib import ExitStack

import concourse.bass as bass
import numpy as np
from concourse import mybir

F32 = mybir.dt.float32
BF16 = mybir.dt.bfloat16
I32 = mybir.dt.int32
ALU = mybir.AluOpType
ACT = mybir.ActivationFunctionType
AX = mybir.AxisListType

IMAGES, C, H, W = 32, 64, 32, 32
PX = H * W
P = 128
TILES = PX // P
HALF = PX // 2
D = 16
HEADS = C // D
TAPS = 9
CORNERS = 4
PARTS = 6
ROWS = PARTS * D
MROW = ROWS
STACK = ROWS + 2
ONE = C
STAT_PARTS = (0, 0, 1, 1, 0, 2)
MOV_PARTS = (0, 1, 0, 1, 2, 0)
MAP_H, MAP_W = H + 1, W + 2
TABLE = MAP_H * MAP_W
EPS = 1e-5
GROUP = 16
STEPS = 5
REG = ((-1, -1, -1, 0, 0, 0, 1, 1, 1), (-1, 0, 1, -1, 0, 1, -1, 0, 1))
CONV_GROUPS = ((0, 1, 2), (3, 4), (5, 6), (7, 8))
OFFS = 2 * TAPS

SHIFT = {"A": 0, "B": 1, "C1": 2, "C2": 3, "C3": 4}
LAST_SHIFT = 4
D_STEPS = {"qk0": 1, "max0": 1, "offsets": 1, "deform": 1, "stat": 1, "qk2": 1, "max2": 1, "sums": 1, "proj": 1,
           "sigma": 1}
E_STEPS = {"v0": 1, "mrow0": 1, "exp0": 1, "xt": 1, "conv": 1, "turn": 2, "v2": 1, "mrow2": 1, "exp2": 1, "x2t": 1}
D_USES = {"A": 10, "B": 8, "C1": 34, "C2": 0, "C3": 4}
E_USES = {"A": 24, "B": 16, "C1": 10, "C2": 64, "C3": 2}
SPLITS, NEGS, NORMS, OFFSET_OPS, STAT_OPS = 3, 2, 3, 14, 23


class Image:

    def __init__(self, j, c):
        self.j, self.c = j, c
        self.parity = c % 2
        self.n = c if isinstance(j, int) else j * 2 + c

    def at(self, per_image, k):
        const = self.c * per_image + k
        return const if isinstance(self.j, int) else self.j * (2 * per_image) + const

    def at_own_parity(self, per_image, k):
        const = self.c // 2 * per_image + k
        return const if isinstance(self.j, int) else self.j * per_image + const


class Iteration:

    def __init__(self, j, c):
        self.j, self.c = j, c
        loop = not isinstance(j, int)
        self.image = {s: Image(j, c - sh) for s, sh in SHIFT.items() if loop or 0 <= c - sh < IMAGES}
        self.steps = order(self.image)
        self.numbers = {}
        for ring, steps in (("d", D_STEPS), ("e", E_STEPS)):
            k = 0
            for _, name, *args in self.steps:
                for use in range(steps.get(name, 0)):
                    self.numbers[(ring, name, *args, use)] = k
                    k += 1

    def _count(self, ring, uses, name, args, use):
        const, slope = self.numbers[(ring, name, *args, use)] + 1, 0
        for s, sh in SHIFT.items():
            if isinstance(self.j, int):
                const += uses[s] * min(max(self.c - sh, 0), IMAGES)
            else:
                const += uses[s] * (self.c - sh)
                slope += 2 * uses[s]
        return const if isinstance(self.j, int) else self.j * slope + const

    def d(self, name, *args, use=0):
        return self._count("d", D_USES, name, args, use)

    def e(self, name, *args, use=0):
        return self._count("e", E_USES, name, args, use)

    def slot(self, ring, name, *args, use=0):
        return self.numbers[(ring, name, *args, use)] % 2

    def before(self):
        return Iteration(self.j, self.c - 1)

    def has_before(self, stage):
        return not isinstance(self.j, int) or 0 <= self.c - 1 - SHIFT[stage] < IMAGES


def wait(eng, sem, value):
    if not (isinstance(value, int) and value <= 0):
        eng.wait_ge(sem, value)


class Chain:

    def __init__(self, eng, sem, image, per_image, first=0):
        self.eng, self.sem, self.image, self.per_image, self.k = eng, sem, image, per_image, first

    def __call__(self, instruction):
        self.k += 1
        instruction.then_inc(self.sem, 1)
        self.eng.wait_ge(self.sem, self.image.at(self.per_image, self.k))


def order(image):
    s = []
    if "A" in image:
        s += [(0.0, "load"), (0.6, "qk0"), (0.61, "split0"), (0.62, "spread0"), (0.65, "v0", 0), (0.66, "v0", 1)]
        s += [(1.3 + 0.08 * t, "max0", t) for t in range(TILES)]
        s += [(1.95, "neg0"), (2.02, "mrow0", 0), (2.04, "mrow0", 1)]
        s += [(2.1 + 0.08 * u, "exp0", u // 2, u % 2) for u in range(16)]
        s += [(3.45, "pv0_end"), (3.46, "norm0"), (3.75, "shift0"), (3.7, "xt", 0), (3.72, "xt", 1), (3.74, "map"),
              (3.9, "conv", 0), (4.0, "conv", 1), (4.15, "offsets")]
    if "B" in image:
        s += [(t - 0.3, "gather", t) for t in range(TILES)]
        s += [(t + 0.1, "scale", t) for t in range(TILES)]
        s += [(t + 0.5, "turn", t) for t in range(TILES)]
        s += [(t + 0.85, "deform", t) for t in range(TILES)]
        s += [(t + 0.95, "relu", t) for t in range(TILES)]
    if "C1" in image:
        s += [(0.2, "stat"), (0.44, "qk2"), (0.45, "split2"), (0.46, "spread2"), (0.47, "v2", 0), (0.48, "v2", 1),
              (0.9, "keep")]
        s += [(2.0 + 0.17 * u, "max2", u // TILES, u % TILES) for u in range(32)]
        s += [(2.0 + 0.17 * (8 * h + 7) + 0.01, "neg2", h) for h in range(HEADS)]
        s += [(2.0 + 0.17 * (8 * h + 7) + 0.3 + 0.1 * b, "mrow2", h, b) for h in range(HEADS) for b in range(2)]
    if "C2" in image:
        s += [(4.3 + 0.054 * u, "exp2", u // 4, u % 4) for u in range(64)]
        s += [(7.95, "pv2_end")]
    if "C3" in image:
        s += [(0.02, "attended"), (0.12, "sums"), (0.4, "proj", 0), (0.41, "proj", 1), (0.42, "store"),
              (0.85, "x2t", 0), (0.86, "x2t", 1), (1.15, "sigma")]
    return sorted(s, key=lambda step: step[0])


def build(nc, a, out):
    with ExitStack() as ctx:
        def sb(name, shape, dt=F32):
            return ctx.enter_context(nc.sbuf_tensor(name, shape, dt))

        def sem(name):
            return ctx.enter_context(nc.semaphore(name))

        parts0_d = nc.dram_tensor("parts0_d", (2, 3, 2 * D, PX), BF16, kind="Internal").ap()
        parts2_d = nc.dram_tensor("parts2_d", (2, 3, 2 * C, PX), BF16, kind="Internal").ap()
        table_d = [nc.dram_tensor(f"table{p}_d", (TABLE, 2 * C), F32, kind="Internal").ap() for p in range(2)]
        x2_d = nc.dram_tensor("x2_d", (IMAGES, C, PX), F32, kind="Internal").ap()

        identf = sb("identf", [P, P])
        identb = sb("identb", [P, P], BF16)
        wqk0 = sb("wqk0", [ONE + 1, 2 * D])
        wv0 = sb("wv0", [ONE + 1, P])
        w6 = sb("w6", [ONE + 1, TAPS, 6])
        woff = sb("woff", [ONE + 1, TAPS, 32])
        grid = sb("grid", [P, TILES, OFFS])
        gather_sel = sb("gather_sel", [P, P])
        wd = sb("wd", [P, 5, C])
        wqk2 = sb("wqk2", [ONE + 1, P])
        wv2 = sb("wv2", [ONE + 1, P])
        qscale = sb("qscale", [P, 1])
        group_mean = sb("group_mean", [C, P])
        sum_sel = sb("sum_sel", [P, P])
        wproj = sb("wproj", [P, C])
        vecs = sb("vecs", [C, 9])
        bn_g, bn_b, bn_m, bn_v, gn_w, gn_b, b_proj, gamma, bias3 = (vecs[:, k:k + 1] for k in range(9))
        w3row = sb("w3row", [C, C])
        mask = sb("mask", [C, C])
        bn = sb("bn", [C, 4])
        newton = sb("newton", [C, 4])
        zeros = sb("zeros", [MAP_W, P])
        nothing = sb("nothing", [1, 1])

        xin = sb("xin", [ONE + 1, 2, PX])
        parts0 = sb("parts0", [2 * D, 3, PX], BF16)
        rest = sb("rest", [P, PX])
        stat0 = sb("stat0", [STACK, PX], BF16)
        mov0 = sb("mov0", [STACK, PX], BF16)
        v0 = sb("v0", [P, TILES, P])
        mx0 = sb("mx0", [P, TILES])
        neg0 = sb("neg0", [P, TILES, 2], BF16)
        p0 = sb("p0", [P, 2, HALF])
        r0 = sb("r0", [C, PX])
        xc = sb("xc", [ONE + 1, 2, (H + 2) * W])
        xl = sb("xl", [ONE + 1, (H + 2) * W])
        xr = sb("xr", [ONE + 1, (H + 2) * W])
        xt = sb("xt", [P, TILES, C])
        cs = rest
        pos = sb("pos", [P, TILES, OFFS])
        flo = sb("flo", [P, TILES, OFFS])
        rnd = sb("rnd", [P, TILES, OFFS], I32)
        one_less = sb("one_less", [P, TILES, OFFS])
        idx = sb("idx", [P, 2, TILES, TAPS], I32)
        wt = sb("wt", [P, 2, TILES, TAPS, CORNERS])

        G = sb("G", [P, 2, TAPS * CORNERS * C])
        gs = sb("gs", [P, 2, CORNERS, TAPS * C])
        ts = sb("ts", [P, 2, 5 * P])
        y1 = sb("y1", [C, 2, P])
        x1 = sb("x1", [C, 2, PX])

        kept = sb("kept", [C, 2, PX])
        bnst = sb("bnst", [C, 2, 6])
        mv = sb("mv", [C, 4])
        stat_in = sb("stat_in", [C, P])
        gm = sb("gm", [C, 8])
        ha = sb("ha", [ONE + 1, PX])
        parts2 = sb("parts2", [P, 3, PX], BF16)
        stat2 = sb("stat2", [STACK, 2, HEADS, PX], BF16)
        mov2 = sb("mov2", [STACK, 2, HEADS, PX], BF16)
        va = sb("va", [P, 2, TILES, P])
        mx2 = sb("mx2", [P, HEADS, TILES])
        neg2 = sb("neg2", [P, HEADS, TILES, 2], BF16)
        p2 = sb("p2", [P, 2, HEADS, HALF])
        att = sb("att", [P, PX])
        r2 = sb("r2", [P, PX])
        x2 = sb("x2", [ONE + 1, PX])
        x2t = r2[:].rearrange("p (t c) -> p t c", c=P)
        sig = sb("sig", [C, P])

        mean = sb("mean", [C, 1])
        mrow = sb("mrow", [1, C])
        cov = sb("cov", [C, C])
        tmp = sb("tmp", [C, C])
        pm = sb("pm", [C, C])
        pa = sb("pa", [C, C])
        w2 = sb("w2", [P, P])
        b2 = sb("b2", [P, 1])
        tr = sb("tr", [C, 4])

        dring = [ctx.enter_context(nc.psum_tensor(f"dring{i}", [P, PX], F32)) for i in range(2)]
        ering = [ctx.enter_context(nc.psum_tensor(f"ering{i}", [P, HALF], F32)) for i in range(2)]
        o = ctx.enter_context(nc.psum_tensor("o", [P, PX], F32))

        s_w = sem("s_w")
        s_ones = sem("s_ones")
        s_border = sem("s_border")
        s_prep = sem("s_prep")
        d_full, d_read = sem("d_full"), sem("d_read")
        e_full, e_read = sem("e_full"), sem("e_read")
        x_in = [sem("x_in0"), sem("x_in1")]
        split0, parts0_out, stacks0_in = sem("split0"), sem("parts0_out"), sem("stacks0_in")
        neg0_done, pv0_done, norm0_done, shifted = sem("neg0_done"), sem("pv0_done"), sem("norm0_done"), sem("shifted")
        map_out, offsets_done = sem("map_out"), sem("offsets_done")
        gathered = [sem("gathered0"), sem("gathered1")]
        scaled, x1_ready = sem("scaled"), sem("x1_ready")
        stat_done, kept_ready = sem("stat_done"), sem("kept_ready")
        split2, parts2_out, stacks2_in = sem("split2"), sem("parts2_out"), sem("stacks2_in")
        neg2_done, pv2_done, o2_read = sem("neg2_done"), sem("pv2_done"), sem("o2_read")
        normed2, x2_out = sem("normed2"), sem("x2_out")
        carried = sem("carried")
        f_dve, f_pe, f_hold = sem("f_dve"), sem("f_pe"), sem("f_hold")
        fin_in = [sem("fin_in0"), sem("fin_in1")]
        fin_out = [sem("fin_out0"), sem("fin_out1")]

        loads = (
            (identf, "identf"), (wqk0, "wqk0"), (wv0, "wv0"), (w6, "w6"), (grid, "grid"),
            (gather_sel, "gather_sel"), (wqk2, "wqk2"), (wv2, "wv2"), (qscale, "qscale"), (group_mean, "group_mean"),
            (sum_sel, "sum_sel"), (wproj, "wproj"), (vecs, "vecs"), (mask, "mask"), (wd, "wd"))
        D_ALL = IMAGES * sum(D_USES.values())

        def run(eng, steps):
            def iteration(it):
                for _, name, *args in it.steps:
                    if name in steps:
                        steps[name](it, *args)
            for c in range(LAST_SHIFT):
                iteration(Iteration(0, c))
            with eng.Fori(LAST_SHIFT // 2, IMAGES // 2) as j:
                for c in range(2):
                    iteration(Iteration(j, c))
            for c in range(IMAGES, IMAGES + LAST_SHIFT):
                iteration(Iteration(0, c))

        ones = (xin[ONE:ONE + 1, :, :], ha[ONE:ONE + 1, :], x2[ONE:ONE + 1, :], xc[ONE:ONE + 1, :, :],
                xl[ONE:ONE + 1, :], xr[ONE:ONE + 1, :], stat0[MROW:STACK, :], stat2[MROW:STACK, :, :, :])
        blanks = (xc[0:C, :, :], xl[0:C, :], xr[0:C, :], zeros[:], sig[:], stat_in[:], woff[:], w2[:], nothing[:])
        N_ONES = len(ones) + len(blanks)
        N_PREP = 1 + 18 + 24 + 15

        fin_src = [p2[:, b, 0:2, :].rearrange("p a n -> p (a n)") for b in range(2)]
        fin_dst = [G[:, b, 0:PX] for b in range(2)]
        x2_pairs = x2_d.rearrange("(m two) c n -> m (two c) n", two=2)
        out_pairs = out.rearrange("(m two) c h w -> m (two c) (h w)", two=2)

        block = ctx.enter_context(nc.Block())

        @block.sync
        def _(sp):
            for tile, name in loads:
                sp.dma_start(tile[:], a[name]).then_inc(s_w, 16)
            sp.dma_start(w3row[:], a["w3row"]).then_inc(x2_out, 16)
            sp.wait_ge(s_ones, N_ONES)
            borders = [t.rearrange("(y x) c -> y x c", x=MAP_W) for t in table_d]
            for m in range(2):
                for y in (0, MAP_H - 1):
                    sp.dma_start(borders[m][y, :, :], zeros[0:MAP_W, :]).then_inc(s_border, 16)
            sp.wait_ge(s_border, 16 * 4)
            for m in range(2):
                for x in (0, MAP_W - 1):
                    sp.dma_start(borders[m][:, x, :], zeros[0:MAP_H, :]).then_inc(s_border, 16)
            sp.wait_ge(s_border, 16 * 8)

            def load(it):
                n = it.image["A"]
                wait(sp, norm0_done, n.at(NORMS, -NORMS))
                sp.dma_start(xin[0:C, n.parity, :], a["x"][bass.ds(n.n, 1), :, :].rearrange("o c n -> (o c) n"))\
                    .then_inc(x_in[n.parity], 16)

            def spread0(it):
                n = it.image["A"]
                sp.wait_ge(split0, n.at(SPLITS, SPLITS))
                sp.dma_start(parts0_d[n.parity].rearrange("t r n -> r t n"), parts0[:]).then_inc(parts0_out, 16)
                sp.wait_ge(parts0_out, n.at(16, 16))
                for b in range(PARTS):
                    sp.dma_start(stat0[D * b:D * b + D, :], parts0_d[n.parity, STAT_PARTS[b], 0:D, :])\
                        .then_inc(stacks0_in, 16)
                    sp.dma_start(mov0[D * b:D * b + D, :], parts0_d[n.parity, MOV_PARTS[b], D:2 * D, :])\
                        .then_inc(stacks0_in, 16)

            def table(it):
                n = it.image["A"]
                sp.wait_ge(e_read, it.e("xt", 1))
                for b in range(2):
                    wait(sp, gathered[b], n.at(TILES // 2 * TAPS * 16, -TILES // 2 * TAPS * 16))
                rows = table_d[n.parity].rearrange("(y x) (s c) -> y x s c", x=MAP_W, s=2)
                for r in range(P // W):
                    for s in range(2):
                        y = r + 1 - s
                        to = rows[y:y + 4 * (TILES - 1) + 1:4, 1:W + 1, s, :]
                        sp.dma_start(to.rearrange("t x c -> x t c"), xt[W * r:W * r + W, :, :]).then_inc(map_out, 16)

            def spread2(it):
                n = it.image["C1"]
                sp.wait_ge(split2, n.at(SPLITS, SPLITS))
                sp.dma_start(parts2_d[n.parity].rearrange("t r n -> r t n"), parts2[:]).then_inc(parts2_out, 16)
                sp.wait_ge(parts2_out, n.at(16, 16))
                for b in range(PARTS):
                    for stack, part, at in ((mov2, MOV_PARTS[b], 0), (stat2, STAT_PARTS[b], C)):
                        src = parts2_d[n.parity, part, at:at + C, :].rearrange("(h d) n -> d h n", h=HEADS)
                        sp.dma_start(stack[D * b:D * b + D, n.parity, :, :], src).then_inc(stacks2_in, 16)

            def store(it):
                n = it.image["C3"]
                sp.wait_ge(d_read, it.d("proj", 1))
                sp.dma_start(x2_d[bass.ds(n.n, 1), :, :].rearrange("o c n -> (o c) n"), x2[0:C, :]).then_inc(x2_out, 16)

            run(sp, {"load": load, "spread0": spread0, "map": table, "spread2": spread2, "store": store})

            sp.wait_ge(x2_out, 16 + 16 * IMAGES)
            with sp.Fori(0, IMAGES // 4) as j:
                for b in range(2):
                    sp.wait_ge(d_full, j * 2 + (D_ALL + b - 1))
                    sp.dma_start(fin_src[b], x2_pairs[bass.ds(j * 2 + b, 1), :, :].rearrange("o c n -> (o c) n"))\
                        .then_inc(fin_in[b], 16)
                for b in range(2):
                    sp.wait_ge(d_read, j * 2 + (D_ALL + b + 1))
                    sp.dma_start(out_pairs[bass.ds(j * 2 + b, 1), :, :].rearrange("o c n -> (o c) n"), fin_dst[b])\
                        .then_inc(fin_out[b], 16)
            for b in range(2):
                sp.wait_ge(fin_out[b], 16 * IMAGES // 4)

        @block.gpsimd
        def _(pool):
            pool.wait_ge(s_ones, N_ONES)

            def gather(it, t):
                n = it.image["B"]
                if t == 0:
                    pool.wait_ge(offsets_done, n.at(OFFSET_OPS, OFFSET_OPS))
                    pool.wait_ge(map_out, n.at(8 * 16, 8 * 16))
                wait(pool, carried, n.at(TILES, t))
                wait(pool, scaled, n.at(2 * TILES, 2 * (t - 2) + 1))
                pool.tensor_tensor(nothing[:], nothing[:], nothing[:], ALU.add).then_inc(carried, 1)
                for k in range(TAPS):
                    pool.indirect_dma_start(
                        G[:, t % 2, CORNERS * C * k:CORNERS * C * (k + 1)], None, table_d[n.parity],
                        bass.IndirectOffsetOnAxis(idx[:, n.parity, t, k:k + 1], 0)).then_inc(gathered[t % 2], 16)

            run(pool, {"gather": gather})

        @block.vector
        def _(dve):
            def newton_rsqrt(step, v, y, t):
                step(dve.tensor_scalar(y.bitcast(I32), v.bitcast(I32), 1, None, ALU.logical_shift_right))
                step(dve.tensor_scalar(y.bitcast(I32), y.bitcast(I32), -1.0, float(0x5F3759DF), ALU.mult, ALU.add))
                for _ in range(3):
                    step(dve.scalar_tensor_tensor(t, y, v, y, ALU.mult, ALU.mult))
                    step(dve.tensor_scalar(t, t, -0.5, 1.5, ALU.mult, ALU.add))
                    step(dve.tensor_tensor(y, y, t, ALU.mult))

            def take(it, name, *args):
                dve.wait_ge(d_full, it.d(name, *args))
                return dring[it.slot("d", name, *args)]

            def split(it, name, n, parts, sem, rows, scale):
                slot = take(it, name)[0:rows, :]
                step = Chain(dve, sem, n, SPLITS)
                rs = rest[0:rows, :]
                if scale is None:
                    step(dve.tensor_copy(parts[:, 0, :], slot))
                    dve.tensor_tensor(rs, slot, parts[:, 0, :], ALU.subtract).then_inc(d_read, 1)
                else:
                    step(dve.tensor_scalar(parts[:, 0, :], slot, scale, None, ALU.mult))
                    dve.scalar_tensor_tensor(rs, slot, scale, parts[:, 0, :], ALU.mult, ALU.subtract)\
                        .then_inc(d_read, 1)
                dve.wait_ge(d_read, it.d(name))
                step(dve.tensor_copy(parts[:, 1, :], rs))
                step(dve.tensor_tensor(parts[:, 2, :], rs, parts[:, 1, :], ALU.subtract))

            def split_l0(it):
                n = it.image["A"]
                wait(dve, parts0_out, n.at(16, 0))
                split(it, "qk0", n, parts0, split0, 2 * D, None)

            def max0(it, t):
                slot = take(it, "max0", t)
                dve.tensor_reduce(mx0[:, t:t + 1], slot[:], AX.X, ALU.max).then_inc(d_read, 1)

            def neg(it, last, sem, n, per_image, first, mx, to):
                dve.wait_ge(d_read, last)
                step = Chain(dve, sem, n, per_image, first)
                step(dve.tensor_scalar(to[:, :, 0], mx, -1.0, None, ALU.mult))
                step(dve.scalar_tensor_tensor(to[:, :, 1], mx, -1.0, to[:, :, 0], ALU.mult, ALU.subtract))

            def neg_l0(it):
                n = it.image["A"]
                if it.has_before("A"):
                    dve.wait_ge(e_full, it.before().e("mrow0", 1))
                neg(it, it.d("max0", TILES - 1), neg0_done, n, NEGS, 0, mx0[:], neg0[:])

            def norm0(it):
                n = it.image["A"]
                dve.wait_ge(pv0_done, n.at(16, 16))
                step = Chain(dve, norm0_done, n, NORMS)
                step(dve.reciprocal(r0[:], o[C:2 * C, :]))
                step(dve.scalar_tensor_tensor(r0[:], o[0:C, :], gamma, r0[:], ALU.mult, ALU.mult))
                step(dve.tensor_tensor(xc[0:C, n.parity, W:W + PX], r0[:], xin[0:C, n.parity, :], ALU.add))

            def offsets(it):
                n = it.image["A"]
                slot = take(it, "offsets").rearrange("p (t c) -> p t c", c=P)
                step = Chain(dve, offsets_done, n, OFFSET_OPS)
                dve.tensor_tensor(pos[:], slot[:, :, 0:OFFS], grid[:], ALU.add).then_inc(d_read, 1)
                dve.wait_ge(d_read, it.d("offsets"))
                step(dve.tensor_scalar(pos[:], pos[:], float(H + 1), 0.0, ALU.min, ALU.max))
                step(dve.tensor_copy(rnd[:], pos[:]))
                step(dve.tensor_copy(flo[:], rnd[:]))
                step(dve.tensor_tensor(one_less[:], flo[:], pos[:], ALU.is_gt))
                step(dve.tensor_tensor(flo[:], flo[:], one_less[:], ALU.subtract))
                step(dve.tensor_scalar(flo[:], flo[:], float(H), None, ALU.min))
                step(dve.tensor_tensor(pos[:], pos[:], flo[:], ALU.subtract))
                step(dve.tensor_scalar(one_less[:], pos[:], -1.0, 1.0, ALU.mult, ALU.add))
                for dx in range(2):
                    for dy in range(2):
                        wy = (one_less, pos)[dy][:, :, 0:TAPS]
                        wx = (one_less, pos)[dx][:, :, TAPS:OFFS]
                        step(dve.tensor_tensor(wt[:, n.parity, :, :, 2 * dx + dy], wx, wy, ALU.mult))
                step(dve.tensor_scalar(one_less[:, :, 0:TAPS], flo[:, :, 0:TAPS], float(MAP_W), None,
                                       ALU.mult))
                step(dve.tensor_tensor(idx[:, n.parity], one_less[:, :, 0:TAPS], flo[:, :, TAPS:OFFS], ALU.add))
                assert step.k == OFFSET_OPS

            def scale(it, t):
                n = it.image["B"]
                if t == 0:
                    dve.wait_ge(offsets_done, n.at(OFFSET_OPS, OFFSET_OPS))
                per = TAPS * 16
                dve.wait_ge(gathered[t % 2], n.at(TILES // 2 * per, (t // 2 + 1) * per))
                if t >= 2:
                    dve.wait_ge(e_full, it.e("turn", t - 2, use=1))
                elif it.has_before("B"):
                    dve.wait_ge(e_full, it.before().e("turn", TILES + t - 2, use=1))
                step = Chain(dve, scaled, n, 2 * TILES, 2 * t)
                g = G[:, t % 2, :].rearrange("p (k c d) -> p k c d", k=TAPS, c=CORNERS)
                to = gs[:, t % 2, :, :].rearrange("p c (k d) -> p k c d", k=TAPS)
                by = wt[:, n.parity, t, :, :].unsqueeze(3).broadcast_to([P, TAPS, CORNERS, C])
                step(dve.tensor_tensor(to, g, by, ALU.mult))
                step(dve.tensor_tensor(gs[:, t % 2, 0:2, :], gs[:, t % 2, 0:2, :], gs[:, t % 2, 2:4, :], ALU.add))

            def deform(it, t):
                n = it.image["B"]
                slot = take(it, "deform", t)
                wait(dve, x1_ready, n.at(TILES, t - 1))
                dve.scalar_tensor_tensor(y1[:, t % 2, :], slot[0:C, 0:P], bn[:, 1:2],
                                         xc[0:C, n.parity, W + t * P:W + (t + 1) * P], ALU.mult, ALU.add)\
                    .then_inc(d_read, 1)

            def stat(it):
                n = it.image["C1"]
                dve.wait_ge(x1_ready, n.at(TILES, TILES))
                step = Chain(dve, stat_done, n, STAT_OPS)
                for b in range(2):
                    step(dve.bn_stats(bnst[:, b, :], x1[:, n.parity, b * HALF:(b + 1) * HALF]))
                sets = bnst[:].rearrange("p a (b s) -> p (a b) s", s=3)
                step(dve.tensor_tensor(mv[:], sets[:, :, 1], sets[:, :, 1], ALU.mult))
                step(dve.scalar_tensor_tensor(mv[:], sets[:, :, 2], 4.0 / PX, mv[:], ALU.mult, ALU.add))
                step(dve.tensor_reduce(stat_in[:, 1:2], mv[:], AX.X, ALU.add))
                step(dve.tensor_reduce(stat_in[:, 0:1], sets[:, :, 1], AX.X, ALU.add))
                slot = take(it, "stat")
                dve.tensor_copy(gm[:, 0:2], slot[0:C, 0:2]).then_inc(d_read, 1)
                dve.wait_ge(d_read, it.d("stat"))
                step(dve.tensor_tensor(gm[:, 2:3], gm[:, 0:1], gm[:, 0:1], ALU.mult))
                step(dve.scalar_tensor_tensor(gm[:, 3:4], gm[:, 1:2], EPS, gm[:, 2:3], ALU.add, ALU.subtract))
                newton_rsqrt(step, gm[:, 3:4], gm[:, 4:5], gm[:, 5:6])
                step(dve.tensor_tensor(gm[:, 5:6], gm[:, 4:5], gn_w, ALU.mult))
                step(dve.tensor_tensor(gm[:, 6:7], gm[:, 0:1], gm[:, 5:6], ALU.mult))
                step(dve.tensor_tensor(gm[:, 7:8], gn_b, gm[:, 6:7], ALU.subtract))
                if it.has_before("C1"):
                    dve.wait_ge(e_full, it.before().e("v2", 1))
                step(dve.tensor_scalar(ha[0:C, :], x1[:, n.parity, :], gm[:, 5:6], gm[:, 7:8], ALU.mult, ALU.add))
                assert step.k == STAT_OPS

            def split_l2(it):
                n = it.image["C1"]
                wait(dve, parts2_out, n.at(16, 0))
                split(it, "qk2", n, parts2, split2, P, qscale[:])

            def max2(it, h, t):
                slot = take(it, "max2", h, t)
                dve.tensor_reduce(mx2[:, h, t:t + 1], slot[:], AX.X, ALU.max).then_inc(d_read, 1)

            def neg_l2(it, h):
                n = it.image["C1"]
                if it.has_before("C1"):
                    dve.wait_ge(e_full, it.before().e("mrow2", h, 1))
                neg(it, it.d("max2", h, TILES - 1), neg2_done, n, NEGS * HEADS, NEGS * h, mx2[:, h, :], neg2[:, h])

            def sums(it):
                n = it.image["C3"]
                slot = take(it, "sums")
                if it.has_before("C3"):
                    dve.wait_ge(d_full, it.before().d("sigma"))
                dve.wait_ge(o2_read, n.at(1, 1))
                dve.reciprocal(r2[:], slot[:]).then_inc(d_read, 1)
                dve.wait_ge(d_read, it.d("sums"))
                dve.tensor_tensor(r2[:], r2[:], att[:], ALU.mult).then_inc(normed2, 1)

            def proj(it, b):
                n = it.image["C3"]
                slot = take(it, "proj", b)
                if b == 0:
                    dve.wait_ge(kept_ready, n.at(1, 1))
                    dve.wait_ge(x2_out, n.at(16, 16))
                    if it.has_before("C3"):
                        dve.wait_ge(e_full, it.before().e("x2t", 1))
                cols = slice(b * HALF, (b + 1) * HALF)
                dve.scalar_tensor_tensor(x2[0:C, cols], slot[0:C, 0:HALF], b_proj, kept[:, n.parity, cols],
                                         ALU.add, ALU.add).then_inc(d_read, 1)

            def sigma(it):
                slot = take(it, "sigma")
                dve.tensor_tensor(sig[:], sig[:], slot[0:C, 0:P], ALU.add).then_inc(d_read, 1)

            for tile in ones:
                dve.memset(tile, 1.0).then_inc(s_ones, 1)
            for tile in blanks:
                dve.memset(tile, 0.0).then_inc(s_ones, 1)
            dve.wait_ge(s_w, 16 * len(loads))
            dve.wait_ge(s_ones, N_ONES)
            step = Chain(dve, s_prep, Image(0, 0), 0)
            step(dve.tensor_copy(identb[:], identf[:]))
            for axis in range(2):
                for k in range(TAPS):
                    to = woff[:, :, TAPS * axis + k]
                    step(dve.tensor_copy(to, w6[:, :, 4 + axis]))
                    for j in range(2):
                        if REG[j][k]:
                            step(dve.tensor_tensor(to, to, w6[:, :, 2 * axis + j],
                                                   ALU.add if REG[j][k] > 0 else ALU.subtract))
            step(dve.tensor_scalar(bn[:, 0:1], bn_v, EPS, None, ALU.add))
            newton_rsqrt(step, bn[:, 0:1], newton[:, 0:1], newton[:, 1:2])
            step(dve.tensor_tensor(bn[:, 1:2], newton[:, 0:1], bn_g, ALU.mult))
            step(dve.tensor_tensor(bn[:, 2:3], bn_m, bn[:, 1:2], ALU.mult))
            step(dve.tensor_tensor(bn[:, 3:4], bn_b, bn[:, 2:3], ALU.subtract))
            assert step.k == N_PREP, step.k
            run(dve, {"split0": split_l0, "max0": max0, "neg0": neg_l0, "norm0": norm0, "offsets": offsets,
                      "scale": scale, "deform": deform, "stat": stat, "split2": split_l2, "max2": max2,
                      "neg2": neg_l2, "sums": sums, "proj": proj, "sigma": sigma})

            dve.wait_ge(d_read, D_ALL)
            step = Chain(dve, f_dve, Image(0, 0), 0)
            count = [0]
            small = dring[0]

            def product():
                count[0] += 1
                dve.wait_ge(f_pe, count[0])

            def hold(instruction):
                held[0] += 1
                instruction.then_inc(f_hold, 1)
                dve.wait_ge(f_hold, held[0])

            held = [0]
            hold(dve.tensor_scalar(mean[:], sig[:, C:C + 1], 1.0 / (IMAGES * PX), None, ALU.mult))
            step(dve.tensor_scalar(cov[:], sig[:, 0:C], 1.0 / (IMAGES * PX), None, ALU.mult))
            product()
            step(dve.tensor_copy(mrow[:], small[0:1, 0:C]))
            product()
            hold(dve.tensor_tensor(cov[:], cov[:], small[0:C, 0:C], ALU.subtract))
            hold(dve.scalar_tensor_tensor(cov[:], identf[0:C, 0:C], EPS, cov[:], ALU.mult, ALU.add))
            hold(dve.tensor_tensor(cov[:], cov[:], mask[:], ALU.mult))
            hold(dve.tensor_tensor(tmp[:], cov[:], identf[0:C, 0:C], ALU.mult))
            step(dve.tensor_reduce(tr[:, 0:1], tmp[:], AX.X, ALU.add))
            product()
            hold(dve.tensor_copy(tr[:, 1:2], small[0:C, 0:1]))
            hold(dve.reciprocal(tr[:, 2:3], tr[:, 1:2]))
            hold(dve.tensor_scalar(cov[:], cov[:], tr[:, 2:3], None, ALU.mult))
            newton_rsqrt(hold, tr[:, 1:2], tr[:, 2:3], tr[:, 3:4])
            step(dve.tensor_copy(pm[:], identf[0:C, 0:C]))
            for k in range(STEPS):
                product()
                step(dve.tensor_copy(pa[:], small[0:C, 0:C]))
                product()
                step(dve.tensor_copy(tmp[:], small[0:C, 0:C]))
                product()
                hold(dve.tensor_scalar(pm[:], pm[:], 1.5, None, ALU.mult))
                (step if k < STEPS - 1 else hold)(dve.scalar_tensor_tensor(pm[:], small[0:C, 0:C], -0.5, pm[:], ALU.mult, ALU.add))
            dve.wait_ge(x2_out, 16)
            hold(dve.scalar_tensor_tensor(w2[0:C, 0:C], pm[:], tr[:, 2:3], w3row[:], ALU.mult, ALU.mult))
            step(dve.tensor_copy(w2[C:P, C:P], w2[0:C, 0:C]))
            product()
            hold(dve.tensor_tensor(b2[0:C, :], bias3, small[0:C, 0:1], ALU.subtract))
            step(dve.tensor_copy(b2[C:P, :], b2[0:C, :]))

            def last(j, b):
                dve.wait_ge(d_full, j * 2 + (D_ALL + b + 1))
                dve.tensor_scalar(fin_dst[b], dring[b][:], b2[:], None, ALU.add).then_inc(d_read, 1)

            for b in range(2):
                last(0, b)
            with dve.Fori(1, IMAGES // 4) as j:
                for b in range(2):
                    dve.wait_ge(fin_out[b], j * 16)
                    last(j, b)

        @block.tensor
        def _(pe):
            def d_slot(it, name, *args):
                wait(pe, d_read, it.d(name, *args) + (-2))
                return dring[it.slot("d", name, *args)]

            def e_slot(it, name, *args, use=0):
                wait(pe, e_read, it.e(name, *args, use=use) + (-2))
                return ering[it.slot("e", name, *args, use=use)]

            def mm(to, lhsT, rhs, start=True, stop=True):
                return pe.matmul(to, lhsT, rhs, start=start, stop=stop)

            def halves(to, lhsT, rhs):
                for b in range(2):
                    last = mm(to[:, b * HALF:(b + 1) * HALF], lhsT, rhs[:, b * HALF:(b + 1) * HALF])
                return last

            def qk0(it):
                n = it.image["A"]
                pe.wait_ge(x_in[n.parity], n.at_own_parity(16, 16))
                halves(d_slot(it, "qk0")[0:2 * D, :], wqk0[:], xin[:, n.parity, :]).then_inc(d_full, 1)

            def v_l0(it, b):
                n = it.image["A"]
                slot = e_slot(it, "v0", b)
                for t in range(4):
                    px = (4 * b + t) * P
                    last = mm(slot[:, t * P:(t + 1) * P], xin[:, n.parity, px:px + P], wv0[:])
                last.then_inc(e_full, 1)

            def max0(it, t):
                n = it.image["A"]
                if t == 0:
                    pe.wait_ge(stacks0_in, n.at(2 * PARTS * 16, 2 * PARTS * 16))
                halves(d_slot(it, "max0", t), mov0[0:ROWS, t * P:(t + 1) * P], stat0[0:ROWS, :]).then_inc(d_full, 1)

            def mrow0(it, b):
                n = it.image["A"]
                slot = e_slot(it, "mrow0", b)
                pe.wait_ge(neg0_done, n.at(NEGS, NEGS))
                for t in range(4):
                    last = mm(slot[MROW:STACK, t * P:(t + 1) * P], neg0[:, 4 * b + t, :], identb[:])
                last.then_inc(e_full, 1)

            def pv0(it, t, b):
                pe.wait_ge(e_read, it.e("exp0", t, b))
                mm(o[:, b * HALF:(b + 1) * HALF], v0[:, t, :], p0[:, b, :], t == 0, t == TILES - 1)\
                    .then_inc(pv0_done, 1)

            def exp0(it, t, b):
                if t == 0 and b == 0:
                    pe.wait_ge(e_read, it.e("mrow0", 1))
                    done = it.image["C2"].at(1, 0) if "C2" in it.image else max(0, min(it.c - SHIFT["C2"], IMAGES))
                    wait(pe, o2_read, done)
                mm(e_slot(it, "exp0", t, b)[:], stat0[:, t * P:(t + 1) * P], mov0[:, b * HALF:(b + 1) * HALF])\
                    .then_inc(e_full, 1)
                if t or b:
                    pv0(it, t if b else t - 1, 1 - b)

            def pv0_end(it):
                pv0(it, TILES - 1, 1)

            def xt_step(it, b):
                n = it.image["A"]
                slot = e_slot(it, "xt", b)
                pe.wait_ge(norm0_done, n.at(NORMS, NORMS))
                for t in range(4):
                    at = W + (4 * b + t) * P
                    last = mm(slot[:, t * P:(t + 1) * P], xc[:, n.parity, at:at + P], identf[0:ONE + 1, :])
                last.then_inc(e_full, 1)

            def conv(it, b):
                n = it.image["A"]
                slot = e_slot(it, "conv", b)
                pe.wait_ge(shifted, n.at(2, 2))
                for k in range(3):
                    for g, taps in enumerate(CONV_GROUPS):
                        if k < len(taps):
                            ky, kx = taps[k] // 3, taps[k] % 3
                            src = (xl, xc[:, n.parity, :], xr)[kx]
                            at = (ky + b * H // 2) * W
                            last = mm(slot[32 * g:32 * g + 32, :], woff[:, taps[k], :], src[:, at:at + HALF],
                                      k == 0, k == len(taps) - 1)
                last.then_inc(e_full, 1)

            def offsets(it):
                slot = d_slot(it, "offsets")
                pe.wait_ge(e_read, it.e("conv", 1))
                for t in range(TILES):
                    last = mm(slot[:, t * P:(t + 1) * P], cs[:, t * P:(t + 1) * P], gather_sel[:])
                last.then_inc(d_full, 1)

            def turn(it, t):
                n = it.image["B"]
                slot = e_slot(it, "turn", t)
                pe.wait_ge(scaled, n.at(2 * TILES, 2 * t + 2))
                for q in range(4):
                    for y in range(2):
                        last = mm(slot[:, q * P:(q + 1) * P], gs[:, t % 2, y, 2 * q * C:2 * (q + 1) * C], identf[:],
                                  y == 0, y == 1)
                last.then_inc(e_full, 1)
                slot = e_slot(it, "turn", t, use=1)
                for y in range(2):
                    last = mm(slot[0:C, 0:P], gs[:, t % 2, y, 8 * C:9 * C], identf[:], y == 0, y == 1)
                last.then_inc(e_full, 1)

            def deform(it, t):
                slot = d_slot(it, "deform", t)
                pe.wait_ge(e_read, it.e("turn", t, use=1))
                for q in range(5):
                    k = P if q < 4 else C
                    last = mm(slot[0:C, 0:P], wd[0:k, q, :], ts[0:k, t % 2, q * P:(q + 1) * P], q == 0, q == 4)
                last.then_inc(d_full, 1)

            def stat(it):
                n = it.image["C1"]
                slot = d_slot(it, "stat")
                pe.wait_ge(stat_done, n.at(STAT_OPS, 6))
                mm(slot[:, 0:P], group_mean[:], stat_in[:]).then_inc(d_full, 1)

            def qk2(it):
                n = it.image["C1"]
                slot = d_slot(it, "qk2")
                pe.wait_ge(stat_done, n.at(STAT_OPS, STAT_OPS))
                halves(slot, wqk2[:], ha[:]).then_inc(d_full, 1)

            def v_l2(it, b):
                slot = e_slot(it, "v2", b)
                for t in range(4):
                    px = (4 * b + t) * P
                    last = mm(slot[:, t * P:(t + 1) * P], ha[:, px:px + P], wv2[:])
                last.then_inc(e_full, 1)

            def max2(it, h, t):
                n = it.image["C1"]
                if h == 0 and t == 0:
                    pe.wait_ge(stacks2_in, n.at(2 * PARTS * 16, 2 * PARTS * 16))
                halves(d_slot(it, "max2", h, t), mov2[0:ROWS, n.parity, h, t * P:(t + 1) * P],
                       stat2[0:ROWS, n.parity, h, :]).then_inc(d_full, 1)

            def mrow2(it, h, b):
                n = it.image["C1"]
                slot = e_slot(it, "mrow2", h, b)
                pe.wait_ge(neg2_done, n.at(NEGS * HEADS, NEGS * (h + 1)))
                for t in range(4):
                    last = mm(slot[MROW:STACK, t * P:(t + 1) * P], neg2[:, h, 4 * b + t, :], identb[:])
                last.then_inc(e_full, 1)

            def pv2(it, w):
                n = it.image["C2"]
                pe.wait_ge(e_read, it.e("exp2", w, HEADS - 1))
                t, b = w // 2, w % 2
                for h in range(HEADS):
                    last = mm(o[32 * h:32 * h + 32, b * HALF:(b + 1) * HALF], va[:, n.parity, t, 32 * h:32 * h + 32],
                              p2[:, w % 2, h, :], t == 0, t == TILES - 1)
                last.then_inc(pv2_done, 1)

            def exp2(it, w, h):
                n = it.image["C2"]
                if w == 0 and h == 0:
                    pe.wait_ge(e_read, it.before().e("mrow2", HEADS - 1, 1))
                    done = it.image["A"].at(NORMS, 2) if "A" in it.image else NORMS * IMAGES
                    pe.wait_ge(norm0_done, done)
                t, b = w // 2, w % 2
                mm(e_slot(it, "exp2", w, h)[:], stat2[:, n.parity, h, t * P:(t + 1) * P],
                   mov2[:, n.parity, h, b * HALF:(b + 1) * HALF]).then_inc(e_full, 1)
                if h == 1 and w:
                    pv2(it, w - 1)

            def pv2_end(it):
                pv2(it, 15)

            def sums(it):
                n = it.image["C3"]
                slot = d_slot(it, "sums")
                pe.wait_ge(o2_read, n.at(1, 1))
                halves(slot, sum_sel[:], att[:]).then_inc(d_full, 1)

            def proj(it, b):
                n = it.image["C3"]
                slot = d_slot(it, "proj", b)
                pe.wait_ge(normed2, n.at(1, 1))
                mm(slot[0:C, 0:HALF], wproj[:], r2[:, b * HALF:(b + 1) * HALF]).then_inc(d_full, 1)

            def x2t_step(it, b):
                slot = e_slot(it, "x2t", b)
                pe.wait_ge(d_read, it.d("proj", 1))
                for t in range(4):
                    px = (4 * b + t) * P
                    last = mm(slot[:, t * P:(t + 1) * P], x2[:, px:px + P], identf[0:ONE + 1, :])
                last.then_inc(e_full, 1)

            def sigma(it):
                slot = d_slot(it, "sigma")
                pe.wait_ge(e_read, it.e("x2t", 1))
                for t in range(TILES):
                    last = mm(slot[0:C, 0:P], x2t[:, t, 0:C], x2t[:, t, :], t == 0, t == TILES - 1)
                last.then_inc(d_full, 1)

            pe.wait_ge(s_w, 16 * len(loads))
            pe.wait_ge(s_ones, N_ONES)
            pe.wait_ge(s_prep, N_PREP)
            run(pe, {"qk0": qk0, "v0": v_l0, "max0": max0, "mrow0": mrow0, "exp0": exp0, "pv0_end": pv0_end,
                     "xt": xt_step, "conv": conv, "offsets": offsets, "turn": turn, "deform": deform, "stat": stat,
                     "qk2": qk2, "v2": v_l2, "max2": max2, "mrow2": mrow2, "exp2": exp2, "pv2_end": pv2_end,
                     "sums": sums, "proj": proj, "x2t": x2t_step, "sigma": sigma})

            small = dring[0]
            k = [0]

            def product(rows, cols, lhsT, rhs):
                k[0] += 1
                pe.wait_ge(f_dve, k[0])
                mm(small[0:rows, 0:cols], lhsT, rhs).then_inc(f_pe, 1)

            product(1, C, mean[:], identf[0:C, 0:C])
            product(C, C, mrow[:], mrow[:])
            product(C, 1, mask[:], tr[:, 0:1])
            for _ in range(STEPS):
                product(C, C, pm[:], pm[:])
                product(C, C, pa[:], pm[:])
                product(C, C, tmp[:], cov[:])
            product(C, 1, w2[0:C, 0:C], mean[:])
            pe.wait_ge(f_dve, k[0] + 1)
            with pe.Fori(0, IMAGES // 4) as j:
                for b in range(2):
                    pe.wait_ge(fin_in[b], j * 16 + 16)
                    pe.wait_ge(d_read, j * 2 + (D_ALL + b - 1))
                    halves(dring[b], w2[:], fin_src[b]).then_inc(d_full, 1)

        @block.scalar
        def _(act):
            def take(it, name, *args, use=0):
                act.wait_ge(e_full, it.e(name, *args, use=use))
                return ering[it.slot("e", name, *args, use=use)]

            def v_l0(it, b):
                n = it.image["A"]
                slot = take(it, "v0", b)
                wait(act, pv0_done, n.at(16, 0))
                act.activation(v0[:, 4 * b:4 * b + 4, :].rearrange("p t c -> p (t c)"), slot[:], ACT.Copy)\
                    .then_inc(e_read, 1)

            def mrow0(it, b):
                slot = take(it, "mrow0", b)
                act.activation(mov0[MROW:STACK, b * HALF:(b + 1) * HALF], slot[MROW:STACK, :], ACT.Copy)\
                    .then_inc(e_read, 1)

            def exp0(it, t, b):
                n = it.image["A"]
                slot = take(it, "exp0", t, b)
                wait(act, pv0_done, n.at(16, 2 * t + b - 1))
                act.activation(p0[:, b, :], slot[:], ACT.Exp).then_inc(e_read, 1)

            def shift0(it):
                n = it.image["A"]
                act.wait_ge(norm0_done, n.at(NORMS, NORMS))
                if it.has_before("A"):
                    act.wait_ge(e_full, it.before().e("conv", 1))
                rows = slice(1, H + 1)
                mid, left, right = (x.rearrange("c (y x) -> c y x", x=W) for x in (xc[0:C, n.parity, :], xl[0:C, :], xr[0:C, :]))
                act.activation(left[:, rows, 1:W], mid[:, rows, 0:W - 1], ACT.Copy).then_inc(shifted, 1)
                act.activation(right[:, rows, 0:W - 1], mid[:, rows, 1:W], ACT.Copy).then_inc(shifted, 1)

            def xt_step(it, b):
                n = it.image["A"]
                slot = take(it, "xt", b).rearrange("p (t c) -> p t c", c=P)
                wait(act, map_out, n.at(8 * 16, 0))
                act.activation(xt[:, 4 * b:4 * b + 4, :], slot[:, :, 0:C], ACT.Copy).then_inc(e_read, 1)

            def conv(it, b):
                slot = take(it, "conv", b)
                if it.has_before("A"):
                    act.wait_ge(d_full, it.before().d("offsets"))
                act.wait_ge(split0, it.image["A"].at(SPLITS, SPLITS))
                if "C1" in it.image:
                    act.wait_ge(split2, it.image["C1"].at(SPLITS, SPLITS))
                act.activation(cs[:, b * HALF:(b + 1) * HALF], slot[:], ACT.Copy).then_inc(e_read, 1)

            def turn(it, t):
                slot = take(it, "turn", t)
                if t >= 2:
                    act.wait_ge(d_full, it.d("deform", t - 2))
                elif it.has_before("B"):
                    act.wait_ge(d_full, it.before().d("deform", TILES + t - 2))
                act.activation(ts[:, t % 2, 0:4 * P], slot[:], ACT.Copy).then_inc(e_read, 1)
                slot = take(it, "turn", t, use=1)
                act.activation(ts[0:C, t % 2, 4 * P:5 * P], slot[0:C, 0:P], ACT.Copy).then_inc(e_read, 1)

            def relu(it, t):
                n = it.image["B"]
                act.wait_ge(d_read, it.d("deform", t))
                if t == 0:
                    wait(act, stat_done, n.at(STAT_OPS, -STAT_OPS))
                    wait(act, kept_ready, n.at(1, -1))
                act.activation(x1[:, n.parity, t * P:(t + 1) * P], y1[:, t % 2, :], ACT.Relu, bias=bn[:, 3:4])\
                    .then_inc(x1_ready, 1)

            def keep(it):
                n = it.image["C1"]
                if "C3" in it.image:
                    act.wait_ge(d_read, it.d("proj", 1))
                act.wait_ge(x1_ready, n.at(TILES, TILES))
                act.activation(kept[:, n.parity, :], x1[:, n.parity, :], ACT.Copy).then_inc(kept_ready, 1)

            def v_l2(it, b):
                n = it.image["C1"]
                slot = take(it, "v2", b)
                wait(act, pv2_done, n.at(16, -16))
                act.activation(va[:, n.parity, 4 * b:4 * b + 4, :].rearrange("p t c -> p (t c)"), slot[:], ACT.Copy)\
                    .then_inc(e_read, 1)

            def mrow2(it, h, b):
                n = it.image["C1"]
                slot = take(it, "mrow2", h, b)
                act.activation(mov2[MROW:STACK, n.parity, h, b * HALF:(b + 1) * HALF], slot[MROW:STACK, :], ACT.Copy)\
                    .then_inc(e_read, 1)

            def exp2(it, w, h):
                n = it.image["C2"]
                slot = take(it, "exp2", w, h)
                wait(act, pv2_done, n.at(16, w - 1))
                act.activation(p2[:, w % 2, h, :], slot[:], ACT.Exp).then_inc(e_read, 1)

            def attended(it):
                n = it.image["C3"]
                act.wait_ge(pv2_done, n.at(16, 16))
                if it.has_before("C3"):
                    act.wait_ge(d_full, it.before().d("proj", 1))
                act.activation(att[:], o[:], ACT.Copy).then_inc(o2_read, 1)

            def x2t_step(it, b):
                slot = take(it, "x2t", b)
                if it.has_before("C3"):
                    act.wait_ge(d_full, it.before().d("sigma"))
                act.activation(x2t[:, 4 * b:4 * b + 4, :].rearrange("p t c -> p (t c)"), slot[:], ACT.Copy)\
                    .then_inc(e_read, 1)

            act.wait_ge(s_w, 16 * len(loads))
            act.wait_ge(s_ones, N_ONES)
            act.wait_ge(s_prep, N_PREP)
            run(act, {"v0": v_l0, "mrow0": mrow0, "exp0": exp0, "shift0": shift0, "xt": xt_step, "conv": conv,
                      "turn": turn, "relu": relu, "keep": keep, "v2": v_l2, "mrow2": mrow2, "exp2": exp2,
                      "attended": attended, "x2t": x2t_step})


def constants():
    f = np.float32
    px = np.arange(PX).reshape(TILES, P)
    grid = np.empty((P, TILES, OFFS), f)
    grid[:, :, 0:TAPS] = (px // W + 1).T[:, :, None]
    grid[:, :, TAPS:] = (px % W + 1).T[:, :, None]
    gather_sel = np.zeros((P, P), f)
    for g in range(4):
        gather_sel[32 * g + np.arange(OFFS), np.arange(OFFS)] = 1
    sum_sel = np.zeros((P, P), f)
    for h in range(HEADS):
        sum_sel[32 * h + D, 32 * h:32 * h + 32] = 1
    channel = np.arange(C)
    return {
        "identf": np.eye(P, dtype=f), "grid": grid,
        "gather_sel": gather_sel, "sum_sel": sum_sel,
        "qscale": np.where(np.arange(P) < C, f(D ** -0.5), f(1))[:, None].astype(f),
        "group_mean": ((channel[:, None] // 8 == np.arange(P)[None, :] // 8) / 32).astype(f),
        "mask": (channel[:, None] // GROUP == channel[None, :] // GROUP).astype(f),
    }


def layout(i):
    f = np.float32
    out = {"x": i["x"].reshape(IMAGES, C, PX)}
    out["wqk0"] = np.concatenate([np.concatenate([i["L0_conv_wq"].T, i["L0_conv_wk"].T], 1),
                                  np.concatenate([i["L0_conv_bq"], i["L0_conv_bk"]])[None]], 0)
    wv0 = np.zeros((C + 1, P), f)
    wv0[0:C, 0:C] = i["L0_conv_wv"].T
    wv0[C, 0:C] = i["L0_conv_bv"]
    wv0[C, C:] = 1
    out["wv0"] = wv0
    w6 = np.zeros((C + 1, TAPS, 6), f)
    w6[0:C] = np.concatenate([i["L1_conv_w_tm"], i["L1_conv_w_tr"]], 0).reshape(6, C, TAPS).transpose(1, 2, 0)
    w6[C, TAPS // 2] = np.concatenate([i["L1_conv_b_tm"], i["L1_conv_b_tr"]])
    out["w6"] = w6
    wd = np.zeros((2, C, 5, C), f)
    taps = i["L1_conv_w_deform"].reshape(C, C, TAPS).transpose(2, 1, 0)
    for k in range(TAPS):
        wd[k % 2, :, k // 2, :] = taps[k]
    out["wd"] = wd.reshape(P, 5, C)
    wqkv, bqkv = i["L2_conv_w_qkv"], i["L2_conv_b_qkv"]
    out["wqk2"] = np.concatenate([wqkv[0:2 * C].T, bqkv[None, 0:2 * C]], 0)
    wv2 = np.zeros((C + 1, HEADS, 2 * D), f)
    wv2[0:C, :, 0:D] = wqkv[2 * C:].T.reshape(C, HEADS, D)
    wv2[C, :, 0:D] = bqkv[2 * C:].reshape(HEADS, D)
    wv2[C, :, D:] = 1
    out["wv2"] = wv2.reshape(C + 1, P)
    wproj = np.zeros((HEADS, 2 * D, C), f)
    wproj[:, 0:D] = i["L2_conv_w_proj"].T.reshape(HEADS, D, C)
    out["wproj"] = wproj.reshape(P, C)
    out["vecs"] = np.stack([i["L1_conv_bn_gamma"], i["L1_conv_bn_beta"], i["L1_conv_bn_mean"], i["L1_conv_bn_var"],
                            i["L2_conv_gn_w"], i["L2_conv_gn_b"], i["L2_conv_b_proj"],
                            np.broadcast_to(i["L0_conv_gamma"], (C,)), i["L3_conv_bias"].reshape(C)], 1)
    out["w3row"] = np.broadcast_to(i["L3_conv_weight"].reshape(1, C), (C, C))
    return out


def kernel(**inputs):
    import concourse.bacc as bacc
    from concourse.bass_utils import run_bass_kernel_spmd

    arrays = layout({k: np.asarray(v) for k, v in inputs.items()}) | constants()
    arrays = {f"in_{k}": np.ascontiguousarray(v) for k, v in arrays.items()}
    nc = bacc.Bacc("TRN2", target_bir_lowering=False, num_devices=1)
    args = {k[3:]: nc.dram_tensor(k, v.shape, mybir.dt.from_np(v.dtype), kind="ExternalInput").ap()
            for k, v in arrays.items()}
    out = nc.dram_tensor("out", (IMAGES, C, H, W), F32, kind="ExternalOutput").ap()
    build(nc, args, out)
    r = run_bass_kernel_spmd(nc, [arrays], core_ids=[0])
    return r.results[0]["out"]
```

```python
from contextlib import ExitStack

import concourse.bass as bass
import numpy as np
from concourse import mybir

F32 = mybir.dt.float32
BF16 = mybir.dt.bfloat16
I32 = mybir.dt.int32
ALU = mybir.AluOpType
ACT = mybir.ActivationFunctionType
AX = mybir.AxisListType

IMAGES, C, H, W = 32, 64, 32, 32
PX = H * W
P = 128
TILES = PX // P
HALF = PX // 2
D = 16
HEADS = C // D
TAPS = 9
CORNERS = 4
PARTS = 6
ROWS = PARTS * D
MROW = ROWS
STACK = ROWS + 2
ONE = C
STAT_PARTS = (0, 0, 1, 1, 0, 2)
MOV_PARTS = (0, 1, 0, 1, 2, 0)
MAP_H, MAP_W = H + 1, W + 2
TABLE = MAP_H * MAP_W
EPS = 1e-5
GROUP = 16
STEPS = 5
REG = ((-1, -1, -1, 0, 0, 0, 1, 1, 1), (-1, 0, 1, -1, 0, 1, -1, 0, 1))
CONV_GROUPS = ((0, 1, 2), (3, 4), (5, 6), (7, 8))
OFFS = 2 * TAPS

SHIFT = {"A": 0, "B": 1, "C1": 2, "C2": 3, "C3": 4}
LAST_SHIFT = 4
D_STEPS = {"qk0": 1, "max0": 1, "out0": 1, "in0": 1, "offsets": 1, "deform": 1, "stat": 1, "qk2": 1, "max2": 1, "sums": 1, "proj": 1,
           "sigma": 1}
E_STEPS = {"v0": 1, "mrow0": 1, "exp0": 1, "back0": 1, "conv": 1, "turn": 2, "v2": 1, "mrow2": 1, "exp2": 1, "back2": 1, "x2t": 1}
D_USES = {"A": 12, "B": 8, "C1": 34, "C2": 0, "C3": 4}
E_USES = {"A": 23, "B": 16, "C1": 10, "C2": 64, "C3": 3}
SPLITS, NEGS, NORMS, SCALES, OFFSET_OPS, STAT_OPS = 2, 2, 2, 3, 14, 23


class Image:

    def __init__(self, j, c):
        self.j, self.c = j, c
        self.parity = c % 2
        self.n = c if isinstance(j, int) else j * 2 + c

    def at(self, per_image, k):
        const = self.c * per_image + k
        return const if isinstance(self.j, int) else self.j * (2 * per_image) + const

    def at_own_parity(self, per_image, k):
        const = self.c // 2 * per_image + k
        return const if isinstance(self.j, int) else self.j * per_image + const


class Iteration:

    def __init__(self, j, c):
        self.j, self.c = j, c
        loop = not isinstance(j, int)
        self.image = {s: Image(j, c - sh) for s, sh in SHIFT.items() if loop or 0 <= c - sh < IMAGES}
        self.steps = order(self.image)
        self.numbers = {}
        for ring, steps in (("d", D_STEPS), ("e", E_STEPS)):
            k = 0
            for _, name, *args in self.steps:
                for use in range(steps.get(name, 0)):
                    self.numbers[(ring, name, *args, use)] = k
                    k += 1

    def _count(self, ring, uses, name, args, use):
        const, slope = self.numbers[(ring, name, *args, use)] + 1, 0
        for s, sh in SHIFT.items():
            if isinstance(self.j, int):
                const += uses[s] * min(max(self.c - sh, 0), IMAGES)
            else:
                const += uses[s] * (self.c - sh)
                slope += 2 * uses[s]
        return const if isinstance(self.j, int) else self.j * slope + const

    def d(self, name, *args, use=0):
        return self._count("d", D_USES, name, args, use)

    def e(self, name, *args, use=0):
        return self._count("e", E_USES, name, args, use)

    def slot(self, ring, name, *args, use=0):
        uses = D_USES if ring == "d" else E_USES
        const = sum(uses[s] * (self.c - sh if not isinstance(self.j, int) else min(max(self.c - sh, 0), IMAGES))
                    for s, sh in SHIFT.items())
        return (const + self.numbers[(ring, name, *args, use)]) % 2

    def before(self):
        return Iteration(self.j, self.c - 1)

    def has_before(self, stage):
        return not isinstance(self.j, int) or 0 <= self.c - 1 - SHIFT[stage] < IMAGES


def wait(eng, sem, value):
    if not (isinstance(value, int) and value <= 0):
        eng.wait_ge(sem, value)


class Chain:

    def __init__(self, eng, sem, image, per_image, first=0):
        self.eng, self.sem, self.image, self.per_image, self.k = eng, sem, image, per_image, first

    def __call__(self, instruction):
        self.k += 1
        instruction.then_inc(self.sem, 1)
        self.eng.wait_ge(self.sem, self.image.at(self.per_image, self.k))


def order(image):
    s = []
    if "A" in image:
        s += [(0.0, "load"), (0.6, "qk0"), (0.61, "split0"), (0.62, "spread0"), (0.65, "v0", 0), (0.66, "v0", 1)]
        s += [(1.3 + 0.08 * t, "max0", t) for t in range(TILES)]
        s += [(1.95, "neg0"), (2.02, "mrow0", 0), (2.04, "mrow0", 1)]
        s += [(2.1 + 0.08 * u, "exp0", u // 2, u % 2) for u in range(16)]
        s += [(3.45, "pv0_end"), (3.46, "attended0"), (3.5, "out0"), (3.51, "in0"), (3.74, "map"), (3.75, "back0"),
              (3.9, "conv", 0), (4.0, "conv", 1), (4.15, "offsets")]
    if "B" in image:
        s += [(t - 0.3, "gather", t) for t in range(TILES)]
        s += [(t + 0.1, "scale", t) for t in range(TILES)]
        s += [(t + 0.5, "turn", t) for t in range(TILES)]
        s += [(t + 0.85, "deform", t) for t in range(TILES)]
        s += [(t + 0.95, "relu", t) for t in range(TILES)]
    if "C1" in image:
        s += [(0.2, "stat"), (0.44, "qk2"), (0.45, "split2"), (0.46, "spread2"), (0.47, "v2", 0), (0.48, "v2", 1),
              (0.9, "keep")]
        s += [(2.0 + 0.17 * u, "max2", u // TILES, u % TILES) for u in range(32)]
        s += [(2.0 + 0.17 * (8 * h + 7) + 0.01, "neg2", h) for h in range(HEADS)]
        s += [(2.0 + 0.17 * (8 * h + 7) + 0.3 + 0.1 * b, "mrow2", h, b) for h in range(HEADS) for b in range(2)]
    if "C2" in image:
        s += [(4.3 + 0.054 * u, "exp2", u // 4, u % 4) for u in range(64)]
        s += [(7.95, "pv2_end")]
    if "C3" in image:
        s += [(0.02, "attended"), (0.12, "sums"), (0.3, "back2"), (0.4, "proj", 0), (0.41, "proj", 1), (0.42, "store"),
              (0.85, "x2t", 0), (0.86, "x2t", 1), (1.15, "sigma")]
    return sorted(s, key=lambda step: step[0])


def build(nc, a, out):
    with ExitStack() as ctx:
        def sb(name, shape, dt=F32):
            return ctx.enter_context(nc.sbuf_tensor(name, shape, dt))

        def sem(name):
            return ctx.enter_context(nc.semaphore(name))

        parts0_d = nc.dram_tensor("parts0_d", (2, 3, 2 * D, PX), BF16, kind="Internal").ap()
        parts2_d = nc.dram_tensor("parts2_d", (2, 3, 2 * C, PX), BF16, kind="Internal").ap()
        table_d = [nc.dram_tensor(f"table{p}_d", (TABLE, 2 * C), F32, kind="Internal").ap() for p in range(2)]
        x2_d = nc.dram_tensor("x2_d", (IMAGES, C, PX), F32, kind="Internal").ap()

        identf = sb("identf", [P, P])
        identb = sb("identb", [P, P], BF16)
        wqk0 = sb("wqk0", [ONE + 1, 2 * D])
        wv0 = sb("wv0", [ONE + 1, P])
        w6 = sb("w6", [ONE + 1, TAPS, 6])
        woff = sb("woff", [ONE + 1, TAPS, 32])
        grid = sb("grid", [P, TILES, OFFS])
        gather_sel = sb("gather_sel", [P, P])
        wd = sb("wd", [P, 5, C])
        wqk2 = sb("wqk2", [ONE + 1, P])
        wv2 = sb("wv2", [ONE + 1, P])
        qscale = sb("qscale", [P, 1])
        group_mean = sb("group_mean", [C, P])
        wproj = sb("wproj", [C, P])
        gamma = sb("gamma", [P, 1])
        vecs = sb("vecs", [C, 8])
        bn_g, bn_b, bn_m, bn_v, gn_w, gn_b, b_proj, bias3 = (vecs[:, k:k + 1] for k in range(8))
        w3row = sb("w3row", [C, C])
        mask = sb("mask", [C, C])
        bn = sb("bn", [C, 4])
        newton = sb("newton", [C, 4])
        zeros = sb("zeros", [MAP_W, P])
        nothing = sb("nothing", [1, 1])

        xin = sb("xin", [ONE + 1, 2, PX])
        parts0 = sb("parts0", [2 * D, 3, PX], BF16)
        rest = sb("rest", [P, PX])
        stat0 = sb("stat0", [STACK, PX], BF16)
        mov0 = sb("mov0", [STACK, PX], BF16)
        v0 = sb("v0", [P, TILES, P])
        mx0 = sb("mx0", [P, TILES])
        neg0 = sb("neg0", [P, TILES, 2], BF16)
        p0 = sb("p0", [P, 2, HALF])
        att0 = sb("att0", [ONE + 1, PX])
        rs0 = sb("rs0", [P, TILES])
        xc = sb("xc", [ONE + 1, 2, (H + 2) * W])
        xl = sb("xl", [ONE + 1, (H + 2) * W])
        xr = sb("xr", [ONE + 1, (H + 2) * W])
        xt = sb("xt", [P, TILES, C])
        cs = rest
        pos = sb("pos", [P, TILES, OFFS])
        flo = sb("flo", [P, TILES, OFFS])
        rnd = sb("rnd", [P, TILES, OFFS], I32)
        one_less = sb("one_less", [P, TILES, OFFS])
        idx = sb("idx", [P, 2, TILES, TAPS], I32)
        wt = sb("wt", [P, 2, TILES, TAPS, CORNERS])

        G = sb("G", [P, 2, TAPS * CORNERS * C])
        gs = sb("gs", [P, 2, CORNERS, TAPS * C])
        ts = sb("ts", [P, 2, 5 * P])
        y1 = sb("y1", [C, 2, P])
        x1 = sb("x1", [C, 2, PX])

        kept = sb("kept", [C, 2, PX])
        bnst = sb("bnst", [C, 2, 6])
        mv = sb("mv", [C, 4])
        stat_in = sb("stat_in", [C, P])
        gm = sb("gm", [C, 8])
        ha = sb("ha", [ONE + 1, PX])
        parts2 = sb("parts2", [P, 3, PX], BF16)
        stat2 = sb("stat2", [STACK, 2, HEADS, PX], BF16)
        mov2 = sb("mov2", [STACK, 2, HEADS, PX], BF16)
        va = sb("va", [P, 2, TILES, P])
        mx2 = sb("mx2", [P, HEADS, TILES])
        neg2 = sb("neg2", [P, HEADS, TILES, 2], BF16)
        p2 = sb("p2", [P, 2, HEADS, HALF])
        att = sb("att", [P, PX])
        rs2 = sb("rs2", [P, TILES, HEADS])
        r2t = sb("r2t", [P, TILES, C])
        x2 = sb("x2", [ONE + 1, PX])
        x2t = sb("x2t", [P, TILES, P])
        sig = sb("sig", [C, P])

        mean = sb("mean", [C, 1])
        mrow = sb("mrow", [1, C])
        cov = sb("cov", [C, C])
        tmp = sb("tmp", [C, C])
        pm = sb("pm", [C, C])
        pa = sb("pa", [C, C])
        w2 = sb("w2", [P, P])
        b2 = sb("b2", [P, 1])
        tr = sb("tr", [C, 4])

        dring = [ctx.enter_context(nc.psum_tensor(f"dring{i}", [P, PX], F32)) for i in range(2)]
        ering = [ctx.enter_context(nc.psum_tensor(f"ering{i}", [P, HALF], F32)) for i in range(2)]
        o = ctx.enter_context(nc.psum_tensor("o", [P, PX], F32))

        s_w = sem("s_w")
        s_ones = sem("s_ones")
        s_border = sem("s_border")
        s_prep = sem("s_prep")
        d_full, d_read = sem("d_full"), sem("d_read")
        e_full, e_read = sem("e_full"), sem("e_read")
        x_in = [sem("x_in0"), sem("x_in1")]
        high0, high2 = sem("high0"), sem("high2")
        split0, parts0_out, stacks0_in = sem("split0"), sem("parts0_out"), sem("stacks0_in")
        neg0_done, pv0_done, o0_read, norm0_done = sem("neg0_done"), sem("pv0_done"), sem("o0_read"), sem("norm0_done")
        map_out, offsets_done = sem("map_out"), sem("offsets_done")
        gathered = [sem("gathered0"), sem("gathered1")]
        scaled, x1_ready = sem("scaled"), sem("x1_ready")
        stat_done, kept_ready = sem("stat_done"), sem("kept_ready")
        split2, parts2_out, stacks2_in = sem("split2"), sem("parts2_out"), sem("stacks2_in")
        neg2_done, pv2_done, o2_read = sem("neg2_done"), sem("pv2_done"), sem("o2_read")
        normed2, x2_out = sem("normed2"), sem("x2_out")
        carried = sem("carried")
        f_dve, f_pe, f_hold = sem("f_dve"), sem("f_pe"), sem("f_hold")
        fin_in = [sem("fin_in0"), sem("fin_in1")]
        fin_out = [sem("fin_out0"), sem("fin_out1")]

        loads = (
            (identf, "identf"), (wqk0, "wqk0"), (wv0, "wv0"), (w6, "w6"), (grid, "grid"),
            (gather_sel, "gather_sel"), (wqk2, "wqk2"), (wv2, "wv2"), (qscale, "qscale"), (group_mean, "group_mean"),
            (gamma, "gamma"), (wproj, "wproj"), (vecs, "vecs"), (mask, "mask"), (wd, "wd"))
        D_ALL = IMAGES * sum(D_USES.values())

        def run(eng, steps):
            def iteration(it):
                for _, name, *args in it.steps:
                    if name in steps:
                        steps[name](it, *args)
            for c in range(LAST_SHIFT):
                iteration(Iteration(0, c))
            with eng.Fori(LAST_SHIFT // 2, IMAGES // 2) as j:
                for c in range(2):
                    iteration(Iteration(j, c))
            for c in range(IMAGES, IMAGES + LAST_SHIFT):
                iteration(Iteration(0, c))

        ones = (xin[ONE:ONE + 1, :, :], ha[ONE:ONE + 1, :], x2[ONE:ONE + 1, :], xc[ONE:ONE + 1, :, :],
                xl[ONE:ONE + 1, :], xr[ONE:ONE + 1, :], stat0[MROW:STACK, :], stat2[MROW:STACK, :, :, :])
        blanks = (xc[0:C, :, :], xl[0:C, :], xr[0:C, :], zeros[:], sig[:], x2t[:], stat_in[:], woff[:], w2[:], nothing[:])
        N_ONES = len(ones) + len(blanks)
        N_PREP = 1 + 18 + 24 + 15

        fin_src = [p2[:, b, 0:2, :].rearrange("p a n -> p (a n)") for b in range(2)]
        fin_dst = [G[:, b, 0:PX] for b in range(2)]
        x2_pairs = x2_d.rearrange("(m two) c n -> m (two c) n", two=2)
        out_pairs = out.rearrange("(m two) c h w -> m (two c) (h w)", two=2)

        block = ctx.enter_context(nc.Block())

        @block.sync
        def _(sp):
            for tile, name in loads:
                sp.dma_start(tile[:], a[name]).then_inc(s_w, 16)
            sp.dma_start(w3row[:], a["w3row"]).then_inc(x2_out, 16)
            sp.wait_ge(s_ones, N_ONES)
            borders = [t.rearrange("(y x) c -> y x c", x=MAP_W) for t in table_d]
            for m in range(2):
                for y in (0, MAP_H - 1):
                    sp.dma_start(borders[m][y, :, :], zeros[0:MAP_W, :]).then_inc(s_border, 16)
            sp.wait_ge(s_border, 16 * 4)
            for m in range(2):
                for x in (0, MAP_W - 1):
                    sp.dma_start(borders[m][:, x, :], zeros[0:MAP_H, :]).then_inc(s_border, 16)
            sp.wait_ge(s_border, 16 * 8)

            def load(it):
                n = it.image["A"]
                if it.has_before("A"):
                    sp.wait_ge(d_read, it.before().d("in0"))
                sp.dma_start(xin[0:C, n.parity, :], a["x"][bass.ds(n.n, 1), :, :].rearrange("o c n -> (o c) n"))\
                    .then_inc(x_in[n.parity], 16)

            def spread0(it):
                n = it.image["A"]
                sp.wait_ge(split0, n.at(SPLITS, SPLITS))
                sp.dma_start(parts0_d[n.parity].rearrange("t r n -> r t n"), parts0[:]).then_inc(parts0_out, 16)
                sp.wait_ge(parts0_out, n.at(16, 16))
                for b in range(PARTS):
                    sp.dma_start(stat0[D * b:D * b + D, :], parts0_d[n.parity, STAT_PARTS[b], 0:D, :])\
                        .then_inc(stacks0_in, 16)
                    sp.dma_start(mov0[D * b:D * b + D, :], parts0_d[n.parity, MOV_PARTS[b], D:2 * D, :])\
                        .then_inc(stacks0_in, 16)

            def table(it):
                n = it.image["A"]
                sp.wait_ge(d_read, it.d("in0"))
                for b in range(2):
                    wait(sp, gathered[b], n.at(TILES // 2 * TAPS * 16, -TILES // 2 * TAPS * 16))
                rows = table_d[n.parity].rearrange("(y x) (s c) -> y x s c", x=MAP_W, s=2)
                for r in range(P // W):
                    for s in range(2):
                        y = r + 1 - s
                        to = rows[y:y + 4 * (TILES - 1) + 1:4, 1:W + 1, s, :]
                        sp.dma_start(to.rearrange("t x c -> x t c"), xt[W * r:W * r + W, :, :]).then_inc(map_out, 16)

            def spread2(it):
                n = it.image["C1"]
                sp.wait_ge(split2, n.at(SPLITS, SPLITS))
                sp.dma_start(parts2_d[n.parity].rearrange("t r n -> r t n"), parts2[:]).then_inc(parts2_out, 16)
                sp.wait_ge(parts2_out, n.at(16, 16))
                for b in range(PARTS):
                    for stack, part, at in ((mov2, MOV_PARTS[b], 0), (stat2, STAT_PARTS[b], C)):
                        src = parts2_d[n.parity, part, at:at + C, :].rearrange("(h d) n -> d h n", h=HEADS)
                        sp.dma_start(stack[D * b:D * b + D, n.parity, :, :], src).then_inc(stacks2_in, 16)

            def store(it):
                n = it.image["C3"]
                sp.wait_ge(d_read, it.d("proj", 1))
                sp.dma_start(x2_d[bass.ds(n.n, 1), :, :].rearrange("o c n -> (o c) n"), x2[0:C, :]).then_inc(x2_out, 16)

            run(sp, {"load": load, "spread0": spread0, "map": table, "spread2": spread2, "store": store})

            sp.wait_ge(x2_out, 16 + 16 * IMAGES)
            with sp.Fori(0, IMAGES // 4) as j:
                for b in range(2):
                    sp.wait_ge(d_full, j * 2 + (D_ALL + b - 1))
                    sp.dma_start(fin_src[b], x2_pairs[bass.ds(j * 2 + b, 1), :, :].rearrange("o c n -> (o c) n"))\
                        .then_inc(fin_in[b], 16)
                for b in range(2):
                    sp.wait_ge(d_read, j * 2 + (D_ALL + b + 1))
                    sp.dma_start(out_pairs[bass.ds(j * 2 + b, 1), :, :].rearrange("o c n -> (o c) n"), fin_dst[b])\
                        .then_inc(fin_out[b], 16)
            for b in range(2):
                sp.wait_ge(fin_out[b], 16 * IMAGES // 4)

        @block.gpsimd
        def _(pool):
            pool.wait_ge(s_ones, N_ONES)

            def gather(it, t):
                n = it.image["B"]
                if t == 0:
                    pool.wait_ge(offsets_done, n.at(OFFSET_OPS, OFFSET_OPS))
                    pool.wait_ge(map_out, n.at(8 * 16, 8 * 16))
                wait(pool, carried, n.at(TILES, t))
                wait(pool, scaled, n.at(SCALES * TILES, SCALES * (t - 2) + 1))
                pool.tensor_tensor(nothing[:], nothing[:], nothing[:], ALU.add).then_inc(carried, 1)
                for k in range(TAPS):
                    pool.indirect_dma_start(
                        G[:, t % 2, CORNERS * C * k:CORNERS * C * (k + 1)], None, table_d[n.parity],
                        bass.IndirectOffsetOnAxis(idx[:, n.parity, t, k:k + 1], 0)).then_inc(gathered[t % 2], 16)

            run(pool, {"gather": gather})

        @block.vector
        def _(dve):
            def newton_rsqrt(step, v, y, t):
                step(dve.tensor_scalar(y.bitcast(I32), v.bitcast(I32), 1, None, ALU.logical_shift_right))
                step(dve.tensor_scalar(y.bitcast(I32), y.bitcast(I32), -1.0, float(0x5F3759DF), ALU.mult, ALU.add))
                for _ in range(3):
                    step(dve.scalar_tensor_tensor(t, y, v, y, ALU.mult, ALU.mult))
                    step(dve.tensor_scalar(t, t, -0.5, 1.5, ALU.mult, ALU.add))
                    step(dve.tensor_tensor(y, y, t, ALU.mult))

            def take(it, name, *args):
                dve.wait_ge(d_full, it.d(name, *args))
                return dring[it.slot("d", name, *args)]

            def split(it, name, n, parts, high, sem, rows, scale):
                slot = take(it, name)[0:rows, :]
                dve.wait_ge(high, n.at(1, 1))
                step = Chain(dve, sem, n, SPLITS)
                rs = rest[0:rows, :]
                dve.scalar_tensor_tensor(rs, slot, scale, parts[:, 0, :], ALU.mult, ALU.subtract).then_inc(d_read, 1)
                dve.wait_ge(d_read, it.d(name))
                step(dve.tensor_copy(parts[:, 1, :], rs))
                step(dve.tensor_tensor(parts[:, 2, :], rs, parts[:, 1, :], ALU.subtract))

            def split_l0(it):
                n = it.image["A"]
                wait(dve, parts0_out, n.at(16, 0))
                split(it, "qk0", n, parts0, high0, split0, 2 * D, 1.0)

            def max0(it, t):
                slot = take(it, "max0", t)
                dve.tensor_reduce(mx0[:, t:t + 1], slot[:], AX.X, ALU.max).then_inc(d_read, 1)

            def neg(it, last, sem, n, per_image, first, mx, to):
                dve.wait_ge(d_read, last)
                step = Chain(dve, sem, n, per_image, first)
                step(dve.tensor_scalar(to[:, :, 0], mx, -1.0, None, ALU.mult))
                step(dve.scalar_tensor_tensor(to[:, :, 1], mx, -1.0, to[:, :, 0], ALU.mult, ALU.subtract))

            def neg_l0(it):
                n = it.image["A"]
                if it.has_before("A"):
                    dve.wait_ge(e_full, it.before().e("mrow0", 1))
                neg(it, it.d("max0", TILES - 1), neg0_done, n, NEGS, 0, mx0[:], neg0[:])

            def out0(it):
                n = it.image["A"]
                slot = take(it, "out0").rearrange("p (t c) -> p t c", c=P)
                step = Chain(dve, norm0_done, n, NORMS)
                step(dve.reciprocal(rs0[:], slot[:, :, C]))
                step(dve.tensor_scalar(rs0[:], rs0[:], gamma[:], None, ALU.mult))
                wait(dve, map_out, n.at(8 * 16, 0))
                if it.has_before("A"):
                    dve.wait_ge(e_full, it.before().e("back0"))
                by = rs0[:].unsqueeze(2).broadcast_to([P, TILES, C])
                dve.tensor_tensor(xt[:], slot[:, :, 0:C], by, ALU.mult).then_inc(d_read, 1)

            def in0(it):
                n = it.image["A"]
                slot = take(it, "in0").rearrange("p (t c) -> p t c", c=P)
                dve.wait_ge(d_read, it.d("out0"))
                dve.tensor_tensor(xt[:], xt[:], slot[:, :, 0:C], ALU.add).then_inc(d_read, 1)

            def offsets(it):
                n = it.image["A"]
                slot = take(it, "offsets").rearrange("p (t c) -> p t c", c=P)
                step = Chain(dve, offsets_done, n, OFFSET_OPS)
                dve.tensor_tensor(pos[:], slot[:, :, 0:OFFS], grid[:], ALU.add).then_inc(d_read, 1)
                dve.wait_ge(d_read, it.d("offsets"))
                step(dve.tensor_scalar(pos[:], pos[:], float(H + 1), 0.0, ALU.min, ALU.max))
                step(dve.tensor_copy(rnd[:], pos[:]))
                step(dve.tensor_copy(flo[:], rnd[:]))
                step(dve.tensor_tensor(one_less[:], flo[:], pos[:], ALU.is_gt))
                step(dve.tensor_tensor(flo[:], flo[:], one_less[:], ALU.subtract))
                step(dve.tensor_scalar(flo[:], flo[:], float(H), None, ALU.min))
                step(dve.tensor_tensor(pos[:], pos[:], flo[:], ALU.subtract))
                step(dve.tensor_scalar(one_less[:], pos[:], -1.0, 1.0, ALU.mult, ALU.add))
                for dx in range(2):
                    for dy in range(2):
                        wy = (one_less, pos)[dy][:, :, 0:TAPS]
                        wx = (one_less, pos)[dx][:, :, TAPS:OFFS]
                        step(dve.tensor_tensor(wt[:, n.parity, :, :, 2 * dx + dy], wx, wy, ALU.mult))
                step(dve.tensor_scalar(one_less[:, :, 0:TAPS], flo[:, :, 0:TAPS], float(MAP_W), None,
                                       ALU.mult))
                step(dve.tensor_tensor(idx[:, n.parity], one_less[:, :, 0:TAPS], flo[:, :, TAPS:OFFS], ALU.add))
                assert step.k == OFFSET_OPS

            def scale(it, t):
                n = it.image["B"]
                if t == 0:
                    dve.wait_ge(offsets_done, n.at(OFFSET_OPS, OFFSET_OPS))
                per = TAPS * 16
                dve.wait_ge(gathered[t % 2], n.at(TILES // 2 * per, (t // 2 + 1) * per))
                if t >= 2:
                    dve.wait_ge(e_full, it.e("turn", t - 2, use=1))
                elif it.has_before("B"):
                    dve.wait_ge(e_full, it.before().e("turn", TILES + t - 2, use=1))
                step = Chain(dve, scaled, n, SCALES * TILES, SCALES * t)
                g = G[:, t % 2, :].rearrange("p (k c d) -> p k c d", k=TAPS, c=CORNERS)
                to = gs[:, t % 2, :, :].rearrange("p c (k d) -> p k c d", k=TAPS)
                by = wt[:, n.parity, t, :, :].unsqueeze(3).broadcast_to([P, TAPS, CORNERS, C])
                step(dve.tensor_tensor(to, g, by, ALU.mult))
                step(dve.tensor_tensor(gs[:, t % 2, 0:2, :], gs[:, t % 2, 0:2, :], gs[:, t % 2, 2:4, :], ALU.add))
                step(dve.tensor_tensor(gs[:, t % 2, 0, :], gs[:, t % 2, 0, :], gs[:, t % 2, 1, :], ALU.add))

            def deform(it, t):
                n = it.image["B"]
                slot = take(it, "deform", t)
                wait(dve, x1_ready, n.at(TILES, t - 1))
                dve.scalar_tensor_tensor(y1[:, t % 2, :], slot[0:C, 0:P], bn[:, 1:2],
                                         xc[0:C, n.parity, W + t * P:W + (t + 1) * P], ALU.mult, ALU.add)\
                    .then_inc(d_read, 1)

            def stat(it):
                n = it.image["C1"]
                dve.wait_ge(x1_ready, n.at(TILES, TILES))
                step = Chain(dve, stat_done, n, STAT_OPS)
                for b in range(2):
                    step(dve.bn_stats(bnst[:, b, :], x1[:, n.parity, b * HALF:(b + 1) * HALF]))
                sets = bnst[:].rearrange("p a (b s) -> p (a b) s", s=3)
                step(dve.tensor_tensor(mv[:], sets[:, :, 1], sets[:, :, 1], ALU.mult))
                step(dve.scalar_tensor_tensor(mv[:], sets[:, :, 2], 4.0 / PX, mv[:], ALU.mult, ALU.add))
                step(dve.tensor_reduce(stat_in[:, 1:2], mv[:], AX.X, ALU.add))
                step(dve.tensor_reduce(stat_in[:, 0:1], sets[:, :, 1], AX.X, ALU.add))
                slot = take(it, "stat")
                dve.tensor_copy(gm[:, 0:2], slot[0:C, 0:2]).then_inc(d_read, 1)
                dve.wait_ge(d_read, it.d("stat"))
                step(dve.tensor_tensor(gm[:, 2:3], gm[:, 0:1], gm[:, 0:1], ALU.mult))
                step(dve.scalar_tensor_tensor(gm[:, 3:4], gm[:, 1:2], EPS, gm[:, 2:3], ALU.add, ALU.subtract))
                newton_rsqrt(step, gm[:, 3:4], gm[:, 4:5], gm[:, 5:6])
                step(dve.tensor_tensor(gm[:, 5:6], gm[:, 4:5], gn_w, ALU.mult))
                step(dve.tensor_tensor(gm[:, 6:7], gm[:, 0:1], gm[:, 5:6], ALU.mult))
                step(dve.tensor_tensor(gm[:, 7:8], gn_b, gm[:, 6:7], ALU.subtract))
                if it.has_before("C1"):
                    dve.wait_ge(e_full, it.before().e("v2", 1))
                step(dve.tensor_scalar(ha[0:C, :], x1[:, n.parity, :], gm[:, 5:6], gm[:, 7:8], ALU.mult, ALU.add))
                assert step.k == STAT_OPS

            def split_l2(it):
                n = it.image["C1"]
                wait(dve, parts2_out, n.at(16, 0))
                split(it, "qk2", n, parts2, high2, split2, P, qscale[:])

            def max2(it, h, t):
                slot = take(it, "max2", h, t)
                dve.tensor_reduce(mx2[:, h, t:t + 1], slot[:], AX.X, ALU.max).then_inc(d_read, 1)

            def neg_l2(it, h):
                n = it.image["C1"]
                if it.has_before("C1"):
                    dve.wait_ge(e_full, it.before().e("mrow2", h, 1))
                neg(it, it.d("max2", h, TILES - 1), neg2_done, n, NEGS * HEADS, NEGS * h, mx2[:, h, :], neg2[:, h])

            def sums(it):
                n = it.image["C3"]
                slot = take(it, "sums").rearrange("p (t h e) -> p t h e", h=HEADS, e=2 * D)
                step = Chain(dve, normed2, n, 1)
                step(dve.reciprocal(rs2[:], slot[:, :, :, D]))
                if it.has_before("C3"):
                    dve.wait_ge(e_full, it.before().e("back2"))
                by = rs2[:].unsqueeze(3).broadcast_to([P, TILES, HEADS, D])
                dve.tensor_tensor(r2t[:].rearrange("p t (h d) -> p t h d", d=D), slot[:, :, :, 0:D], by, ALU.mult)\
                    .then_inc(d_read, 1)

            def proj(it, b):
                n = it.image["C3"]
                slot = take(it, "proj", b)
                if b == 0:
                    dve.wait_ge(kept_ready, n.at(1, 1))
                    dve.wait_ge(x2_out, n.at(16, 16))
                    if it.has_before("C3"):
                        dve.wait_ge(e_full, it.before().e("x2t", 1))
                cols = slice(b * HALF, (b + 1) * HALF)
                dve.scalar_tensor_tensor(x2[0:C, cols], slot[0:C, 0:HALF], b_proj, kept[:, n.parity, cols],
                                         ALU.add, ALU.add).then_inc(d_read, 1)

            def sigma(it):
                slot = take(it, "sigma")
                dve.tensor_tensor(sig[:], sig[:], slot[0:C, 0:P], ALU.add).then_inc(d_read, 1)

            for tile in ones:
                dve.memset(tile, 1.0).then_inc(s_ones, 1)
            for tile in blanks:
                dve.memset(tile, 0.0).then_inc(s_ones, 1)
            dve.wait_ge(s_w, 16 * len(loads))
            dve.wait_ge(s_ones, N_ONES)
            step = Chain(dve, s_prep, Image(0, 0), 0)
            step(dve.tensor_copy(identb[:], identf[:]))
            for axis in range(2):
                for k in range(TAPS):
                    to = woff[:, :, TAPS * axis + k]
                    step(dve.tensor_copy(to, w6[:, :, 4 + axis]))
                    for j in range(2):
                        if REG[j][k]:
                            step(dve.tensor_tensor(to, to, w6[:, :, 2 * axis + j],
                                                   ALU.add if REG[j][k] > 0 else ALU.subtract))
            step(dve.tensor_scalar(bn[:, 0:1], bn_v, EPS, None, ALU.add))
            newton_rsqrt(step, bn[:, 0:1], newton[:, 0:1], newton[:, 1:2])
            step(dve.tensor_tensor(bn[:, 1:2], newton[:, 0:1], bn_g, ALU.mult))
            step(dve.tensor_tensor(bn[:, 2:3], bn_m, bn[:, 1:2], ALU.mult))
            step(dve.tensor_tensor(bn[:, 3:4], bn_b, bn[:, 2:3], ALU.subtract))
            assert step.k == N_PREP, step.k
            run(dve, {"split0": split_l0, "max0": max0, "neg0": neg_l0, "out0": out0, "in0": in0,
                      "offsets": offsets, "scale": scale, "deform": deform, "stat": stat, "split2": split_l2, "max2": max2,
                      "neg2": neg_l2, "sums": sums, "proj": proj, "sigma": sigma})

            dve.wait_ge(d_read, D_ALL)
            step = Chain(dve, f_dve, Image(0, 0), 0)
            count = [0]
            small = dring[0]

            def product():
                count[0] += 1
                dve.wait_ge(f_pe, count[0])

            def hold(instruction):
                held[0] += 1
                instruction.then_inc(f_hold, 1)
                dve.wait_ge(f_hold, held[0])

            held = [0]
            hold(dve.tensor_scalar(mean[:], sig[:, C:C + 1], 1.0 / (IMAGES * PX), None, ALU.mult))
            step(dve.tensor_scalar(cov[:], sig[:, 0:C], 1.0 / (IMAGES * PX), None, ALU.mult))
            product()
            step(dve.tensor_copy(mrow[:], small[0:1, 0:C]))
            product()
            hold(dve.tensor_tensor(cov[:], cov[:], small[0:C, 0:C], ALU.subtract))
            hold(dve.scalar_tensor_tensor(cov[:], identf[0:C, 0:C], EPS, cov[:], ALU.mult, ALU.add))
            hold(dve.tensor_tensor(cov[:], cov[:], mask[:], ALU.mult))
            hold(dve.tensor_tensor(tmp[:], cov[:], identf[0:C, 0:C], ALU.mult))
            step(dve.tensor_reduce(tr[:, 0:1], tmp[:], AX.X, ALU.add))
            product()
            hold(dve.tensor_copy(tr[:, 1:2], small[0:C, 0:1]))
            hold(dve.reciprocal(tr[:, 2:3], tr[:, 1:2]))
            hold(dve.tensor_scalar(cov[:], cov[:], tr[:, 2:3], None, ALU.mult))
            newton_rsqrt(hold, tr[:, 1:2], tr[:, 2:3], tr[:, 3:4])
            step(dve.tensor_copy(pm[:], identf[0:C, 0:C]))
            for k in range(STEPS):
                product()
                step(dve.tensor_copy(pa[:], small[0:C, 0:C]))
                product()
                step(dve.tensor_copy(tmp[:], small[0:C, 0:C]))
                product()
                hold(dve.tensor_scalar(pm[:], pm[:], 1.5, None, ALU.mult))
                (step if k < STEPS - 1 else hold)(dve.scalar_tensor_tensor(pm[:], small[0:C, 0:C], -0.5, pm[:], ALU.mult, ALU.add))
            dve.wait_ge(x2_out, 16)
            hold(dve.scalar_tensor_tensor(w2[0:C, 0:C], pm[:], tr[:, 2:3], w3row[:], ALU.mult, ALU.mult))
            step(dve.tensor_copy(w2[C:P, C:P], w2[0:C, 0:C]))
            product()
            hold(dve.tensor_tensor(b2[0:C, :], bias3, small[0:C, 0:1], ALU.subtract))
            step(dve.tensor_copy(b2[C:P, :], b2[0:C, :]))

            def last(j, b):
                dve.wait_ge(d_full, j * 2 + (D_ALL + b + 1))
                dve.tensor_scalar(fin_dst[b], dring[b][:], b2[:], None, ALU.add).then_inc(d_read, 1)

            for b in range(2):
                last(0, b)
            with dve.Fori(1, IMAGES // 4) as j:
                for b in range(2):
                    dve.wait_ge(fin_out[b], j * 16)
                    last(j, b)

        @block.tensor
        def _(pe):
            def d_slot(it, name, *args):
                wait(pe, d_read, it.d(name, *args) + (-2))
                return dring[it.slot("d", name, *args)]

            def e_slot(it, name, *args, use=0):
                wait(pe, e_read, it.e(name, *args, use=use) + (-2))
                return ering[it.slot("e", name, *args, use=use)]

            ident1 = identf[0:ONE + 1, 0:ONE + 1]

            def mm(to, lhsT, rhs, start=True, stop=True):
                return pe.matmul(to, lhsT, rhs, start=start, stop=stop)

            def halves(to, lhsT, rhs):
                for b in range(2):
                    last = mm(to[:, b * HALF:(b + 1) * HALF], lhsT, rhs[:, b * HALF:(b + 1) * HALF])
                return last

            def qk0(it):
                n = it.image["A"]
                pe.wait_ge(x_in[n.parity], n.at_own_parity(16, 16))
                halves(d_slot(it, "qk0")[0:2 * D, :], wqk0[:], xin[:, n.parity, :]).then_inc(d_full, 1)

            def v_l0(it, b):
                n = it.image["A"]
                slot = e_slot(it, "v0", b)
                for t in range(4):
                    px = (4 * b + t) * P
                    last = mm(slot[:, t * P:(t + 1) * P], xin[:, n.parity, px:px + P], wv0[:])
                last.then_inc(e_full, 1)

            def max0(it, t):
                n = it.image["A"]
                if t == 0:
                    pe.wait_ge(stacks0_in, n.at(2 * PARTS * 16, 2 * PARTS * 16))
                halves(d_slot(it, "max0", t), mov0[0:ROWS, t * P:(t + 1) * P], stat0[0:ROWS, :]).then_inc(d_full, 1)

            def mrow0(it, b):
                n = it.image["A"]
                slot = e_slot(it, "mrow0", b)
                pe.wait_ge(neg0_done, n.at(NEGS, NEGS))
                for t in range(4):
                    last = mm(slot[MROW:STACK, t * P:(t + 1) * P], neg0[:, 4 * b + t, :], identb[:])
                last.then_inc(e_full, 1)

            def pv0(it, t, b):
                pe.wait_ge(e_read, it.e("exp0", t, b))
                mm(o[:, b * HALF:(b + 1) * HALF], v0[:, t, :], p0[:, b, :], t == 0, t == TILES - 1)\
                    .then_inc(pv0_done, 1)

            def exp0(it, t, b):
                if t == 0 and b == 0:
                    pe.wait_ge(e_read, it.e("mrow0", 1))
                    done = it.image["C2"].at(1, 0) if "C2" in it.image else max(0, min(it.c - SHIFT["C2"], IMAGES))
                    wait(pe, o2_read, done)
                mm(e_slot(it, "exp0", t, b)[:], stat0[:, t * P:(t + 1) * P], mov0[:, b * HALF:(b + 1) * HALF])\
                    .then_inc(e_full, 1)
                if t or b:
                    pv0(it, t if b else t - 1, 1 - b)

            def pv0_end(it):
                pv0(it, TILES - 1, 1)

            def out0(it):
                slot = d_slot(it, "out0")
                pe.wait_ge(o0_read, it.image["A"].at(1, 1))
                for t in range(TILES):
                    last = pe.transpose(slot[:, t * P:t * P + C + 1], att0[:, t * P:(t + 1) * P], ident1)
                last.then_inc(d_full, 1)

            def in0(it):
                n = it.image["A"]
                slot = d_slot(it, "in0")
                for t in range(TILES):
                    last = pe.transpose(slot[:, t * P:t * P + C + 1], xin[:, n.parity, t * P:(t + 1) * P], ident1)
                last.then_inc(d_full, 1)

            def back(slot, src):
                flat = src[:].rearrange("p t c -> p (t c)")
                for q in range(TILES // 2):
                    last = pe.transpose(slot[:, q * P:(q + 1) * P], flat[:, q * P:(q + 1) * P], identf[:])
                last.then_inc(e_full, 1)

            def back0(it):
                slot = e_slot(it, "back0")
                pe.wait_ge(d_read, it.d("in0"))
                back(slot, xt)

            def conv(it, b):
                n = it.image["A"]
                slot = e_slot(it, "conv", b)
                pe.wait_ge(e_read, it.e("back0"))
                for k in range(3):
                    for g, taps in enumerate(CONV_GROUPS):
                        if k < len(taps):
                            ky, kx = taps[k] // 3, taps[k] % 3
                            src = (xl, xc[:, n.parity, :], xr)[kx]
                            at = (ky + b * H // 2) * W
                            last = mm(slot[32 * g:32 * g + 32, :], woff[:, taps[k], :], src[:, at:at + HALF],
                                      k == 0, k == len(taps) - 1)
                last.then_inc(e_full, 1)

            def offsets(it):
                slot = d_slot(it, "offsets")
                pe.wait_ge(e_read, it.e("conv", 1))
                for t in range(TILES):
                    last = mm(slot[:, t * P:(t + 1) * P], cs[:, t * P:(t + 1) * P], gather_sel[:])
                last.then_inc(d_full, 1)

            def turn(it, t):
                n = it.image["B"]
                slot = e_slot(it, "turn", t)
                pe.wait_ge(scaled, n.at(SCALES * TILES, SCALES * (t + 1)))
                for q in range(4):
                    last = pe.transpose(slot[:, q * P:(q + 1) * P], gs[:, t % 2, 0, 2 * q * C:2 * (q + 1) * C],
                                        identf[:])
                last.then_inc(e_full, 1)
                slot = e_slot(it, "turn", t, use=1)
                flat = gs[:, t % 2, :, :].rearrange("p c k -> p (c k)")
                pe.transpose(slot[:, 0:P], flat[:, 8 * C:10 * C], identf[:]).then_inc(e_full, 1)

            def deform(it, t):
                slot = d_slot(it, "deform", t)
                pe.wait_ge(e_read, it.e("turn", t, use=1))
                for q in range(5):
                    k = P if q < 4 else C
                    last = mm(slot[0:C, 0:P], wd[0:k, q, :], ts[0:k, t % 2, q * P:(q + 1) * P], q == 0, q == 4)
                last.then_inc(d_full, 1)

            def stat(it):
                n = it.image["C1"]
                slot = d_slot(it, "stat")
                pe.wait_ge(stat_done, n.at(STAT_OPS, 6))
                mm(slot[:, 0:P], group_mean[:], stat_in[:]).then_inc(d_full, 1)

            def qk2(it):
                n = it.image["C1"]
                slot = d_slot(it, "qk2")
                pe.wait_ge(stat_done, n.at(STAT_OPS, STAT_OPS))
                halves(slot, wqk2[:], ha[:]).then_inc(d_full, 1)

            def v_l2(it, b):
                slot = e_slot(it, "v2", b)
                for t in range(4):
                    px = (4 * b + t) * P
                    last = mm(slot[:, t * P:(t + 1) * P], ha[:, px:px + P], wv2[:])
                last.then_inc(e_full, 1)

            def max2(it, h, t):
                n = it.image["C1"]
                if h == 0 and t == 0:
                    pe.wait_ge(stacks2_in, n.at(2 * PARTS * 16, 2 * PARTS * 16))
                halves(d_slot(it, "max2", h, t), mov2[0:ROWS, n.parity, h, t * P:(t + 1) * P],
                       stat2[0:ROWS, n.parity, h, :]).then_inc(d_full, 1)

            def mrow2(it, h, b):
                n = it.image["C1"]
                slot = e_slot(it, "mrow2", h, b)
                pe.wait_ge(neg2_done, n.at(NEGS * HEADS, NEGS * (h + 1)))
                for t in range(4):
                    last = mm(slot[MROW:STACK, t * P:(t + 1) * P], neg2[:, h, 4 * b + t, :], identb[:])
                last.then_inc(e_full, 1)

            def pv2(it, w):
                n = it.image["C2"]
                pe.wait_ge(e_read, it.e("exp2", w, HEADS - 1))
                t, b = w // 2, w % 2
                for h in range(HEADS):
                    last = mm(o[32 * h:32 * h + 32, b * HALF:(b + 1) * HALF], va[:, n.parity, t, 32 * h:32 * h + 32],
                              p2[:, w % 2, h, :], t == 0, t == TILES - 1)
                last.then_inc(pv2_done, 1)

            def exp2(it, w, h):
                n = it.image["C2"]
                if w == 0 and h == 0:
                    pe.wait_ge(e_read, it.before().e("mrow2", HEADS - 1, 1))
                    pe.wait_ge(o0_read, it.image["A"].at(1, 1) if "A" in it.image else IMAGES)
                t, b = w // 2, w % 2
                mm(e_slot(it, "exp2", w, h)[:], stat2[:, n.parity, h, t * P:(t + 1) * P],
                   mov2[:, n.parity, h, b * HALF:(b + 1) * HALF]).then_inc(e_full, 1)
                if h == 1 and w:
                    pv2(it, w - 1)

            def pv2_end(it):
                pv2(it, 15)

            def sums(it):
                n = it.image["C3"]
                slot = d_slot(it, "sums")
                pe.wait_ge(o2_read, n.at(1, 1))
                for t in range(TILES):
                    last = pe.transpose(slot[:, t * P:(t + 1) * P], att[:, t * P:(t + 1) * P], identf[:])
                last.then_inc(d_full, 1)

            def back2(it):
                slot = e_slot(it, "back2")
                pe.wait_ge(d_read, it.d("sums"))
                back(slot, r2t)

            def proj(it, b):
                slot = d_slot(it, "proj", b)
                pe.wait_ge(e_read, it.e("back2"))
                mm(slot[:, 0:HALF], wproj[:], att[0:C, b * HALF:(b + 1) * HALF]).then_inc(d_full, 1)

            def x2t_step(it, b):
                slot = e_slot(it, "x2t", b)
                pe.wait_ge(d_read, it.d("proj", 1))
                for t in range(4):
                    px = (4 * b + t) * P
                    last = pe.transpose(slot[:, t * P:t * P + C + 1], x2[:, px:px + P], ident1)
                last.then_inc(e_full, 1)

            def sigma(it):
                slot = d_slot(it, "sigma")
                pe.wait_ge(e_read, it.e("x2t", 1))
                for t in range(TILES):
                    last = mm(slot[0:C, 0:P], x2t[:, t, 0:C], x2t[:, t, :], t == 0, t == TILES - 1)
                last.then_inc(d_full, 1)

            pe.wait_ge(s_w, 16 * len(loads))
            pe.wait_ge(s_ones, N_ONES)
            pe.wait_ge(s_prep, N_PREP)
            run(pe, {"qk0": qk0, "v0": v_l0, "max0": max0, "mrow0": mrow0, "exp0": exp0, "pv0_end": pv0_end,
                     "out0": out0, "in0": in0, "back0": back0, "conv": conv, "offsets": offsets, "turn": turn,
                     "deform": deform, "stat": stat,
                     "qk2": qk2, "v2": v_l2, "max2": max2, "mrow2": mrow2, "exp2": exp2, "pv2_end": pv2_end,
                     "sums": sums, "back2": back2, "proj": proj, "x2t": x2t_step, "sigma": sigma})

            small = dring[0]
            k = [0]

            def product(rows, cols, lhsT, rhs):
                k[0] += 1
                pe.wait_ge(f_dve, k[0])
                mm(small[0:rows, 0:cols], lhsT, rhs).then_inc(f_pe, 1)

            product(1, C, mean[:], identf[0:C, 0:C])
            product(C, C, mrow[:], mrow[:])
            product(C, 1, mask[:], tr[:, 0:1])
            for _ in range(STEPS):
                product(C, C, pm[:], pm[:])
                product(C, C, pa[:], pm[:])
                product(C, C, tmp[:], cov[:])
            product(C, 1, w2[0:C, 0:C], mean[:])
            pe.wait_ge(f_dve, k[0] + 1)
            with pe.Fori(0, IMAGES // 4) as j:
                for b in range(2):
                    pe.wait_ge(fin_in[b], j * 16 + 16)
                    pe.wait_ge(d_read, j * 2 + (D_ALL + b - 1))
                    halves(dring[b], w2[:], fin_src[b]).then_inc(d_full, 1)

        @block.scalar
        def _(act):
            def take(it, name, *args, use=0):
                act.wait_ge(e_full, it.e(name, *args, use=use))
                return ering[it.slot("e", name, *args, use=use)]

            def v_l0(it, b):
                n = it.image["A"]
                slot = take(it, "v0", b)
                wait(act, pv0_done, n.at(16, 0))
                act.activation(v0[:, 4 * b:4 * b + 4, :].rearrange("p t c -> p (t c)"), slot[:], ACT.Copy)\
                    .then_inc(e_read, 1)

            def mrow0(it, b):
                slot = take(it, "mrow0", b)
                act.activation(mov0[MROW:STACK, b * HALF:(b + 1) * HALF], slot[MROW:STACK, :], ACT.Copy)\
                    .then_inc(e_read, 1)

            def exp0(it, t, b):
                n = it.image["A"]
                slot = take(it, "exp0", t, b)
                wait(act, pv0_done, n.at(16, 2 * t + b - 1))
                act.activation(p0[:, b, :], slot[:], ACT.Exp).then_inc(e_read, 1)

            def high(name, parts, image_of, stored, done, rows, **scale):
                def step(it):
                    n = it.image[image_of]
                    act.wait_ge(d_full, it.d(name))
                    wait(act, stored, n.at(16, 0))
                    act.activation(parts[:, 0, :], dring[it.slot("d", name)][0:rows, :], ACT.Copy, **scale)\
                        .then_inc(done, 1)
                return step

            def attended0(it):
                n = it.image["A"]
                act.wait_ge(pv0_done, n.at(16, 16))
                if it.has_before("A"):
                    act.wait_ge(d_full, it.before().d("out0"))
                act.activation(att0[:], o[0:ONE + 1, :], ACT.Copy).then_inc(o0_read, 1)

            def back0(it):
                n = it.image["A"]
                slot = take(it, "back0")
                if it.has_before("A"):
                    act.wait_ge(e_full, it.before().e("conv", 1))
                for move, image in ((0, xc[0:C, n.parity]), (1, xl[0:C, :]), (-1, xr[0:C, :])):
                    rows = image[:, W:W + PX].rearrange("c (q s r x) -> c q s r x", s=2, r=P // W, x=W)
                    for odd in range(2):
                        src = slot[odd * C:(odd + 1) * C, :].rearrange("c (q r x) -> c q r x", r=P // W, x=W)
                        last = act.activation(rows[:, :, odd, :, max(move, 0):W + min(move, 0)],
                                              src[:, :, :, max(-move, 0):W - max(move, 0)], ACT.Copy)
                last.then_inc(e_read, 1)

            def conv(it, b):
                slot = take(it, "conv", b)
                if it.has_before("A"):
                    act.wait_ge(d_full, it.before().d("offsets"))
                act.wait_ge(split0, it.image["A"].at(SPLITS, SPLITS))
                if "C1" in it.image:
                    act.wait_ge(split2, it.image["C1"].at(SPLITS, SPLITS))
                act.activation(cs[:, b * HALF:(b + 1) * HALF], slot[:], ACT.Copy).then_inc(e_read, 1)

            def turn(it, t):
                slot = take(it, "turn", t)
                if t >= 2:
                    act.wait_ge(d_full, it.d("deform", t - 2))
                elif it.has_before("B"):
                    act.wait_ge(d_full, it.before().d("deform", TILES + t - 2))
                act.activation(ts[:, t % 2, 0:4 * P], slot[:], ACT.Copy).then_inc(e_read, 1)
                slot = take(it, "turn", t, use=1)
                act.activation(ts[0:C, t % 2, 4 * P:5 * P], slot[0:C, 0:P], ACT.Copy).then_inc(e_read, 1)

            def relu(it, t):
                n = it.image["B"]
                act.wait_ge(d_read, it.d("deform", t))
                if t == 0:
                    wait(act, stat_done, n.at(STAT_OPS, -STAT_OPS))
                    wait(act, kept_ready, n.at(1, -1))
                act.activation(x1[:, n.parity, t * P:(t + 1) * P], y1[:, t % 2, :], ACT.Relu, bias=bn[:, 3:4])\
                    .then_inc(x1_ready, 1)

            def keep(it):
                n = it.image["C1"]
                if "C3" in it.image:
                    act.wait_ge(d_read, it.d("proj", 1))
                act.wait_ge(x1_ready, n.at(TILES, TILES))
                act.activation(kept[:, n.parity, :], x1[:, n.parity, :], ACT.Copy).then_inc(kept_ready, 1)

            def v_l2(it, b):
                n = it.image["C1"]
                slot = take(it, "v2", b)
                wait(act, pv2_done, n.at(16, -16))
                act.activation(va[:, n.parity, 4 * b:4 * b + 4, :].rearrange("p t c -> p (t c)"), slot[:], ACT.Copy)\
                    .then_inc(e_read, 1)

            def mrow2(it, h, b):
                n = it.image["C1"]
                slot = take(it, "mrow2", h, b)
                act.activation(mov2[MROW:STACK, n.parity, h, b * HALF:(b + 1) * HALF], slot[MROW:STACK, :], ACT.Copy)\
                    .then_inc(e_read, 1)

            def exp2(it, w, h):
                n = it.image["C2"]
                slot = take(it, "exp2", w, h)
                wait(act, pv2_done, n.at(16, w - 1))
                act.activation(p2[:, w % 2, h, :], slot[:], ACT.Exp).then_inc(e_read, 1)

            def attended(it):
                n = it.image["C3"]
                act.wait_ge(pv2_done, n.at(16, 16))
                if it.has_before("C3"):
                    act.wait_ge(d_full, it.before().d("proj", 1))
                act.activation(att[:], o[:], ACT.Copy).then_inc(o2_read, 1)

            def back2(it):
                slot = take(it, "back2")
                to = att[0:C, :].rearrange("c (q s p) -> c q s p", s=2, p=P)
                for odd in range(2):
                    last = act.activation(to[:, :, odd, :],
                                          slot[odd * C:(odd + 1) * C, :].rearrange("c (q p) -> c q p", p=P), ACT.Copy)
                last.then_inc(e_read, 1)

            def x2t_step(it, b):
                slot = take(it, "x2t", b).rearrange("p (t c) -> p t c", c=P)
                if it.has_before("C3"):
                    act.wait_ge(d_full, it.before().d("sigma"))
                act.activation(x2t[:, 4 * b:4 * b + 4, 0:C + 1], slot[:, :, 0:C + 1], ACT.Copy)\
                    .then_inc(e_read, 1)

            act.wait_ge(s_w, 16 * len(loads))
            act.wait_ge(s_ones, N_ONES)
            act.wait_ge(s_prep, N_PREP)
            run(act, {"split0": high("qk0", parts0, "A", parts0_out, high0, 2 * D),
                      "split2": high("qk2", parts2, "C1", parts2_out, high2, P, scale=qscale[:]),
                      "v0": v_l0, "mrow0": mrow0, "exp0": exp0, "attended0": attended0, "back0": back0, "conv": conv,
                      "turn": turn, "relu": relu, "keep": keep, "v2": v_l2, "mrow2": mrow2, "exp2": exp2,
                      "attended": attended, "back2": back2, "x2t": x2t_step})


def constants():
    f = np.float32
    px = np.arange(PX).reshape(TILES, P)
    grid = np.empty((P, TILES, OFFS), f)
    grid[:, :, 0:TAPS] = (px // W + 1).T[:, :, None]
    grid[:, :, TAPS:] = (px % W + 1).T[:, :, None]
    gather_sel = np.zeros((P, P), f)
    for g in range(4):
        gather_sel[32 * g + np.arange(OFFS), np.arange(OFFS)] = 1
    channel = np.arange(C)
    return {
        "identf": np.eye(P, dtype=f), "grid": grid,
        "gather_sel": gather_sel,
        "qscale": np.where(np.arange(P) < C, f(D ** -0.5), f(1))[:, None].astype(f),
        "group_mean": ((channel[:, None] // 8 == np.arange(P)[None, :] // 8) / 32).astype(f),
        "mask": (channel[:, None] // GROUP == channel[None, :] // GROUP).astype(f),
    }


def layout(i):
    f = np.float32
    out = {"x": i["x"].reshape(IMAGES, C, PX)}
    out["wqk0"] = np.concatenate([np.concatenate([i["L0_conv_wq"].T, i["L0_conv_wk"].T], 1),
                                  np.concatenate([i["L0_conv_bq"], i["L0_conv_bk"]])[None]], 0)
    wv0 = np.zeros((C + 1, P), f)
    wv0[0:C, 0:C] = i["L0_conv_wv"].T
    wv0[C, 0:C] = i["L0_conv_bv"]
    wv0[C, C:] = 1
    out["wv0"] = wv0
    w6 = np.zeros((C + 1, TAPS, 6), f)
    w6[0:C] = np.concatenate([i["L1_conv_w_tm"], i["L1_conv_w_tr"]], 0).reshape(6, C, TAPS).transpose(1, 2, 0)
    w6[C, TAPS // 2] = np.concatenate([i["L1_conv_b_tm"], i["L1_conv_b_tr"]])
    out["w6"] = w6
    wd = np.zeros((2, C, 5, C), f)
    taps = i["L1_conv_w_deform"].reshape(C, C, TAPS).transpose(2, 1, 0)
    for k in range(TAPS):
        wd[k % 2, :, k // 2, :] = taps[k]
    out["wd"] = wd.reshape(P, 5, C)
    wqkv, bqkv = i["L2_conv_w_qkv"], i["L2_conv_b_qkv"]
    out["wqk2"] = np.concatenate([wqkv[0:2 * C].T, bqkv[None, 0:2 * C]], 0)
    wv2 = np.zeros((C + 1, HEADS, 2 * D), f)
    wv2[0:C, :, 0:D] = wqkv[2 * C:].T.reshape(C, HEADS, D)
    wv2[C, :, 0:D] = bqkv[2 * C:].reshape(HEADS, D)
    wv2[C, :, D:] = 1
    out["wv2"] = wv2.reshape(C + 1, P)
    out["wproj"] = np.concatenate([i["L2_conv_w_proj"].T, np.zeros((C, C), f)], 1)
    out["gamma"] = np.broadcast_to(i["L0_conv_gamma"], (P, 1))
    out["vecs"] = np.stack([i["L1_conv_bn_gamma"], i["L1_conv_bn_beta"], i["L1_conv_bn_mean"], i["L1_conv_bn_var"],
                            i["L2_conv_gn_w"], i["L2_conv_gn_b"], i["L2_conv_b_proj"],
                            i["L3_conv_bias"].reshape(C)], 1)
    out["w3row"] = np.broadcast_to(i["L3_conv_weight"].reshape(1, C), (C, C))
    return out


def kernel(**inputs):
    import concourse.bacc as bacc
    from concourse.bass_utils import run_bass_kernel_spmd

    arrays = layout({k: np.asarray(v) for k, v in inputs.items()}) | constants()
    arrays = {f"in_{k}": np.ascontiguousarray(v) for k, v in arrays.items()}
    nc = bacc.Bacc("TRN2", target_bir_lowering=False, num_devices=1)
    args = {k[3:]: nc.dram_tensor(k, v.shape, mybir.dt.from_np(v.dtype), kind="ExternalInput").ap()
            for k, v in arrays.items()}
    out = nc.dram_tensor("out", (IMAGES, C, H, W), F32, kind="ExternalOutput").ap()
    build(nc, args, out)
    r = run_bass_kernel_spmd(nc, [arrays], core_ids=[0])
    return r.results[0]["out"]
```

```python
from contextlib import ExitStack

import concourse.bass as bass
import numpy as np
from concourse import mybir

F32 = mybir.dt.float32
BF16 = mybir.dt.bfloat16
I32 = mybir.dt.int32
ALU = mybir.AluOpType
ACT = mybir.ActivationFunctionType
AX = mybir.AxisListType

IMAGES, C, H, W = 32, 64, 32, 32
PX = H * W
P = 128
TILES = PX // P
HALF = PX // 2
D = 16
HEADS = C // D
TAPS = 9
CORNERS = 4
PARTS = 6
ROWS = PARTS * D
MROW = ROWS
STACK = ROWS + 2
ONE = C
STAT_PARTS = (0, 0, 1, 1, 0, 2)
MOV_PARTS = (0, 1, 0, 1, 2, 0)
MAP_H, MAP_W = H + 1, W + 2
TABLE = MAP_H * MAP_W
EPS = 1e-5
GROUP = 16
STEPS = 5
REG = ((-1, -1, -1, 0, 0, 0, 1, 1, 1), (-1, 0, 1, -1, 0, 1, -1, 0, 1))
CONV_GROUPS = ((0, 1, 2), (3, 4), (5, 6), (7, 8))
OFFS = 2 * TAPS

SHIFT = {"A0": 0, "A1": 1, "B0": 1, "B1": 2, "C1": 2, "M": 3, "C2": 4, "C3": 5}
LAST_SHIFT = 5
B_TILES = {"B1": range(TILES // 2, TILES), "B0": range(TILES // 2)}
PEELED = LAST_SHIFT + LAST_SHIFT % 2
D_STEPS = {"qk0": 1, "max0": 1, "out0": 1, "in0": 1, "offsets": 1, "deform": 1, "stat": 1, "qk2": 1, "max2": 1,
           "sums": 1, "proj": 1,
           "sigma": 1}
E_STEPS = {"v0": 1, "mrow0": 1, "exp0": 1, "back0": 1, "conv": 1, "turn": 2, "v2": 1, "mrow2": 1, "exp2": 1, "back2": 1, "x2t": 1}
D_USES = {"A0": 9, "A1": 3, "B0": 2, "B1": 2, "C1": 2, "M": 32, "C2": 0, "C3": 4}
E_USES = {"A0": 2, "A1": 21, "B0": 8, "B1": 8, "C1": 2, "M": 8, "C2": 64, "C3": 3}
SPLITS, NEGS, NORMS, SCALES, OFFSET_OPS, STAT_OPS = 2, 2, 2, 5, 14, 23


class Image:

    def __init__(self, j, c):
        self.j, self.c = j, c
        self.parity = c % 2
        self.n = c if isinstance(j, int) else j * 2 + c

    def at(self, per_image, k):
        const = self.c * per_image + k
        return const if isinstance(self.j, int) else self.j * (2 * per_image) + const

    def at_own_parity(self, per_image, k):
        const = self.c // 2 * per_image + k
        return const if isinstance(self.j, int) else self.j * per_image + const


class Iteration:

    def __init__(self, j, c):
        self.j, self.c = j, c
        loop = not isinstance(j, int)
        self.image = {s: Image(j, c - sh) for s, sh in SHIFT.items() if loop or 0 <= c - sh < IMAGES}
        self.steps = order(self.image)
        self.numbers = {}
        for ring, steps in (("d", D_STEPS), ("e", E_STEPS)):
            k = 0
            for _, name, *args in self.steps:
                for use in range(steps.get(name, 0)):
                    self.numbers[(ring, name, *args, use)] = k
                    k += 1

    def _count(self, ring, uses, name, args, use):
        const, slope = self.numbers[(ring, name, *args, use)] + 1, 0
        for s, sh in SHIFT.items():
            if isinstance(self.j, int):
                const += uses[s] * min(max(self.c - sh, 0), IMAGES)
            else:
                const += uses[s] * (self.c - sh)
                slope += 2 * uses[s]
        return const if isinstance(self.j, int) else self.j * slope + const

    def d(self, name, *args, use=0):
        return self._count("d", D_USES, name, args, use)

    def e(self, name, *args, use=0):
        return self._count("e", E_USES, name, args, use)

    def slot(self, ring, name, *args, use=0):
        uses = D_USES if ring == "d" else E_USES
        const = sum(uses[s] * (self.c - sh if not isinstance(self.j, int) else min(max(self.c - sh, 0), IMAGES))
                    for s, sh in SHIFT.items())
        return (const + self.numbers[(ring, name, *args, use)]) % 2

    def before(self):
        return Iteration(self.j, self.c - 1)

    def has_before(self, stage):
        return not isinstance(self.j, int) or 0 <= self.c - 1 - SHIFT[stage] < IMAGES


def b_stage(t):
    return "B1" if t in B_TILES["B1"] else "B0"


def tiles_before(it, t, k):
    if t - k < 0:
        return it if "B1" in it.image else None
    return it if b_stage(t - k) == b_stage(t) else it.before()


def wait(eng, sem, value):
    if not (isinstance(value, int) and value <= 0):
        eng.wait_ge(sem, value)


class Chain:

    def __init__(self, eng, sem, image, per_image, first=0):
        self.eng, self.sem, self.image, self.per_image, self.k = eng, sem, image, per_image, first

    def __call__(self, instruction):
        self.k += 1
        instruction.then_inc(self.sem, 1)
        self.eng.wait_ge(self.sem, self.image.at(self.per_image, self.k))


PLACE = {
    "load": 4.0143, "qk0": 4.6, "v0": 5.4173, "max0": 5.8593, "max0_next": 0.2392, "neg0": 7.5568,
    "mrow0": -0.3558, "exp0": 0.1, "exp0_next": 0.08, "attended0": 1.3453, "out0": 1.5415, "back0": 1.7054,
    "conv": 1.9, "conv_next": 0.2125, "offsets": 2.2957, "gather": -0.6056, "scale": -0.1, "scale_next": 0.0645,
    "turn": 0.5, "deform": 0.8796, "relu": 0.9209, "means": 4.2831, "stat": 4.6924, "qk2": 6.1296,
    "spread2": 7.8, "v2": 7.9257, "keep": 0.8956, "max2": 0.7102, "max2_next": 0.22, "max2_swing": 0,
    "max2_phase": 0.0, "neg2": 0.0261, "mrow2": 0.3763, "mrow2_next": 0.0884, "exp2": 1.4985,
    "exp2_next": 0.097, "exp2_swing": 0.5, "exp2_phase": 0.7, "pv2_end": 7.7234, "attended": 0.02,
    "sums": 0.1688, "back2": 0.4313, "proj": 0.5551, "x2t": 0.9061, "sigma": 1.8346,
}


def order(image):
    at, s = PLACE, []

    def swung(name, k):
        x = at[name] + k * at[name + "_next"]
        return x + at[name + "_swing"] / 6.2832 * float(np.sin(6.2832 * (x - at[name + "_phase"])))

    if "A0" in image:
        s += [(at["load"], "load"), (at["qk0"], "qk0"), (at["qk0"] + 0.002, "split0"), (at["qk0"] + 0.004, "spread0")]
        s += [(at["v0"] + 0.001 * b, "v0", b) for b in range(2)]
        s += [(at["max0"] + at["max0_next"] * t, "max0", t) for t in range(TILES)] + [(at["neg0"], "neg0")]
    if "A1" in image:
        s += [(at["mrow0"], "mrow0", 0), (at["mrow0"] + 0.001, "mrow0", 1)]
        s += [(at["exp0"] + at["exp0_next"] * u, "exp0", u // 2, u % 2) for u in range(16)]
        s += [(at["exp0"] + at["exp0_next"] * 15 + 0.06, "pv0_end"), (at["attended0"], "attended0")]
        s += [(at["out0"], "out0"), (at["out0"] + 0.005, "in0"), (at["out0"] + 0.01, "map"), (at["back0"], "back0")]
        s += [(at["conv"] + at["conv_next"] * b, "conv", b) for b in range(2)] + [(at["offsets"], "offsets")]
    for stage, tiles in B_TILES.items():
        if stage in image:
            for t in tiles:
                here = (t + TILES // 2) % TILES
                s += [(here + at["gather"], "gather", t), (here + at["turn"], "turn", t)]
                s += [(here + at["scale"] + at["scale_next"] * k, "scale", t, k) for k in range(4)]
                if t % 2:
                    s += [(here + at["deform"], "deform", t // 2), (here + at["relu"], "relu", t // 2)]
    if "C1" in image:
        s += [(at["means"], "means"), (at["stat"], "stat"), (at["qk2"], "qk2"), (at["qk2"] + 0.002, "split2"),
              (at["spread2"], "spread2")]
        s += [(at["v2"] + 0.001 * b, "v2", b) for b in range(2)]
    if "M" in image:
        s += [(at["keep"], "keep")]
        s += [(swung("max2", u), "max2", u // TILES, u % TILES) for u in range(HEADS * TILES)]
        for h in range(HEADS):
            done = swung("max2", TILES * h + TILES - 1)
            s += [(done + at["neg2"], "neg2", h)]
            s += [(done + at["mrow2"] + at["mrow2_next"] * b, "mrow2", h, b) for b in range(2)]
    if "C2" in image:
        s += [(swung("exp2", u), "exp2", u // HEADS, u % HEADS) for u in range(64)] + [(at["pv2_end"], "pv2_end")]
    if "C3" in image:
        s += [(at["attended"], "attended"), (at["sums"], "sums"), (at["back2"], "back2"), (at["proj"], "proj", 0),
              (at["proj"] + 0.001, "proj", 1), (at["proj"] + 0.002, "store"), (at["x2t"], "x2t", 0),
              (at["x2t"] + 0.001, "x2t", 1), (at["sigma"], "sigma")]
    return sorted(s, key=lambda step: step[0])


def build(nc, a, out):
    with ExitStack() as ctx:
        def sb(name, shape, dt=F32):
            return ctx.enter_context(nc.sbuf_tensor(name, shape, dt))

        def sem(name):
            return ctx.enter_context(nc.semaphore(name))

        parts0_d = nc.dram_tensor("parts0_d", (2, 3, 2 * D, PX), BF16, kind="Internal").ap()
        parts2_d = nc.dram_tensor("parts2_d", (2, 3, 2 * C, PX), BF16, kind="Internal").ap()
        table_d = [nc.dram_tensor(f"table{p}_d", (TABLE, 2 * C), F32, kind="Internal").ap() for p in range(2)]
        x2_d = nc.dram_tensor("x2_d", (IMAGES, C, PX), F32, kind="Internal").ap()

        identf = sb("identf", [P, P])
        identb = sb("identb", [P, P], BF16)
        wqk0 = sb("wqk0", [P, 2 * D])
        wv0 = sb("wv0", [P, P])
        w6 = sb("w6", [P, TAPS, 6])
        woff = sb("woff", [P, TAPS, 32])
        grid = sb("grid", [P, TILES, OFFS])
        gather_sel = sb("gather_sel", [P, P])
        wd = sb("wd", [P, 5, C])
        wqk2 = sb("wqk2", [P, P])
        wv2 = sb("wv2", [P, P])
        qscale = sb("qscale", [P, 1])
        group_mean = sb("group_mean", [P, P])
        wproj = sb("wproj", [P, P])
        gamma = sb("gamma", [P, 1])
        vecs = sb("vecs", [P, 8])
        bn_g, bn_b, bn_m, bn_v = (vecs[:, k:k + 1] for k in range(4))
        gn_w, gn_b, bias3 = (vecs[0:C, k:k + 1] for k in (4, 5, 7))
        b_proj = vecs[C:P, 6:7]
        w3row = sb("w3row", [C, C])
        mask = sb("mask", [C, C])
        bn = sb("bn", [P, 4])
        newton = sb("newton", [P, 4])
        zeros = sb("zeros", [MAP_W, P])
        nothing = sb("nothing", [1, 1])

        xin = sb("xin", [P, 2, PX])
        parts0 = sb("parts0", [2 * D, 3, PX], BF16)
        rest = sb("rest", [P, PX])
        stat0 = sb("stat0", [STACK, PX], BF16)
        mov0 = sb("mov0", [STACK, PX], BF16)
        v0 = sb("v0", [P, TILES, P])
        mx0 = sb("mx0", [P, TILES])
        neg0 = sb("neg0", [P, TILES, 2], BF16)
        p0 = sb("p0", [P, 2, HALF])
        att0 = sb("att0", [P, PX])
        rs0 = sb("rs0", [P, TILES])
        xc = sb("xc", [P, 2, (H + 2) * W])
        xl = sb("xl", [P, (H + 2) * W])
        xr = sb("xr", [P, (H + 2) * W])
        xt = sb("xt", [P, TILES, C])
        cs = rest
        pos = sb("pos", [P, TILES, OFFS])
        flo = sb("flo", [P, TILES, OFFS])
        rnd = sb("rnd", [P, TILES, OFFS], I32)
        one_less = sb("one_less", [P, TILES, OFFS])
        idx = sb("idx", [P, 2, TILES, TAPS], I32)
        wt = sb("wt", [P, 2, TILES, TAPS, CORNERS])

        G = sb("G", [P, 2, TAPS * CORNERS * C])
        gs = sb("gs", [P, 2, CORNERS, TAPS * C])
        ts = sb("ts", [P, 4, 5 * P])
        res = sb("res", [P, 2, HALF])
        y1 = sb("y1", [P, 2, P])
        x1k = sb("x1k", [P, 2, PX])
        x1, kept = x1k[0:C], x1k[C:P]

        bnst = sb("bnst", [C, 2, 6])
        mv = sb("mv", [C, 4])
        stat_in = sb("stat_in", [P, P])
        gm = sb("gm", [C, 8])
        ha = sb("ha", [P, PX])
        parts2 = sb("parts2", [P, 3, PX], BF16)
        stat2 = sb("stat2", [STACK, 2, HEADS, PX], BF16)
        mov2 = sb("mov2", [STACK, 2, HEADS, PX], BF16)
        va = sb("va", [P, 2, TILES, P])
        mx2 = sb("mx2", [P, HEADS, TILES])
        neg2 = sb("neg2", [P, HEADS, TILES, 2], BF16)
        p2 = sb("p2", [P, 2, HEADS, HALF])
        att = sb("att", [P, PX])
        rs2 = sb("rs2", [P, TILES, HEADS])
        r2t = sb("r2t", [P, TILES, C])
        x2 = sb("x2", [P, PX])
        x2t = sb("x2t", [P, TILES, P])
        sig = sb("sig", [C, P])

        mean = sb("mean", [C, 1])
        mrow = sb("mrow", [1, C])
        cov, tmp, pm, pa = (att0[0:C, k * C:(k + 1) * C] for k in range(4))
        w2 = sb("w2", [P, P])
        b2 = sb("b2", [P, 1])
        tr = sb("tr", [C, 4])

        dring = [ctx.enter_context(nc.psum_tensor(f"dring{i}", [P, PX], F32)) for i in range(2)]
        ering = [ctx.enter_context(nc.psum_tensor(f"ering{i}", [P, HALF], F32)) for i in range(2)]
        o = ctx.enter_context(nc.psum_tensor("o", [P, PX], F32))

        s_w = sem("s_w")
        s_ones = sem("s_ones")
        s_border = sem("s_border")
        s_prep = sem("s_prep")
        d_full, d_read = sem("d_full"), sem("d_read")
        e_full, e_read = sem("e_full"), sem("e_read")
        x_in = [sem("x_in0"), sem("x_in1")]
        high0, high2 = sem("high0"), sem("high2")
        split0, parts0_out, stacks0_in = sem("split0"), sem("parts0_out"), sem("stacks0_in")
        neg0_done, pv0_done, o0_read, norm0_done = sem("neg0_done"), sem("pv0_done"), sem("o0_read"), sem("norm0_done")
        map_out, offsets_done = sem("map_out"), sem("offsets_done")
        gathered = [sem("gathered0"), sem("gathered1")]
        scaled, x1_ready = sem("scaled"), sem("x1_ready")
        stat_done, kept_ready = sem("stat_done"), sem("kept_ready")
        split2, parts2_out, stacks2_in = sem("split2"), sem("parts2_out"), sem("stacks2_in")
        neg2_done, pv2_done, o2_read = sem("neg2_done"), sem("pv2_done"), sem("o2_read")
        normed2, x2_out = sem("normed2"), sem("x2_out")
        carried = sem("carried")
        f_dve, f_pe, f_hold = sem("f_dve"), sem("f_pe"), sem("f_hold")
        fin_in = [sem("fin_in0"), sem("fin_in1")]
        fin_out = [sem("fin_out0"), sem("fin_out1")]

        loads = (
            (identf, "identf"), (wqk0, "wqk0"), (wv0, "wv0"), (w6, "w6"), (grid, "grid"),
            (gather_sel, "gather_sel"), (wqk2, "wqk2"), (wv2, "wv2"), (qscale, "qscale"), (group_mean, "group_mean"),
            (gamma, "gamma"), (wproj, "wproj"), (vecs, "vecs"), (mask, "mask"), (wd, "wd"))
        D_ALL = IMAGES * sum(D_USES.values())

        def run(eng, steps):
            def iteration(it):
                for _, name, *args in it.steps:
                    if name in steps:
                        steps[name](it, *args)
            for c in range(PEELED):
                iteration(Iteration(0, c))
            with eng.Fori(PEELED // 2, IMAGES // 2) as j:
                for c in range(2):
                    iteration(Iteration(j, c))
            for c in range(IMAGES, IMAGES + LAST_SHIFT):
                iteration(Iteration(0, c))

        ones = (xin[ONE:P, :, :], ha[ONE:P, :], x2[0:C, :], xc[ONE:P, :, :], xl[ONE:P, :],
                xr[ONE:P, :], stat0[MROW:STACK, :], stat2[MROW:STACK, :, :, :])
        blanks = (xc[0:C, :, :], xl[0:C, :], xr[0:C, :], zeros[:], sig[:], stat_in[:], woff[:], w2[:], nothing[:])
        N_ONES = len(ones) + len(blanks)
        N_PREP = 1 + 18 + 24 + 15

        fin_src = [p2[:, b, 0:2, :].rearrange("p a n -> p (a n)") for b in range(2)]
        fin_dst = [G[:, b, 0:PX] for b in range(2)]
        x2_pairs = x2_d.rearrange("(m two) c n -> m (two c) n", two=2)
        out_pairs = out.rearrange("(m two) c h w -> m (two c) (h w)", two=2)

        block = ctx.enter_context(nc.Block())

        @block.sync
        def _(sp):
            for tile, name in loads:
                sp.dma_start(tile[:], a[name]).then_inc(s_w, 16)
            sp.dma_start(w3row[:], a["w3row"]).then_inc(x2_out, 16)
            sp.wait_ge(s_ones, N_ONES)
            borders = [t.rearrange("(y x) c -> y x c", x=MAP_W) for t in table_d]
            for m in range(2):
                for y in (0, MAP_H - 1):
                    sp.dma_start(borders[m][y, :, :], zeros[0:MAP_W, :]).then_inc(s_border, 16)
            sp.wait_ge(s_border, 16 * 4)
            for m in range(2):
                for x in (0, MAP_W - 1):
                    sp.dma_start(borders[m][:, x, :], zeros[0:MAP_H, :]).then_inc(s_border, 16)
            sp.wait_ge(s_border, 16 * 8)

            def load(it):
                n = it.image["A0"]
                if "A1" in it.image:
                    sp.wait_ge(d_read, it.d("in0"))
                sp.dma_start(xin[0:C, n.parity, :], a["x"][bass.ds(n.n, 1), :, :].rearrange("o c n -> (o c) n"))\
                    .then_inc(x_in[n.parity], 16)

            def spread0(it):
                n = it.image["A0"]
                sp.wait_ge(split0, n.at(SPLITS, SPLITS))
                sp.dma_start(parts0_d[n.parity].rearrange("t r n -> r t n"), parts0[:]).then_inc(parts0_out, 16)
                sp.wait_ge(parts0_out, n.at(16, 16))
                for b in range(PARTS):
                    sp.dma_start(stat0[D * b:D * b + D, :], parts0_d[n.parity, STAT_PARTS[b], 0:D, :])\
                        .then_inc(stacks0_in, 16)
                    sp.dma_start(mov0[D * b:D * b + D, :], parts0_d[n.parity, MOV_PARTS[b], D:2 * D, :])\
                        .then_inc(stacks0_in, 16)

            def table(it):
                n = it.image["A1"]
                sp.wait_ge(d_read, it.d("in0"))
                rows = table_d[n.parity].rearrange("(y x) (s c) -> y x s c", x=MAP_W, s=2)
                for r in range(P // W):
                    for s in range(2):
                        y = r + 1 - s
                        to = rows[y:y + 4 * (TILES - 1) + 1:4, 1:W + 1, s, :]
                        sp.dma_start(to.rearrange("t x c -> x t c"), xt[W * r:W * r + W, :, :]).then_inc(map_out, 16)

            def spread2(it):
                n = it.image["C1"]
                sp.wait_ge(parts2_out, n.at(16, 16))
                for b in range(PARTS):
                    for stack, part, at in ((mov2, MOV_PARTS[b], 0), (stat2, STAT_PARTS[b], C)):
                        src = parts2_d[n.parity, part, at:at + C, :].rearrange("(h d) n -> d h n", h=HEADS)
                        sp.dma_start(stack[D * b:D * b + D, n.parity, :, :], src).then_inc(stacks2_in, 16)

            def store(it):
                n = it.image["C3"]
                sp.wait_ge(d_read, it.d("proj", 1))
                sp.dma_start(x2_d[bass.ds(n.n, 1), :, :].rearrange("o c n -> (o c) n"), x2[C:P, :]).then_inc(x2_out, 16)

            run(sp, {"load": load, "spread0": spread0, "map": table, "spread2": spread2, "store": store})

            sp.wait_ge(x2_out, 16 + 16 * IMAGES)
            with sp.Fori(0, IMAGES // 4) as j:
                for b in range(2):
                    sp.wait_ge(d_full, j * 2 + (D_ALL + b - 1))
                    sp.dma_start(fin_src[b], x2_pairs[bass.ds(j * 2 + b, 1), :, :].rearrange("o c n -> (o c) n"))\
                        .then_inc(fin_in[b], 16)

        @block.gpsimd
        def _(pool):
            pool.wait_ge(s_ones, N_ONES)

            def gather(it, t):
                n = it.image[b_stage(t)]
                if t == 0:
                    pool.wait_ge(offsets_done, n.at(OFFSET_OPS, OFFSET_OPS))
                    pool.wait_ge(map_out, n.at(8 * 16, 8 * 16))
                wait(pool, carried, n.at(TILES, t))
                wait(pool, scaled, n.at(SCALES * TILES, SCALES * (t - 2) + 3))
                pool.tensor_tensor(nothing[:], nothing[:], nothing[:], ALU.add).then_inc(carried, 1)
                for k in range(TAPS):
                    pool.indirect_dma_start(
                        G[:, t % 2, CORNERS * C * k:CORNERS * C * (k + 1)], None, table_d[n.parity],
                        bass.IndirectOffsetOnAxis(idx[:, n.parity, t, k:k + 1], 0)).then_inc(gathered[t % 2], 16)

            run(pool, {"gather": gather})

        @block.vector
        def _(dve):
            def newton_rsqrt(step, v, y, t):
                step(dve.tensor_scalar(y.bitcast(I32), v.bitcast(I32), 1, None, ALU.logical_shift_right))
                step(dve.tensor_scalar(y.bitcast(I32), y.bitcast(I32), -1.0, float(0x5F3759DF), ALU.mult, ALU.add))
                for _ in range(3):
                    step(dve.scalar_tensor_tensor(t, y, v, y, ALU.mult, ALU.mult))
                    step(dve.tensor_scalar(t, t, -0.5, 1.5, ALU.mult, ALU.add))
                    step(dve.tensor_tensor(y, y, t, ALU.mult))

            def take(it, name, *args):
                dve.wait_ge(d_full, it.d(name, *args))
                return dring[it.slot("d", name, *args)]

            def split(it, name, n, parts, high, sem, rows, scale):
                slot = take(it, name)[0:rows, :]
                dve.wait_ge(high, n.at(1, 1))
                step = Chain(dve, sem, n, SPLITS)
                rs = rest[0:rows, :]
                dve.scalar_tensor_tensor(rs, slot, scale, parts[:, 0, :], ALU.mult, ALU.subtract).then_inc(d_read, 1)
                dve.wait_ge(d_read, it.d(name))
                step(dve.tensor_copy(parts[:, 1, :], rs))
                step(dve.tensor_tensor(parts[:, 2, :], rs, parts[:, 1, :], ALU.subtract))

            def split_l0(it):
                n = it.image["A0"]
                wait(dve, parts0_out, n.at(16, 0))
                split(it, "qk0", n, parts0, high0, split0, 2 * D, 1.0)

            def max0(it, t):
                slot = take(it, "max0", t)
                dve.tensor_reduce(mx0[:, t:t + 1], slot[:], AX.X, ALU.max).then_inc(d_read, 1)

            def neg(it, last, sem, n, per_image, first, mx, to):
                dve.wait_ge(d_read, last)
                step = Chain(dve, sem, n, per_image, first)
                step(dve.tensor_scalar(to[:, :, 0], mx, -1.0, None, ALU.mult))
                step(dve.scalar_tensor_tensor(to[:, :, 1], mx, -1.0, to[:, :, 0], ALU.mult, ALU.subtract))

            def neg_l0(it):
                n = it.image["A0"]
                if "A1" in it.image:
                    dve.wait_ge(e_full, it.e("mrow0", 1))
                neg(it, it.d("max0", TILES - 1), neg0_done, n, NEGS, 0, mx0[:], neg0[:])

            def out0(it):
                n = it.image["A1"]
                slot = take(it, "out0").rearrange("p (t c) -> p t c", c=P)
                step = Chain(dve, norm0_done, n, NORMS)
                step(dve.reciprocal(rs0[:], slot[:, :, C]))
                step(dve.tensor_scalar(rs0[:], rs0[:], gamma[:], None, ALU.mult))
                wait(dve, map_out, n.at(8 * 16, 0))
                if it.has_before("A1"):
                    dve.wait_ge(e_full, it.before().e("back0"))
                by = rs0[:].unsqueeze(2).broadcast_to([P, TILES, C])
                dve.tensor_tensor(xt[:], slot[:, :, 0:C], by, ALU.mult).then_inc(d_read, 1)

            def in0(it):
                n = it.image["A1"]
                slot = take(it, "in0").rearrange("p (t c) -> p t c", c=P)
                dve.wait_ge(d_read, it.d("out0"))
                dve.tensor_tensor(xt[:], xt[:], slot[:, :, 0:C], ALU.add).then_inc(d_read, 1)

            def offsets(it):
                n = it.image["A1"]
                slot = take(it, "offsets").rearrange("p (t c) -> p t c", c=P)
                step = Chain(dve, offsets_done, n, OFFSET_OPS)
                dve.tensor_tensor(pos[:], slot[:, :, 0:OFFS], grid[:], ALU.add).then_inc(d_read, 1)
                dve.wait_ge(d_read, it.d("offsets"))
                step(dve.tensor_scalar(pos[:], pos[:], float(H + 1), 0.0, ALU.min, ALU.max))
                step(dve.tensor_copy(rnd[:], pos[:]))
                step(dve.tensor_copy(flo[:], rnd[:]))
                step(dve.tensor_tensor(one_less[:], flo[:], pos[:], ALU.is_gt))
                step(dve.tensor_tensor(flo[:], flo[:], one_less[:], ALU.subtract))
                step(dve.tensor_scalar(flo[:], flo[:], float(H), None, ALU.min))
                step(dve.tensor_tensor(pos[:], pos[:], flo[:], ALU.subtract))
                step(dve.tensor_scalar(one_less[:], pos[:], -1.0, 1.0, ALU.mult, ALU.add))
                for dx in range(2):
                    for dy in range(2):
                        wy = (one_less, pos)[dy][:, :, 0:TAPS]
                        wx = (one_less, pos)[dx][:, :, TAPS:OFFS]
                        step(dve.tensor_tensor(wt[:, n.parity, :, :, 2 * dx + dy], wx, wy, ALU.mult))
                step(dve.tensor_scalar(one_less[:, :, 0:TAPS], flo[:, :, 0:TAPS], float(MAP_W), None,
                                       ALU.mult))
                step(dve.tensor_tensor(idx[:, n.parity], one_less[:, :, 0:TAPS], flo[:, :, TAPS:OFFS], ALU.add))
                assert step.k == OFFSET_OPS

            def scale(it, t, part):
                n = it.image[b_stage(t)]
                step = Chain(dve, scaled, n, SCALES * TILES, SCALES * t + part)
                if part == 3:
                    step(dve.tensor_tensor(gs[:, t % 2, 0:2, :], gs[:, t % 2, 0:2, :], gs[:, t % 2, 2:4, :], ALU.add))
                    step(dve.tensor_tensor(gs[:, t % 2, 0, :], gs[:, t % 2, 0, :], gs[:, t % 2, 1, :], ALU.add))
                    return
                if part == 0:
                    if t == 0:
                        dve.wait_ge(offsets_done, n.at(OFFSET_OPS, OFFSET_OPS))
                    per = TAPS * 16
                    dve.wait_ge(gathered[t % 2], n.at(TILES // 2 * per, (t // 2 + 1) * per))
                    other = tiles_before(it, t, 2)
                    if other is not None:
                        dve.wait_ge(e_full, other.e("turn", (t - 2) % TILES, use=1))
                taps = slice(3 * part, 3 * part + 3)
                g = G[:, t % 2, :].rearrange("p (k c d) -> p k c d", k=TAPS, c=CORNERS)[:, taps]
                to = gs[:, t % 2, :, :].rearrange("p c (k d) -> p k c d", k=TAPS)[:, taps]
                by = wt[:, n.parity, t, taps, :].unsqueeze(3).broadcast_to([P, 3, CORNERS, C])
                step(dve.tensor_tensor(to, g, by, ALU.mult))

            def deform(it, m):
                n = it.image[b_stage(2 * m)]
                slot = take(it, "deform", m)
                wait(dve, x1_ready, n.at(TILES, 2 * (m - 1)))
                dve.scalar_tensor_tensor(y1[:, m % 2, :], slot[:, 0:P], bn[:, 1:2],
                                         res[:, n.parity, m * P:(m + 1) * P], ALU.mult, ALU.add).then_inc(d_read, 1)

            def means(it):
                n = it.image["C1"]
                dve.wait_ge(x1_ready, n.at(TILES, TILES))
                step = Chain(dve, stat_done, n, STAT_OPS)
                for b in range(2):
                    step(dve.bn_stats(bnst[:, b, :], x1[:, n.parity, b * HALF:(b + 1) * HALF]))
                sets = bnst[:].rearrange("p a (b s) -> p (a b) s", s=3)
                step(dve.tensor_tensor(mv[:], sets[:, :, 1], sets[:, :, 1], ALU.mult))
                step(dve.scalar_tensor_tensor(mv[:], sets[:, :, 2], 4.0 / PX, mv[:], ALU.mult, ALU.add))
                step(dve.tensor_reduce(stat_in[0:C, 1:2], mv[:], AX.X, ALU.add))
                step(dve.tensor_reduce(stat_in[0:C, 0:1], sets[:, :, 1], AX.X, ALU.add))

            def stat(it):
                n = it.image["C1"]
                step = Chain(dve, stat_done, n, STAT_OPS, 6)
                slot = take(it, "stat")
                dve.tensor_copy(gm[:, 0:2], slot[0:C, 0:2]).then_inc(d_read, 1)
                dve.wait_ge(d_read, it.d("stat"))
                step(dve.tensor_tensor(gm[:, 2:3], gm[:, 0:1], gm[:, 0:1], ALU.mult))
                step(dve.scalar_tensor_tensor(gm[:, 3:4], gm[:, 1:2], EPS, gm[:, 2:3], ALU.add, ALU.subtract))
                newton_rsqrt(step, gm[:, 3:4], gm[:, 4:5], gm[:, 5:6])
                step(dve.tensor_tensor(gm[:, 5:6], gm[:, 4:5], gn_w, ALU.mult))
                step(dve.tensor_tensor(gm[:, 6:7], gm[:, 0:1], gm[:, 5:6], ALU.mult))
                step(dve.tensor_tensor(gm[:, 7:8], gn_b, gm[:, 6:7], ALU.subtract))
                if it.has_before("C1"):
                    dve.wait_ge(e_full, it.before().e("v2", 1))
                step(dve.tensor_scalar(ha[0:C, :], x1[:, n.parity, :], gm[:, 5:6], gm[:, 7:8], ALU.mult, ALU.add))
                assert step.k == STAT_OPS

            def split_l2(it):
                n = it.image["C1"]
                wait(dve, parts2_out, n.at(16, 0))
                split(it, "qk2", n, parts2, high2, split2, P, qscale[:])

            def max2(it, h, t):
                slot = take(it, "max2", h, t)
                dve.tensor_reduce(mx2[:, h, t:t + 1], slot[:], AX.X, ALU.max).then_inc(d_read, 1)

            def neg_l2(it, h):
                n = it.image["M"]
                if it.has_before("M"):
                    dve.wait_ge(e_full, it.before().e("mrow2", h, 1))
                neg(it, it.d("max2", h, TILES - 1), neg2_done, n, NEGS * HEADS, NEGS * h, mx2[:, h, :], neg2[:, h])

            def sums(it):
                n = it.image["C3"]
                slot = take(it, "sums").rearrange("p (t h e) -> p t h e", h=HEADS, e=2 * D)
                step = Chain(dve, normed2, n, 1)
                step(dve.reciprocal(rs2[:], slot[:, :, :, D]))
                if it.has_before("C3"):
                    dve.wait_ge(e_full, it.before().e("back2"))
                by = rs2[:].unsqueeze(3).broadcast_to([P, TILES, HEADS, D])
                dve.tensor_tensor(r2t[:].rearrange("p t (h d) -> p t h d", d=D), slot[:, :, :, 0:D], by, ALU.mult)\
                    .then_inc(d_read, 1)

            def proj(it, b):
                n = it.image["C3"]
                slot = take(it, "proj", b)
                if b == 0:
                    dve.wait_ge(kept_ready, n.at(1, 1))
                    dve.wait_ge(x2_out, n.at(16, 16))
                    if it.has_before("C3"):
                        dve.wait_ge(e_full, it.before().e("x2t", 1))
                cols = slice(b * HALF, (b + 1) * HALF)
                dve.scalar_tensor_tensor(x2[C:P, cols], slot[C:P, 0:HALF], b_proj, kept[:, n.parity, cols],
                                         ALU.add, ALU.add).then_inc(d_read, 1)

            def sigma(it):
                slot = take(it, "sigma")
                dve.tensor_tensor(sig[:], sig[:], slot[0:C, 0:P], ALU.add).then_inc(d_read, 1)

            for tile in ones:
                dve.memset(tile, 1.0).then_inc(s_ones, 1)
            for tile in blanks:
                dve.memset(tile, 0.0).then_inc(s_ones, 1)
            dve.wait_ge(s_w, 16 * len(loads))
            dve.wait_ge(s_ones, N_ONES)
            step = Chain(dve, s_prep, Image(0, 0), 0)
            step(dve.tensor_copy(identb[:], identf[:]))
            for axis in range(2):
                for k in range(TAPS):
                    to = woff[:, :, TAPS * axis + k]
                    step(dve.tensor_copy(to, w6[:, :, 4 + axis]))
                    for j in range(2):
                        if REG[j][k]:
                            step(dve.tensor_tensor(to, to, w6[:, :, 2 * axis + j],
                                                   ALU.add if REG[j][k] > 0 else ALU.subtract))
            step(dve.tensor_scalar(bn[:, 0:1], bn_v, EPS, None, ALU.add))
            newton_rsqrt(step, bn[:, 0:1], newton[:, 0:1], newton[:, 1:2])
            step(dve.tensor_tensor(bn[:, 1:2], newton[:, 0:1], bn_g, ALU.mult))
            step(dve.tensor_tensor(bn[:, 2:3], bn_m, bn[:, 1:2], ALU.mult))
            step(dve.tensor_tensor(bn[:, 3:4], bn_b, bn[:, 2:3], ALU.subtract))
            assert step.k == N_PREP, step.k
            run(dve, {"split0": split_l0, "max0": max0, "neg0": neg_l0, "out0": out0, "in0": in0,
                      "offsets": offsets, "scale": scale, "deform": deform, "means": means, "stat": stat, "split2": split_l2, "max2": max2,
                      "neg2": neg_l2, "sums": sums, "proj": proj, "sigma": sigma})

            dve.wait_ge(d_read, D_ALL)
            step = Chain(dve, f_dve, Image(0, 0), 0)
            count = [0]
            small = dring[0]

            def product():
                count[0] += 1
                dve.wait_ge(f_pe, count[0])

            def hold(instruction):
                held[0] += 1
                instruction.then_inc(f_hold, 1)
                dve.wait_ge(f_hold, held[0])

            held = [0]
            hold(dve.tensor_scalar(mean[:], sig[:, 0:1], 1.0 / (IMAGES * PX), None, ALU.mult))
            step(dve.tensor_scalar(cov[:], sig[:, C:P], 1.0 / (IMAGES * PX), None, ALU.mult))
            product()
            step(dve.tensor_copy(mrow[:], small[0:1, 0:C]))
            product()
            hold(dve.tensor_tensor(cov[:], cov[:], small[0:C, 0:C], ALU.subtract))
            hold(dve.scalar_tensor_tensor(cov[:], identf[0:C, 0:C], EPS, cov[:], ALU.mult, ALU.add))
            hold(dve.tensor_tensor(cov[:], cov[:], mask[:], ALU.mult))
            hold(dve.tensor_tensor(tmp[:], cov[:], identf[0:C, 0:C], ALU.mult))
            step(dve.tensor_reduce(tr[:, 0:1], tmp[:], AX.X, ALU.add))
            product()
            hold(dve.tensor_copy(tr[:, 1:2], small[0:C, 0:1]))
            hold(dve.reciprocal(tr[:, 2:3], tr[:, 1:2]))
            hold(dve.tensor_scalar(cov[:], cov[:], tr[:, 2:3], None, ALU.mult))
            newton_rsqrt(hold, tr[:, 1:2], tr[:, 2:3], tr[:, 3:4])
            step(dve.tensor_copy(pm[:], identf[0:C, 0:C]))
            for k in range(STEPS):
                product()
                step(dve.tensor_copy(pa[:], small[0:C, 0:C]))
                product()
                step(dve.tensor_copy(tmp[:], small[0:C, 0:C]))
                product()
                hold(dve.tensor_scalar(pm[:], pm[:], 1.5, None, ALU.mult))
                (step if k < STEPS - 1 else hold)(dve.scalar_tensor_tensor(pm[:], small[0:C, 0:C], -0.5, pm[:], ALU.mult, ALU.add))
            dve.wait_ge(x2_out, 16)
            hold(dve.scalar_tensor_tensor(w2[0:C, 0:C], pm[:], tr[:, 2:3], w3row[:], ALU.mult, ALU.mult))
            step(dve.tensor_copy(w2[C:P, C:P], w2[0:C, 0:C]))
            product()
            hold(dve.tensor_tensor(b2[0:C, :], bias3, small[0:C, 0:1], ALU.subtract))
            step(dve.tensor_copy(b2[C:P, :], b2[0:C, :]))

            def last(j, b):
                dve.wait_ge(d_full, j * 2 + (D_ALL + b + 1))
                dve.tensor_scalar(fin_dst[b], dring[b][:], b2[:], None, ALU.add).then_inc(d_read, 1)

            for b in range(2):
                last(0, b)
            with dve.Fori(1, IMAGES // 4) as j:
                for b in range(2):
                    dve.wait_ge(fin_out[b], j * 16)
                    last(j, b)

        @block.tensor
        def _(pe):
            def d_slot(it, name, *args):
                wait(pe, d_read, it.d(name, *args) + (-2))
                return dring[it.slot("d", name, *args)]

            def e_slot(it, name, *args, use=0):
                wait(pe, e_read, it.e(name, *args, use=use) + (-2))
                return ering[it.slot("e", name, *args, use=use)]

            def mm(to, lhsT, rhs, start=True, stop=True):
                return pe.matmul(to, lhsT, rhs, start=start, stop=stop)

            def halves(to, lhsT, rhs):
                for b in range(2):
                    last = mm(to[:, b * HALF:(b + 1) * HALF], lhsT, rhs[:, b * HALF:(b + 1) * HALF])
                return last

            def qk0(it):
                n = it.image["A0"]
                pe.wait_ge(x_in[n.parity], n.at_own_parity(16, 16))
                halves(d_slot(it, "qk0")[0:2 * D, :], wqk0[:], xin[:, n.parity, :]).then_inc(d_full, 1)

            def v_l0(it, b):
                n = it.image["A0"]
                slot = e_slot(it, "v0", b)
                for t in range(4):
                    px = (4 * b + t) * P
                    last = mm(slot[:, t * P:(t + 1) * P], xin[:, n.parity, px:px + P], wv0[:])
                last.then_inc(e_full, 1)

            def max0(it, t):
                n = it.image["A0"]
                if t == 0:
                    pe.wait_ge(stacks0_in, n.at(2 * PARTS * 16, 2 * PARTS * 16))
                halves(d_slot(it, "max0", t), mov0[0:ROWS, t * P:(t + 1) * P], stat0[0:ROWS, :]).then_inc(d_full, 1)

            def mrow0(it, b):
                n = it.image["A1"]
                slot = e_slot(it, "mrow0", b)
                pe.wait_ge(neg0_done, n.at(NEGS, NEGS))
                for t in range(4):
                    last = mm(slot[MROW:STACK, t * P:(t + 1) * P], neg0[:, 4 * b + t, :], identb[:])
                last.then_inc(e_full, 1)

            def pv0(it, t, b):
                pe.wait_ge(e_read, it.e("exp0", t, b))
                mm(o[:, b * HALF:(b + 1) * HALF], v0[:, t, :], p0[:, b, :], t == 0, t == TILES - 1)\
                    .then_inc(pv0_done, 1)

            def exp0(it, t, b):
                if t == 0 and b == 0:
                    pe.wait_ge(e_read, it.e("mrow0", 1))
                    done = it.image["C2"].at(1, 0) if "C2" in it.image else max(0, min(it.c - SHIFT["C2"], IMAGES))
                    wait(pe, o2_read, done)
                mm(e_slot(it, "exp0", t, b)[:], stat0[:, t * P:(t + 1) * P], mov0[:, b * HALF:(b + 1) * HALF])\
                    .then_inc(e_full, 1)
                if t or b:
                    pv0(it, t if b else t - 1, 1 - b)

            def pv0_end(it):
                pv0(it, TILES - 1, 1)

            def out0(it):
                slot = d_slot(it, "out0")
                pe.wait_ge(o0_read, it.image["A1"].at(1, 1))
                for t in range(TILES):
                    last = pe.transpose(slot[:, t * P:(t + 1) * P], att0[:, t * P:(t + 1) * P], identf[:])
                last.then_inc(d_full, 1)

            def in0(it):
                n = it.image["A1"]
                slot = d_slot(it, "in0")
                for t in range(TILES):
                    last = pe.transpose(slot[:, t * P:(t + 1) * P], xin[:, n.parity, t * P:(t + 1) * P], identf[:])
                last.then_inc(d_full, 1)

            def back(slot, src):
                flat = src[:].rearrange("p t c -> p (t c)")
                for q in range(TILES // 2):
                    last = pe.transpose(slot[:, q * P:(q + 1) * P], flat[:, q * P:(q + 1) * P], identf[:])
                last.then_inc(e_full, 1)

            def back0(it):
                slot = e_slot(it, "back0")
                pe.wait_ge(d_read, it.d("in0"))
                back(slot, xt)

            def conv(it, b):
                n = it.image["A1"]
                slot = e_slot(it, "conv", b)
                pe.wait_ge(e_read, it.e("back0"))
                for k in range(3):
                    for g, taps in enumerate(CONV_GROUPS):
                        if k < len(taps):
                            ky, kx = taps[k] // 3, taps[k] % 3
                            src = (xl, xc[:, n.parity, :], xr)[kx]
                            at = (ky + b * H // 2) * W
                            last = mm(slot[32 * g:32 * g + 32, :], woff[:, taps[k], :], src[:, at:at + HALF],
                                      k == 0, k == len(taps) - 1)
                last.then_inc(e_full, 1)

            def offsets(it):
                slot = d_slot(it, "offsets")
                pe.wait_ge(e_read, it.e("conv", 1))
                for t in range(TILES):
                    last = mm(slot[:, t * P:(t + 1) * P], cs[:, t * P:(t + 1) * P], gather_sel[:])
                last.then_inc(d_full, 1)

            def turn(it, t):
                n = it.image[b_stage(t)]
                slot = e_slot(it, "turn", t)
                pe.wait_ge(scaled, n.at(SCALES * TILES, SCALES * (t + 1)))
                for q in range(4):
                    last = pe.transpose(slot[:, q * P:(q + 1) * P], gs[:, t % 2, 0, 2 * q * C:2 * (q + 1) * C],
                                        identf[:])
                last.then_inc(e_full, 1)
                slot = e_slot(it, "turn", t, use=1)
                flat = gs[:, t % 2, :, :].rearrange("p c k -> p (c k)")
                pe.transpose(slot[:, 0:P], flat[:, 8 * C:10 * C], identf[:]).then_inc(e_full, 1)

            def deform(it, m):
                slot = d_slot(it, "deform", m)
                pe.wait_ge(e_read, it.e("turn", 2 * m + 1, use=1))
                for q in range(5):
                    for odd in range(2):
                        last = mm(slot[odd * C:(odd + 1) * C, 0:P], wd[:, q, :],
                                  ts[:, (2 * m + odd) % 4, q * P:(q + 1) * P], q == 0, q == 4)
                last.then_inc(d_full, 1)

            def stat(it):
                n = it.image["C1"]
                slot = d_slot(it, "stat")
                pe.wait_ge(stat_done, n.at(STAT_OPS, 6))
                mm(slot[:, 0:P], group_mean[:], stat_in[:]).then_inc(d_full, 1)

            def qk2(it):
                n = it.image["C1"]
                slot = d_slot(it, "qk2")
                pe.wait_ge(stat_done, n.at(STAT_OPS, STAT_OPS))
                halves(slot, wqk2[:], ha[:]).then_inc(d_full, 1)

            def v_l2(it, b):
                slot = e_slot(it, "v2", b)
                for t in range(4):
                    px = (4 * b + t) * P
                    last = mm(slot[:, t * P:(t + 1) * P], ha[:, px:px + P], wv2[:])
                last.then_inc(e_full, 1)

            def max2(it, h, t):
                n = it.image["M"]
                if h == 0 and t == 0:
                    pe.wait_ge(stacks2_in, n.at(2 * PARTS * 16, 2 * PARTS * 16))
                halves(d_slot(it, "max2", h, t), mov2[0:ROWS, n.parity, h, t * P:(t + 1) * P],
                       stat2[0:ROWS, n.parity, h, :]).then_inc(d_full, 1)

            def mrow2(it, h, b):
                n = it.image["M"]
                slot = e_slot(it, "mrow2", h, b)
                pe.wait_ge(neg2_done, n.at(NEGS * HEADS, NEGS * (h + 1)))
                for t in range(4):
                    last = mm(slot[MROW:STACK, t * P:(t + 1) * P], neg2[:, h, 4 * b + t, :], identb[:])
                last.then_inc(e_full, 1)

            def pv2(it, w):
                n = it.image["C2"]
                pe.wait_ge(e_read, it.e("exp2", w, HEADS - 1))
                t, b = w // 2, w % 2
                for h in range(HEADS):
                    last = mm(o[32 * h:32 * h + 32, b * HALF:(b + 1) * HALF], va[:, n.parity, t, 32 * h:32 * h + 32],
                              p2[:, w % 2, h, :], t == 0, t == TILES - 1)
                last.then_inc(pv2_done, 1)

            def exp2(it, w, h):
                n = it.image["C2"]
                if w == 0 and h == 0:
                    pe.wait_ge(e_read, it.before().e("mrow2", HEADS - 1, 1))
                    pe.wait_ge(o0_read, it.image["A1"].at(1, 1) if "A1" in it.image else IMAGES)
                t, b = w // 2, w % 2
                mm(e_slot(it, "exp2", w, h)[:], stat2[:, n.parity, h, t * P:(t + 1) * P],
                   mov2[:, n.parity, h, b * HALF:(b + 1) * HALF]).then_inc(e_full, 1)
                if h == 1 and w:
                    pv2(it, w - 1)

            def pv2_end(it):
                pv2(it, 15)

            def sums(it):
                n = it.image["C3"]
                slot = d_slot(it, "sums")
                pe.wait_ge(o2_read, n.at(1, 1))
                for t in range(TILES):
                    last = pe.transpose(slot[:, t * P:(t + 1) * P], att[:, t * P:(t + 1) * P], identf[:])
                last.then_inc(d_full, 1)

            def back2(it):
                slot = e_slot(it, "back2")
                pe.wait_ge(d_read, it.d("sums"))
                back(slot, r2t)

            def proj(it, b):
                slot = d_slot(it, "proj", b)
                pe.wait_ge(e_read, it.e("back2"))
                mm(slot[:, 0:HALF], wproj[:], att[:, b * HALF:(b + 1) * HALF]).then_inc(d_full, 1)

            def x2t_step(it, b):
                slot = e_slot(it, "x2t", b)
                pe.wait_ge(d_read, it.d("proj", 1))
                for t in range(4):
                    px = (4 * b + t) * P
                    last = pe.transpose(slot[:, t * P:(t + 1) * P], x2[:, px:px + P], identf[:])
                last.then_inc(e_full, 1)

            def sigma(it):
                slot = d_slot(it, "sigma")
                pe.wait_ge(e_read, it.e("x2t", 1))
                for t in range(TILES):
                    last = mm(slot[0:C, 0:P], x2t[:, t, C:P], x2t[:, t, :], t == 0, t == TILES - 1)
                last.then_inc(d_full, 1)

            pe.wait_ge(s_w, 16 * len(loads))
            pe.wait_ge(s_ones, N_ONES)
            pe.wait_ge(s_prep, N_PREP)
            run(pe, {"qk0": qk0, "v0": v_l0, "max0": max0, "mrow0": mrow0, "exp0": exp0, "pv0_end": pv0_end,
                     "out0": out0, "in0": in0, "back0": back0, "conv": conv, "offsets": offsets, "turn": turn,
                     "deform": deform, "stat": stat,
                     "qk2": qk2, "v2": v_l2, "max2": max2, "mrow2": mrow2, "exp2": exp2, "pv2_end": pv2_end,
                     "sums": sums, "back2": back2, "proj": proj, "x2t": x2t_step, "sigma": sigma})

            small = dring[0]
            k = [0]

            def product(rows, cols, lhsT, rhs):
                k[0] += 1
                pe.wait_ge(f_dve, k[0])
                mm(small[0:rows, 0:cols], lhsT, rhs).then_inc(f_pe, 1)

            product(1, C, mean[:], identf[0:C, 0:C])
            product(C, C, mrow[:], mrow[:])
            product(C, 1, mask[:], tr[:, 0:1])
            for _ in range(STEPS):
                product(C, C, pm[:], pm[:])
                product(C, C, pa[:], pm[:])
                product(C, C, tmp[:], cov[:])
            product(C, 1, w2[0:C, 0:C], mean[:])
            pe.wait_ge(f_dve, k[0] + 1)
            with pe.Fori(0, IMAGES // 4) as j:
                for b in range(2):
                    pe.wait_ge(fin_in[b], j * 16 + 16)
                    pe.wait_ge(d_read, j * 2 + (D_ALL + b - 1))
                    halves(dring[b], w2[:], fin_src[b]).then_inc(d_full, 1)

        @block.scalar
        def _(act):
            def take(it, name, *args, use=0):
                act.wait_ge(e_full, it.e(name, *args, use=use))
                return ering[it.slot("e", name, *args, use=use)]

            def v_l0(it, b):
                n = it.image["A0"]
                slot = take(it, "v0", b)
                wait(act, pv0_done, n.at(16, 0))
                act.activation(v0[:, 4 * b:4 * b + 4, :].rearrange("p t c -> p (t c)"), slot[:], ACT.Copy)\
                    .then_inc(e_read, 1)

            def mrow0(it, b):
                slot = take(it, "mrow0", b)
                act.activation(mov0[MROW:STACK, b * HALF:(b + 1) * HALF], slot[MROW:STACK, :], ACT.Copy)\
                    .then_inc(e_read, 1)

            def exp0(it, t, b):
                n = it.image["A1"]
                slot = take(it, "exp0", t, b)
                wait(act, pv0_done, n.at(16, 2 * t + b - 1))
                act.activation(p0[:, b, :], slot[:], ACT.Exp).then_inc(e_read, 1)

            def high(name, parts, image_of, stored, done, rows, **scale):
                def step(it):
                    n = it.image[image_of]
                    act.wait_ge(d_full, it.d(name))
                    wait(act, stored, n.at(16, 0))
                    act.activation(parts[:, 0, :], dring[it.slot("d", name)][0:rows, :], ACT.Copy, **scale)\
                        .then_inc(done, 1)
                return step

            def spread2(it):
                n = it.image["C1"]
                act.wait_ge(split2, n.at(SPLITS, SPLITS))
                act.dma_start(parts2_d[n.parity].rearrange("t r n -> r t n"), parts2[:]).then_inc(parts2_out, 16)

            def attended0(it):
                n = it.image["A1"]
                act.wait_ge(pv0_done, n.at(16, 16))
                if it.has_before("A1"):
                    act.wait_ge(d_full, it.before().d("out0"))
                act.activation(att0[:], o[:], ACT.Copy).then_inc(o0_read, 1)

            def back0(it):
                n = it.image["A1"]
                slot = take(it, "back0")
                if it.has_before("A1"):
                    act.wait_ge(e_full, it.before().e("conv", 1))
                act.activation(res[:, n.parity, :], slot[:], ACT.Identity, bias=bn[:, 3:4])
                for move, image in ((0, xc[0:C, n.parity]), (1, xl[0:C, :]), (-1, xr[0:C, :])):
                    rows = image[:, W:W + PX].rearrange("c (q s r x) -> c q s r x", s=2, r=P // W, x=W)
                    for odd in range(2):
                        src = slot[odd * C:(odd + 1) * C, :].rearrange("c (q r x) -> c q r x", r=P // W, x=W)
                        last = act.activation(rows[:, :, odd, :, max(move, 0):W + min(move, 0)],
                                              src[:, :, :, max(-move, 0):W - max(move, 0)], ACT.Copy)
                last.then_inc(e_read, 1)

            def conv(it, b):
                slot = take(it, "conv", b)
                if it.has_before("A1"):
                    act.wait_ge(d_full, it.before().d("offsets"))
                act.wait_ge(split0, it.image["A1"].at(SPLITS, SPLITS))
                if "C1" in it.image:
                    wait(act, split2, it.image["C1"].at(SPLITS, 0))
                act.activation(cs[:, b * HALF:(b + 1) * HALF], slot[:], ACT.Copy).then_inc(e_read, 1)

            def turn(it, t):
                slot = take(it, "turn", t)
                other = tiles_before(it, t, 4)
                if other is not None:
                    act.wait_ge(d_full, other.d("deform", (t - 4) % TILES // 2))
                act.activation(ts[:, t % 4, 0:4 * P], slot[:], ACT.Copy).then_inc(e_read, 1)
                slot = take(it, "turn", t, use=1)
                act.activation(ts[:, t % 4, 4 * P:5 * P], slot[:, 0:P], ACT.Copy).then_inc(e_read, 1)

            def relu(it, m):
                n = it.image[b_stage(2 * m)]
                act.wait_ge(d_read, it.d("deform", m))
                if m == 0:
                    wait(act, stat_done, n.at(STAT_OPS, -STAT_OPS))
                    wait(act, kept_ready, n.at(1, -1))
                for odd in range(2):
                    px = (2 * m + odd) * P
                    act.activation(x1[:, n.parity, px:px + P], y1[odd * C:(odd + 1) * C, m % 2, :], ACT.Relu)\
                        .then_inc(x1_ready, 1)

            def keep(it):
                n = it.image["M"]
                if "C3" in it.image:
                    act.wait_ge(d_read, it.d("proj", 1))
                act.wait_ge(x1_ready, n.at(TILES, TILES))
                act.activation(kept[:, n.parity, :], x1[:, n.parity, :], ACT.Copy).then_inc(kept_ready, 1)

            def v_l2(it, b):
                n = it.image["C1"]
                slot = take(it, "v2", b)
                wait(act, pv2_done, n.at(16, -16))
                act.activation(va[:, n.parity, 4 * b:4 * b + 4, :].rearrange("p t c -> p (t c)"), slot[:], ACT.Copy)\
                    .then_inc(e_read, 1)

            def mrow2(it, h, b):
                n = it.image["M"]
                slot = take(it, "mrow2", h, b)
                act.activation(mov2[MROW:STACK, n.parity, h, b * HALF:(b + 1) * HALF], slot[MROW:STACK, :], ACT.Copy)\
                    .then_inc(e_read, 1)

            def exp2(it, w, h):
                n = it.image["C2"]
                slot = take(it, "exp2", w, h)
                wait(act, pv2_done, n.at(16, w - 1))
                act.activation(p2[:, w % 2, h, :], slot[:], ACT.Exp).then_inc(e_read, 1)

            def attended(it):
                n = it.image["C3"]
                act.wait_ge(pv2_done, n.at(16, 16))
                if it.has_before("C3"):
                    act.wait_ge(d_full, it.before().d("proj", 1))
                act.activation(att[:], o[:], ACT.Copy).then_inc(o2_read, 1)

            def back2(it):
                slot = take(it, "back2")
                to = att[0:C, :].rearrange("c (q s p) -> c q s p", s=2, p=P)
                for odd in range(2):
                    last = act.activation(to[:, :, odd, :],
                                          slot[odd * C:(odd + 1) * C, :].rearrange("c (q p) -> c q p", p=P), ACT.Copy)
                last.then_inc(e_read, 1)

            def x2t_step(it, b):
                slot = take(it, "x2t", b).rearrange("p (t c) -> p t c", c=P)
                if it.has_before("C3"):
                    act.wait_ge(d_full, it.before().d("sigma"))
                act.activation(x2t[:, 4 * b:4 * b + 4, :], slot[:], ACT.Copy)\
                    .then_inc(e_read, 1)

            act.wait_ge(s_w, 16 * len(loads))
            act.wait_ge(s_ones, N_ONES)
            act.wait_ge(s_prep, N_PREP)
            run(act, {"split0": high("qk0", parts0, "A0", parts0_out, high0, 2 * D),
                      "split2": high("qk2", parts2, "C1", parts2_out, high2, P, scale=qscale[:]),
                      "v0": v_l0, "mrow0": mrow0, "exp0": exp0, "attended0": attended0, "back0": back0, "conv": conv,
                      "spread2": spread2,
                      "turn": turn, "relu": relu, "keep": keep, "v2": v_l2, "mrow2": mrow2, "exp2": exp2,
                      "attended": attended, "back2": back2, "x2t": x2t_step})

            with act.Fori(0, IMAGES // 4) as j:
                for b in range(2):
                    act.wait_ge(d_read, j * 2 + (D_ALL + b + 1))
                    act.dma_start(out_pairs[bass.ds(j * 2 + b, 1), :, :].rearrange("o c n -> (o c) n"), fin_dst[b])\
                        .then_inc(fin_out[b], 16)
            for b in range(2):
                act.wait_ge(fin_out[b], 16 * IMAGES // 4)


def constants():
    f = np.float32
    px = np.arange(PX).reshape(TILES, P)
    grid = np.empty((P, TILES, OFFS), f)
    grid[:, :, 0:TAPS] = (px // W + 1).T[:, :, None]
    grid[:, :, TAPS:] = (px % W + 1).T[:, :, None]
    gather_sel = np.zeros((P, P), f)
    for g in range(4):
        gather_sel[32 * g + np.arange(OFFS), np.arange(OFFS)] = 1
    channel = np.arange(C)
    return {
        "identf": np.eye(P, dtype=f), "grid": grid,
        "gather_sel": gather_sel,
        "qscale": np.where(np.arange(P) < C, f(D ** -0.5), f(1))[:, None].astype(f),
        "group_mean": ((np.arange(P)[:, None] // 8 == np.arange(P)[None, :] // 8) / 32).astype(f),
        "mask": (channel[:, None] // GROUP == channel[None, :] // GROUP).astype(f),
    }


def layout(i):
    f = np.float32
    out = {"x": i["x"].reshape(IMAGES, C, PX)}

    def rows(w):
        return np.concatenate([w, np.zeros((P - w.shape[0],) + w.shape[1:], f)], 0)
    out["wqk0"] = rows(np.concatenate([np.concatenate([i["L0_conv_wq"].T, i["L0_conv_wk"].T], 1),
                                       np.concatenate([i["L0_conv_bq"], i["L0_conv_bk"]])[None]], 0))
    wv0 = np.zeros((C + 1, P), f)
    wv0[0:C, 0:C] = i["L0_conv_wv"].T
    wv0[C, 0:C] = i["L0_conv_bv"]
    wv0[C, C:] = 1
    out["wv0"] = rows(wv0)
    w6 = np.zeros((C + 1, TAPS, 6), f)
    w6[0:C] = np.concatenate([i["L1_conv_w_tm"], i["L1_conv_w_tr"]], 0).reshape(6, C, TAPS).transpose(1, 2, 0)
    w6[C, TAPS // 2] = np.concatenate([i["L1_conv_b_tm"], i["L1_conv_b_tr"]])
    out["w6"] = rows(w6)
    wd = np.zeros((2, C, 5, C), f)
    taps = i["L1_conv_w_deform"].reshape(C, C, TAPS).transpose(2, 1, 0)
    for k in range(TAPS):
        wd[k % 2, :, k // 2, :] = taps[k]
    out["wd"] = wd.reshape(P, 5, C)
    wqkv, bqkv = i["L2_conv_w_qkv"], i["L2_conv_b_qkv"]
    out["wqk2"] = rows(np.concatenate([wqkv[0:2 * C].T, bqkv[None, 0:2 * C]], 0))
    wv2 = np.zeros((C + 1, HEADS, 2 * D), f)
    wv2[0:C, :, 0:D] = wqkv[2 * C:].T.reshape(C, HEADS, D)
    wv2[C, :, 0:D] = bqkv[2 * C:].reshape(HEADS, D)
    wv2[C, :, D:] = 1
    out["wv2"] = rows(wv2.reshape(C + 1, P))
    out["wproj"] = rows(np.concatenate([np.zeros((C, C), f), i["L2_conv_w_proj"].T], 1))
    out["gamma"] = np.broadcast_to(i["L0_conv_gamma"], (P, 1))
    vecs = np.stack([i["L1_conv_bn_gamma"], i["L1_conv_bn_beta"], i["L1_conv_bn_mean"], i["L1_conv_bn_var"],
                     i["L2_conv_gn_w"], i["L2_conv_gn_b"], i["L2_conv_b_proj"],
                     i["L3_conv_bias"].reshape(C)], 1)
    out["vecs"] = np.concatenate([vecs, vecs], 0)
    out["w3row"] = np.broadcast_to(i["L3_conv_weight"].reshape(1, C), (C, C))
    return out


def kernel(**inputs):
    import concourse.bacc as bacc
    from concourse.bass_utils import run_bass_kernel_spmd

    arrays = layout({k: np.asarray(v) for k, v in inputs.items()}) | constants()
    arrays = {f"in_{k}": np.ascontiguousarray(v) for k, v in arrays.items()}
    nc = bacc.Bacc("TRN2", target_bir_lowering=False, num_devices=1)
    args = {k[3:]: nc.dram_tensor(k, v.shape, mybir.dt.from_np(v.dtype), kind="ExternalInput").ap()
            for k, v in arrays.items()}
    out = nc.dram_tensor("out", (IMAGES, C, H, W), F32, kind="ExternalOutput").ap()
    build(nc, args, out)
    r = run_bass_kernel_spmd(nc, [arrays], core_ids=[0])
    return r.results[0]["out"]
```
